# Optimizing a Trainium2 kernel written in Bass

```python
import numpy as np
import jax
import jax.numpy as jnp

def _softmax(x, axis=-1):
    return jax.nn.softmax(x, axis=axis)

def _gelu(x):
    return jax.nn.gelu(x, approximate=True)

def _silu(x):
    return jax.nn.silu(x)

def _sigmoid(x):
    return jax.nn.sigmoid(x)

def _layernorm(x, axis=-1, eps=1e-05):
    m = jnp.mean(x, axis=axis, keepdims=True)
    v = jnp.var(x, axis=axis, keepdims=True)
    return (x - m) / jnp.sqrt(v + eps)

def _scatter_add(tgt, idx, src, axis=0):
    return tgt.at[idx].add(src)

def _segment_sum(src, seg, n):
    return jax.ops.segment_sum(src, seg, n)
kernel_name = 'mk_macaron_d2_jaxref_r8_7b9735'

def setup_inputs(seed: int=0):
    np.random.seed(seed)
    _w = jnp.asarray

    def _L0_attn_setup():
        import jax, jax.numpy as jnp
        import numpy as np
        E, H, W = (128, 16, 32)
        D = E // H

        def _rmsnorm(t, w):
            eps = jnp.finfo(t.dtype).eps
            return t * jax.lax.rsqrt(jnp.mean(t * t, axis=-1, keepdims=True) + eps) * w
        key = jax.random.key(seed)
        ks = jax.random.split(key, 11)
        B, T = (2, 256)
        s = 1.0 / np.sqrt(E)
        return {'x': jax.random.normal(ks[0], (B, T, E), jnp.float32), 'wq': jax.random.normal(ks[1], (E, E), jnp.float32) * s, 'bq': jnp.zeros((E,), jnp.float32), 'wk': jax.random.normal(ks[2], (E, E), jnp.float32) * s, 'bk': jnp.zeros((E,), jnp.float32), 'wv': jax.random.normal(ks[3], (E, E), jnp.float32) * s, 'bv': jnp.zeros((E,), jnp.float32), 'wo': jax.random.normal(ks[4], (E, E), jnp.float32) * s, 'bo': jnp.zeros((E,), jnp.float32), 'qn_w': jnp.ones((D,), jnp.float32), 'kn_w': jnp.ones((D,), jnp.float32)}
    _L0_attn_in = _L0_attn_setup()

    def _L0_ffn_setup():
        import jax, jax.numpy as jnp
        import numpy as np
        B, S, D, H, E = (4, 256, 128, 512, 8)
        key = jax.random.key(seed)
        ks = jax.random.split(key, 8)
        s_d = 1.0 / np.sqrt(D)
        s_h = 1.0 / np.sqrt(H)
        return {'x': jax.random.normal(ks[0], (B, S, D), dtype=jnp.float32), 'gate_w': jax.random.uniform(ks[1], (E, D), jnp.float32, -s_d, s_d), 'gate_b': jax.random.uniform(ks[2], (E,), jnp.float32, -s_d, s_d), 'w1': jax.random.uniform(ks[3], (E, H, D), jnp.float32, -s_d, s_d), 'b1': jax.random.uniform(ks[4], (E, H), jnp.float32, -s_d, s_d), 'w2': jax.random.uniform(ks[5], (E, D, H), jnp.float32, -s_h, s_h), 'b2': jax.random.uniform(ks[6], (E, D), jnp.float32, -s_h, s_h)}
    _L0_ffn_in = _L0_ffn_setup()

    def _L1_attn_setup():
        import jax, jax.numpy as jnp
        import numpy as np
        B, L, D_MODEL, D_STATE = (8, 512, 128, 64)
        key = jax.random.key(seed)
        k1, k2, k3, k4 = jax.random.split(key, 4)
        u = jax.random.normal(k1, (B, L, D_MODEL), dtype=jnp.float32)
        A_log = jnp.log(jnp.arange(1, D_STATE + 1, dtype=jnp.float32))
        D = jax.random.normal(k2, (D_MODEL,), dtype=jnp.float32)
        C_re = jax.random.normal(k3, (D_MODEL, D_STATE), dtype=jnp.float32)
        C_im = jax.random.normal(k4, (D_MODEL, D_STATE), dtype=jnp.float32)
        log_dt = jnp.log(jnp.full((D_MODEL,), 0.01, dtype=jnp.float32))
        return {'u': u, 'A_log': A_log, 'D': D, 'C_re': C_re, 'C_im': C_im, 'log_dt': log_dt}
    _L1_attn_in = _L1_attn_setup()

    def _L1_ffn_setup():
        import jax, jax.numpy as jnp
        import numpy as np
        D_MODEL = 128
        N_HEADS = 16
        HEAD_DIM = D_MODEL // N_HEADS
        KV_LATENT = 64
        N_EXPERTS = 4
        D_HIDDEN = 4 * D_MODEL
        B, T = (2, 128)

        def rmsnorm(x, w, eps=1e-06):
            return w * (x * jax.lax.rsqrt(jnp.mean(x * x, axis=-1, keepdims=True) + eps))

        def layernorm(x, g, b, eps=1e-05):
            mu = jnp.mean(x, axis=-1, keepdims=True)
            var = jnp.mean((x - mu) ** 2, axis=-1, keepdims=True)
            return (x - mu) * jax.lax.rsqrt(var + eps) * g + b

        def apply_rope(x):
            t, d = (x.shape[2], x.shape[3])
            half = d // 2
            pos = jnp.arange(t, dtype=x.dtype)[:, None]
            inv_freq = 1.0 / 10000.0 ** (jnp.arange(half, dtype=x.dtype) / half)
            ang = pos * inv_freq[None, :]
            sin, cos = (jnp.sin(ang), jnp.cos(ang))
            x1, x2 = (x[..., :half], x[..., half:])
            return jnp.concatenate([x1 * cos - x2 * sin, x1 * sin + x2 * cos], axis=-1)

        def mla_attention(x, Wq, Wdkv, Wuk, Wuv, Wo, ln_g, ln_b):
            b, t, _ = x.shape
            q = (x @ Wq.T).reshape(b, t, N_HEADS, HEAD_DIM).transpose(0, 2, 1, 3)
            latent = layernorm(x @ Wdkv.T, ln_g, ln_b)
            k = (latent @ Wuk.T).reshape(b, t, N_HEADS, HEAD_DIM).transpose(0, 2, 1, 3)
            v = (latent @ Wuv.T).reshape(b, t, N_HEADS, HEAD_DIM).transpose(0, 2, 1, 3)
            q = apply_rope(q)
            k = apply_rope(k)
            scores = jnp.einsum('bhqd,bhkd->bhqk', q, k) / np.sqrt(HEAD_DIM)
            causal = jnp.tril(jnp.ones((t, t), dtype=bool))
            scores = jnp.where(causal, scores, -jnp.inf)
            attn = jax.nn.softmax(scores, axis=-1)
            out = jnp.einsum('bhqk,bhkd->bhqd', attn, v).transpose(0, 2, 1, 3).reshape(b, t, D_MODEL)
            return out @ Wo.T

        def moe(x, gate_w, gate_b, W1, b1, W2, b2):
            logits = x @ gate_w.T + gate_b
            top = jnp.argmax(logits, axis=-1)
            onehot = jax.nn.one_hot(top, N_EXPERTS, dtype=x.dtype)
            h = jax.nn.relu(jnp.einsum('btd,ehd->bteh', x, W1) + b1)
            y = jnp.einsum('bteh,edh->bted', h, W2) + b2
            return jnp.einsum('bted,bte->btd', y, onehot)
        key = jax.random.key(seed)
        ks = jax.random.split(key, 16)
        s = lambda fan_in: 1.0 / np.sqrt(fan_in)
        return {'x': jax.random.normal(ks[0], (B, T, D_MODEL), jnp.float32), 'norm1_w': jnp.ones((D_MODEL,), jnp.float32), 'norm2_w': jnp.ones((D_MODEL,), jnp.float32), 'Wq': jax.random.normal(ks[1], (D_MODEL, D_MODEL), jnp.float32) * s(D_MODEL), 'Wdkv': jax.random.normal(ks[2], (KV_LATENT, D_MODEL), jnp.float32) * s(D_MODEL), 'Wuk': jax.random.normal(ks[3], (D_MODEL, KV_LATENT), jnp.float32) * s(KV_LATENT), 'Wuv': jax.random.normal(ks[4], (D_MODEL, KV_LATENT), jnp.float32) * s(KV_LATENT), 'Wo': jax.random.normal(ks[5], (D_MODEL, D_MODEL), jnp.float32) * s(D_MODEL), 'ln_g': jnp.ones((KV_LATENT,), jnp.float32), 'ln_b': jnp.zeros((KV_LATENT,), jnp.float32), 'gate_w': jax.random.normal(ks[6], (N_EXPERTS, D_MODEL), jnp.float32) * s(D_MODEL), 'gate_b': jnp.zeros((N_EXPERTS,), jnp.float32), 'W1': jax.random.normal(ks[7], (N_EXPERTS, D_HIDDEN, D_MODEL), jnp.float32) * s(D_MODEL), 'b1': jnp.zeros((N_EXPERTS, D_HIDDEN), jnp.float32), 'W2': jax.random.normal(ks[8], (N_EXPERTS, D_MODEL, D_HIDDEN), jnp.float32) * s(D_HIDDEN), 'b2': jnp.zeros((N_EXPERTS, D_MODEL), jnp.float32)}
    _L1_ffn_in = _L1_ffn_setup()
    _d = {'L0_attn_x': _L0_attn_in['x'], 'L0_attn_wq': _L0_attn_in['wq'], 'L0_attn_bq': _L0_attn_in['bq'], 'L0_attn_wk': _L0_attn_in['wk'], 'L0_attn_bk': _L0_attn_in['bk'], 'L0_attn_wv': _L0_attn_in['wv'], 'L0_attn_bv': _L0_attn_in['bv'], 'L0_attn_wo': _L0_attn_in['wo'], 'L0_attn_bo': _L0_attn_in['bo'], 'L0_attn_qn_w': _L0_attn_in['qn_w'], 'L0_attn_kn_w': _L0_attn_in['kn_w'], 'L0_ffn_gate_w': _L0_ffn_in['gate_w'], 'L0_ffn_gate_b': _L0_ffn_in['gate_b'], 'L0_ffn_w1': _L0_ffn_in['w1'], 'L0_ffn_b1': _L0_ffn_in['b1'], 'L0_ffn_w2': _L0_ffn_in['w2'], 'L0_ffn_b2': _L0_ffn_in['b2'], 'L1_attn_A_log': _L1_attn_in['A_log'], 'L1_attn_D': _L1_attn_in['D'], 'L1_attn_C_re': _L1_attn_in['C_re'], 'L1_attn_C_im': _L1_attn_in['C_im'], 'L1_attn_log_dt': _L1_attn_in['log_dt'], 'L1_ffn_norm1_w': _L1_ffn_in['norm1_w'], 'L1_ffn_norm2_w': _L1_ffn_in['norm2_w'], 'L1_ffn_Wq': _L1_ffn_in['Wq'], 'L1_ffn_Wdkv': _L1_ffn_in['Wdkv'], 'L1_ffn_Wuk': _L1_ffn_in['Wuk'], 'L1_ffn_Wuv': _L1_ffn_in['Wuv'], 'L1_ffn_Wo': _L1_ffn_in['Wo'], 'L1_ffn_ln_g': _L1_ffn_in['ln_g'], 'L1_ffn_ln_b': _L1_ffn_in['ln_b'], 'L1_ffn_gate_w': _L1_ffn_in['gate_w'], 'L1_ffn_gate_b': _L1_ffn_in['gate_b'], 'L1_ffn_W1': _L1_ffn_in['W1'], 'L1_ffn_b1': _L1_ffn_in['b1'], 'L1_ffn_W2': _L1_ffn_in['W2'], 'L1_ffn_b2': _L1_ffn_in['b2']}
    _x0 = _d['L0_attn_x']
    _d['L0_attn_x'] = jax.random.normal(jax.random.fold_in(jax.random.key(seed), 1), (1, 2048, 128), dtype=_x0.dtype)
    del _x0
    return _d

def reference(L0_attn_x, L0_attn_wq, L0_attn_bq, L0_attn_wk, L0_attn_bk, L0_attn_wv, L0_attn_bv, L0_attn_wo, L0_attn_bo, L0_attn_qn_w, L0_attn_kn_w, L0_ffn_gate_w, L0_ffn_gate_b, L0_ffn_w1, L0_ffn_b1, L0_ffn_w2, L0_ffn_b2, L1_attn_A_log, L1_attn_D, L1_attn_C_re, L1_attn_C_im, L1_attn_log_dt, L1_ffn_norm1_w, L1_ffn_norm2_w, L1_ffn_Wq, L1_ffn_Wdkv, L1_ffn_Wuk, L1_ffn_Wuv, L1_ffn_Wo, L1_ffn_ln_g, L1_ffn_ln_b, L1_ffn_gate_w, L1_ffn_gate_b, L1_ffn_W1, L1_ffn_b1, L1_ffn_W2, L1_ffn_b2):

    def _L0_attn_ref(x, wq, bq, wk, bk, wv, bv, wo, bo, qn_w, kn_w):
        import jax, jax.numpy as jnp
        import numpy as np
        E, H, W = (128, 16, 32)
        D = E // H

        def _rmsnorm(t, w):
            eps = jnp.finfo(t.dtype).eps
            return t * jax.lax.rsqrt(jnp.mean(t * t, axis=-1, keepdims=True) + eps) * w
        B, T, _ = x.shape
        q = (x @ wq + bq).reshape(B, T, H, D).transpose(0, 2, 1, 3)
        k = (x @ wk + bk).reshape(B, T, H, D).transpose(0, 2, 1, 3)
        v = (x @ wv + bv).reshape(B, T, H, D).transpose(0, 2, 1, 3)
        q = _rmsnorm(q, qn_w)
        k = _rmsnorm(k, kn_w)
        scores = jnp.einsum('bhqd,bhkd->bhqk', q, k) / jnp.sqrt(jnp.float32(D))
        row = jnp.arange(T)[:, None]
        col = jnp.arange(T)[None, :]
        invalid = (col > row) | (row - col >= W)
        neg_inf = jnp.float32(-jnp.inf)
        scores = jnp.where(invalid, neg_inf, scores)
        masked_attn = jnp.where(invalid, 0.0, jax.nn.softmax(scores, axis=-1))
        gene_means = jnp.mean(jax.nn.sigmoid(masked_attn), axis=-1)
        denom = gene_means + 0.5
        sum_inv = jnp.sum(1.0 / denom, axis=2, keepdims=True)
        fitness = 1.0 / (denom * sum_inv)
        scores = scores + jnp.log(fitness)[..., None]
        attn = jax.nn.softmax(scores, axis=-1)
        out = jnp.einsum('bhqk,bhkd->bhqd', attn, v)
        out = out.transpose(0, 2, 1, 3).reshape(B, T, E)
        return out @ wo + bo

    def _L0_ffn_ref(x, gate_w, gate_b, w1, b1, w2, b2):
        import jax, jax.numpy as jnp
        import numpy as np
        B, S, D, H, E = (4, 256, 128, 512, 8)
        b, s, d = x.shape
        xf = x.reshape(-1, d)
        logits = xf @ gate_w.T + gate_b
        top1 = jnp.argmax(logits, axis=-1)
        out = jnp.zeros_like(xf)
        n_experts = w1.shape[0]
        for e in range(n_experts):
            h = jax.nn.relu(xf @ w1[e].T + b1[e])
            y = h @ w2[e].T + b2[e]
            out = out + jnp.where((top1 == e)[:, None], y, jnp.zeros((), y.dtype))
        return out.reshape(b, s, d)

    def _L1_attn_ref(u, A_log, D, C_re, C_im, log_dt):
        import jax, jax.numpy as jnp
        import numpy as np
        B, L, D_MODEL, D_STATE = (8, 512, 128, 64)
        L_ = u.shape[1]
        dt = jnp.exp(log_dt)
        A = -jnp.exp(A_log)
        t = jnp.arange(L_, dtype=u.dtype)
        at = dt[:, None, None] * A[None, None, :] * t[None, :, None]
        K = jnp.einsum('mn,mln->ml', C_re, jnp.exp(at))
        u_f = jnp.fft.rfft(u.transpose(0, 2, 1), n=2 * L_)
        k_f = jnp.fft.rfft(K, n=2 * L_)
        y = jnp.fft.irfft(u_f * k_f, n=2 * L_)[..., :L_]
        return y.transpose(0, 2, 1) + u * D

    def _L1_ffn_ref(x, norm1_w, norm2_w, Wq, Wdkv, Wuk, Wuv, Wo, ln_g, ln_b, gate_w, gate_b, W1, b1, W2, b2):
        import jax, jax.numpy as jnp
        import numpy as np
        D_MODEL = 128
        N_HEADS = 16
        HEAD_DIM = D_MODEL // N_HEADS
        KV_LATENT = 64
        N_EXPERTS = 4
        D_HIDDEN = 4 * D_MODEL
        B, T = (2, 128)

        def rmsnorm(x, w, eps=1e-06):
            return w * (x * jax.lax.rsqrt(jnp.mean(x * x, axis=-1, keepdims=True) + eps))

        def layernorm(x, g, b, eps=1e-05):
            mu = jnp.mean(x, axis=-1, keepdims=True)
            var = jnp.mean((x - mu) ** 2, axis=-1, keepdims=True)
            return (x - mu) * jax.lax.rsqrt(var + eps) * g + b

        def apply_rope(x):
            t, d = (x.shape[2], x.shape[3])
            half = d // 2
            pos = jnp.arange(t, dtype=x.dtype)[:, None]
            inv_freq = 1.0 / 10000.0 ** (jnp.arange(half, dtype=x.dtype) / half)
            ang = pos * inv_freq[None, :]
            sin, cos = (jnp.sin(ang), jnp.cos(ang))
            x1, x2 = (x[..., :half], x[..., half:])
            return jnp.concatenate([x1 * cos - x2 * sin, x1 * sin + x2 * cos], axis=-1)

        def mla_attention(x, Wq, Wdkv, Wuk, Wuv, Wo, ln_g, ln_b):
            b, t, _ = x.shape
            q = (x @ Wq.T).reshape(b, t, N_HEADS, HEAD_DIM).transpose(0, 2, 1, 3)
            latent = layernorm(x @ Wdkv.T, ln_g, ln_b)
            k = (latent @ Wuk.T).reshape(b, t, N_HEADS, HEAD_DIM).transpose(0, 2, 1, 3)
            v = (latent @ Wuv.T).reshape(b, t, N_HEADS, HEAD_DIM).transpose(0, 2, 1, 3)
            q = apply_rope(q)
            k = apply_rope(k)
            scores = jnp.einsum('bhqd,bhkd->bhqk', q, k) / np.sqrt(HEAD_DIM)
            causal = jnp.tril(jnp.ones((t, t), dtype=bool))
            scores = jnp.where(causal, scores, -jnp.inf)
            attn = jax.nn.softmax(scores, axis=-1)
            out = jnp.einsum('bhqk,bhkd->bhqd', attn, v).transpose(0, 2, 1, 3).reshape(b, t, D_MODEL)
            return out @ Wo.T

        def moe(x, gate_w, gate_b, W1, b1, W2, b2):
            logits = x @ gate_w.T + gate_b
            top = jnp.argmax(logits, axis=-1)
            onehot = jax.nn.one_hot(top, N_EXPERTS, dtype=x.dtype)
            h = jax.nn.relu(jnp.einsum('btd,ehd->bteh', x, W1) + b1)
            y = jnp.einsum('bteh,edh->bted', h, W2) + b2
            return jnp.einsum('bted,bte->btd', y, onehot)
        x = x + mla_attention(rmsnorm(x, norm1_w), Wq, Wdkv, Wuk, Wuv, Wo, ln_g, ln_b)
        x = x + moe(rmsnorm(x, norm2_w), gate_w, gate_b, W1, b1, W2, b2)
        return x
    x = L0_attn_x
    x = x + 0.5 * _L0_ffn_ref(_layernorm(x, axis=-1), L0_ffn_gate_w, L0_ffn_gate_b, L0_ffn_w1, L0_ffn_b1, L0_ffn_w2, L0_ffn_b2)
    x = x + _L0_attn_ref(_layernorm(x, axis=-1), L0_attn_wq, L0_attn_bq, L0_attn_wk, L0_attn_bk, L0_attn_wv, L0_attn_bv, L0_attn_wo, L0_attn_bo, L0_attn_qn_w, L0_attn_kn_w)
    x = x + 0.5 * _L0_ffn_ref(_layernorm(x, axis=-1), L0_ffn_gate_w, L0_ffn_gate_b, L0_ffn_w1, L0_ffn_b1, L0_ffn_w2, L0_ffn_b2)
    x = x + 0.5 * _L1_ffn_ref(_layernorm(x, axis=-1), L1_ffn_norm1_w, L1_ffn_norm2_w, L1_ffn_Wq, L1_ffn_Wdkv, L1_ffn_Wuk, L1_ffn_Wuv, L1_ffn_Wo, L1_ffn_ln_g, L1_ffn_ln_b, L1_ffn_gate_w, L1_ffn_gate_b, L1_ffn_W1, L1_ffn_b1, L1_ffn_W2, L1_ffn_b2)
    x = x + _L1_attn_ref(_layernorm(x, axis=-1), L1_attn_A_log, L1_attn_D, L1_attn_C_re, L1_attn_C_im, L1_attn_log_dt)
    x = x + 0.5 * _L1_ffn_ref(_layernorm(x, axis=-1), L1_ffn_norm1_w, L1_ffn_norm2_w, L1_ffn_Wq, L1_ffn_Wdkv, L1_ffn_Wuk, L1_ffn_Wuv, L1_ffn_Wo, L1_ffn_ln_g, L1_ffn_ln_b, L1_ffn_gate_w, L1_ffn_gate_b, L1_ffn_W1, L1_ffn_b1, L1_ffn_W2, L1_ffn_b2)
    return x

_drawn_inputs = setup_inputs


def setup_inputs(seed=0):
    import zlib

    import numpy as np

    out = dict(_drawn_inputs(seed))
    spreads = {'L0_attn_bq': (0.0, 0.1),
     'L0_attn_bk': (0.0, 0.496),
     'L0_attn_bv': (0.0, 0.1),
     'L0_attn_bo': (0.0, 0.1),
     'L0_attn_qn_w': (1.0, 0.6),
     'L0_attn_kn_w': (1.0, 0.2),
     'L1_attn_log_dt': (-4.605170249938965, 0.2),
     'L1_ffn_norm1_w': (1.0, 0.2),
     'L1_ffn_norm2_w': (1.0, 0.2),
     'L1_ffn_ln_g': (1.0, 0.2),
     'L1_ffn_ln_b': (0.0, 0.1),
     'L1_ffn_gate_b': (0.0, 0.1),
     'L1_ffn_b1': (0.0, 0.1),
     'L1_ffn_b2': (0.0, 0.1)}
    factors = {'L1_attn_D': 3.334}
    for name, (base, spread) in spreads.items():
        noise = np.random.default_rng([zlib.crc32(name.encode()), seed]).standard_normal(out[name].shape)
        drawn = base * np.exp(spread * noise) if base else spread * noise
        out[name] = jnp.asarray(drawn.astype(out[name].dtype))
    for name, factor in factors.items():
        out[name] = (out[name] * factor).astype(out[name].dtype)
    return out
```

```python
from contextlib import ExitStack

import concourse.bass as bass
from concourse import mybir

F32 = mybir.dt.float32
BF16 = mybir.dt.bfloat16
ALU = mybir.AluOpType
ACT = mybir.ActivationFunctionType
AX = mybir.AxisListType

P = 128
T = 2048
NT = T // P
D = 128
NH = 16
HD = D // NH
W = 32
HID = 512
HC = HID // P
NE0, NE1 = 8, 4
KV = 64
NS = 64
GT = 4
NG = NT // GT
GW = GT * P
SLOT = 64
MASKED = -1e30
EPS_LN, EPS_RMS = 1e-5, 1e-6
EPS_F32 = 1.1920928955078125e-07
INV_SQRT_HD = 1.0 / HD ** 0.5


class Core:

    def __init__(self, nc, ctx):
        self.nc, self.ctx = nc, ctx
        self.eng = {"pe": nc.tensor, "dve": nc.vector, "act": nc.scalar, "pool": nc.gpsimd, "sp": nc.sync}
        self.seen = {e: {} for e in self.eng}
        self.last = {}
        self.count = {}
        self.sems = {}
        self.stage_name = ""

    def stage(self, name):
        self.stage_name = name

    def sem(self, name):
        if name not in self.sems:
            self.sems[name] = self.ctx.enter_context(self.nc.semaphore(name))
            self.count[name] = 0
        return self.sems[name]

    def wait(self, engine, *tokens):
        for token in tokens:
            if token is None:
                continue
            name, value = token
            if self.seen[engine].get(name, 0) < value:
                self.seen[engine][name] = value
                self.eng[engine].wait_ge(self.sems[name], value)

    def done(self, engine, instruction):
        name = f"{self.stage_name}_{engine}"
        instruction.then_inc(self.sem(name), 1)
        self.count[name] += 1
        self.last[engine] = (name, self.count[name])
        return self.last[engine]

    def dma(self, engine, name, out, in_):
        sem = self.sem(name)
        self.eng[engine].dma_start(out, in_).then_inc(sem, 16)
        self.count[name] += 16
        return name, self.count[name]

    def barrier(self):
        for engine in ("pe", "dve", "act", "pool"):
            self.wait(engine, *self.last.values())


def bcast(ap, n):
    return ap.unsqueeze(len(ap.shape)).broadcast_to(list(ap.shape) + [n])


def on_all(ap, offset, n):
    return bass.AP(tensor=ap.tensor, offset=offset, ap=[[0, P], [1, n]])


def build(nc, ins, out, upto=6):
    with ExitStack() as ctx:
        core = Core(nc, ctx)
        wait, done, dma, barrier = core.wait, core.done, core.dma, core.barrier
        pe, dve, act, pool = nc.tensor, nc.vector, nc.scalar, nc.gpsimd

        def sb(name, shape, dt=F32):
            return ctx.enter_context(nc.sbuf_tensor(name, shape, dt))

        psum = ctx.enter_context(nc.psum_tensor("psum", [P, 8, GW], F32))
        bank_free = [[] for _ in range(8)]

        X = sb("X", [P, NT, D])
        Y = sb("Y", [P, NT, D])
        YT = sb("YT", [P, T])
        ACC = sb("ACC", [P, NT, D])
        ident = sb("ident", [P, P])
        identb = sb("identb", [P, P], BF16)
        stats = sb("stats", [P, NT, 6])
        meanvar = sb("meanvar", [P, NT, 2])
        rstd = sb("rstd", [P, NT])
        small = sb("small", [P, 8, P])

        big_w = sb("big_w", [P, 64 * 129])
        w1_0 = big_w[:, 0:NE0 * HID].rearrange("p (e h) -> p e h", e=NE0)
        w2_0 = big_w[:, NE0 * HID:2 * NE0 * HID].rearrange("p (e c d) -> p e c d", e=NE0, c=HC)
        E_far = big_w[:, :].rearrange("p (a x) -> p a x", a=64)
        w4 = sb("w4", [P, 2 * NE1 * HID])
        w1_1 = w4[:, 0:NE1 * HID].rearrange("p (e h) -> p e h", e=NE1)
        w2_1 = w4[:, NE1 * HID:2 * NE1 * HID].rearrange("p (e c d) -> p e c d", e=NE1, c=HC)

        ARENA = 112 * 256
        arena = sb("arena", [P, ARENA])

        def take(start, n, dt=F32):
            part = arena[:, start:start + n]
            return part if dt is F32 else part.bitcast(dt)

        hidden = [take(96 * 256 + i * 8 * 256, HC * GW).rearrange("p (c t) -> p c t", c=HC) for i in range(2)]

        def load(name, shape, src, dt=F32, engine="sp", group="ld_const"):
            t = sb(name, shape, dt)
            return t, dma(engine, group, t[:], src)

        x_view = ins["L0_attn_x"][0].rearrange("(i p) f -> p i f", p=P)
        x_in = [dma("sp", f"ld_x{g}", X[:, GT * g:GT * g + GT, :], x_view[:, GT * g:GT * g + GT, :]) for g in range(NG)]
        small_group = "ld_moe0"
        gate0, _ = load("gate0", [P, NE0], ins["gate0"], group=small_group, engine="act")
        gateb0, _ = load("gateb0", [P, NE0], on_all(ins["L0_ffn_gate_b"], 0, NE0), group=small_group, engine="act")
        b1_0, _ = load("b1_0", [P, NE0 * HC], ins["b1_0"], group=small_group, engine="act")
        b2_0, _ = load("b2_0", [NE0, D], ins["L0_ffn_b2"], group=small_group, engine="act")
        order0, _ = load("order0", [P, NE0], ins["order0"], group=small_group, engine="act")
        dma("act", small_group, w1_0, ins["w1_0"])
        moe0_in = dma("act", small_group, w2_0, ins["w2_0"])

        wqkv, _ = load("wqkv", [P, 3 * D], ins["wqkv"])
        qk_w = sb("qk_w", [P, 2, HD])
        dma("sp", "ld_const", qk_w[:, 0, :], on_all(ins["L0_attn_qn_w"], 0, HD))
        dma("sp", "ld_const", qk_w[:, 1, :], on_all(ins["L0_attn_kn_w"], 0, HD))
        wo0, _ = load("wo0", [P, D], ins["L0_attn_wo"])
        bo, _ = load("bo", [P, D], on_all(ins["L0_attn_bo"], 0, D))
        window_mask, _ = load("window_mask", [P, 2, 2 * W], ins["window_mask"])
        gate1, _ = load("gate1", [P, NE1], ins["gate1"])
        gateb1, _ = load("gateb1", [P, NE1], on_all(ins["L1_ffn_gate_b"], 0, NE1))
        b1_1, _ = load("b1_1", [P, NE1 * HC], ins["b1_1"])
        b2_1, _ = load("b2_1", [NE1, D], ins["L1_ffn_b2"])
        order1, _ = load("order1", [P, NE1], ins["order1"])
        norm_w, _ = load("norm_w", [P, 2], ins["norm_w"])
        ln_gb, _ = load("ln_gb", [KV, 2], ins["ln_gb"])
        wqd, _ = load("wqd", [P, D + KV], ins["wqd"])
        wukv, _ = load("wukv", [KV, 2 * D], ins["wukv"])
        wo1, _ = load("wo1", [P, D], ins["wo1"])
        rope, _ = load("rope", [P, 2, NT, HD], ins["rope"])
        skip_d, _ = load("skip_d", [P, D], on_all(ins["L1_attn_D"], 0, D))
        c_pair, _ = load("c_pair", [P, 64], ins["c_pair"])
        logdt_pair = sb("logdt_pair", [P, 64])
        for r in range(2):
            dma("sp", "ld_const", logdt_pair[64 * r:64 * r + 64, :],
                bass.AP(tensor=ins["logdt_pair"].tensor, offset=64 * r, ap=[[0, 64], [1, 64]]))
        alog_col = sb("alog_col", [P, 1])
        for r in range(2):
            dma("sp", "ld_const", alog_col[64 * r:64 * r + 64, :], ins["alog_col"])
        logdt_all, alog_all = small[:, 5, :], small[:, 6, 0:NS]
        back_col, _ = load("back_col", [P, 1], ins["back_col"])
        dma("sp", "ld_const", w1_1, ins["w1_1"])
        const_in = dma("sp", "ld_const", w2_1, ins["w2_1"])

        core.stage("setup")
        ones = sb("ones", [P, P])
        mask_q = sb("mask_q", [P, P], BF16)
        mask_k = sb("mask_k", [P, P], BF16)
        pairs2 = sb("pairs2", [P, 32])
        t_z = done("pool", pool.memset(ident[:], 0.0))
        wait("pool", t_z)
        t_id = done("pool", pool.affine_select(out=ident[:], in_=ident[:], compare_op=ALU.not_equal, fill=1.0,
                                               base=0, pattern=[[-1, P]], channel_multiplier=1))
        wait("pool", t_id)
        t_idb = done("pool", pool.tensor_copy(identb[:], ident[:]))
        t_m = done("pool", pool.memset(mask_q[:], 0.0))
        t_m2 = done("pool", pool.memset(mask_k[:], 0.0))
        t_ones = done("pool", pool.memset(ones[:], 1.0))
        t_p = done("pool", pool.memset(pairs2[:], 0.0))
        wait("pool", t_p)
        done("pool", pool.affine_select(out=mask_q[:], in_=mask_q[:], compare_op=ALU.is_ge, fill=MASKED,
                                        base=0, pattern=[[-1, P]], channel_multiplier=1))
        done("pool", pool.affine_select(out=mask_k[:], in_=mask_k[:], compare_op=ALU.is_ge, fill=MASKED,
                                        base=0, pattern=[[1, P]], channel_multiplier=-1))
        for r in range(2):
            wait("pool", core.last["pool"])
            t_setup = done("pool", pool.memset(pairs2[64 * r:64 * r + 64, r:r + 1], 1.0))
        wait("pe", t_setup)

        def layer_norm(ready):
            tok = []
            for i in range(NT):
                wait("dve", ready[i // GT])
                tok.append(done("dve", dve.bn_stats(stats[:, i, :], X[:, i, :])))
            for i in range(NT):
                wait("dve", tok[i])
                t = done("dve", dve.bn_aggr(meanvar[:, i, :], stats[:, i, :]))
            t = rsqrt(meanvar[:, :, 1], rstd[:, :], 1.0, EPS_LN, t)
            wait("dve", t)
            return [done("dve", dve.tensor_scalar(Y[:, i, :], X[:, i, :], meanvar[:, i, 0:1], rstd[:, i:i + 1],
                                                  ALU.subtract, ALU.mult)) for i in range(NT)]

        def rsqrt(src, dst, scale, eps, ready):
            wait("dve", ready)
            t = done("dve", dve.tensor_scalar(dst, src, scale, eps, ALU.mult, ALU.add))
            wait("act", t)
            t = done("act", act.activation(dst, dst, ACT.Sqrt))
            wait("dve", t)
            return done("dve", dve.reciprocal(dst, dst))

        def rms_stats(src, ready):
            for i in range(NT):
                wait("act", ready[i])
                t = done("act", act.activation(ACC[:, i, :], src[:, i, :], ACT.Square,
                                               accum_out=rstd[:, i:i + 1]))
            return rsqrt(rstd[:, :], rstd[:, :], 1.0 / D, EPS_RMS, t)

        def feature_major(src, ready, scale_col=None, banks=(6, 7)):
            tok = []
            for g in range(NG):
                b = banks[g % 2]
                wait("pe", *bank_free[b])
                for i in range(GT):
                    wait("pe", ready[GT * g + i])
                    mm = pe.transpose(psum[:, b, i * P:(i + 1) * P], src[:, GT * g + i, :], ident[:])
                t = done("pe", mm)
                dst = YT[:, g * GW:(g + 1) * GW]
                if g % 2:
                    wait("act", t)
                    t = done("act", act.activation(dst, psum[:, b, :], ACT.Copy) if scale_col is None
                             else act.activation(dst, psum[:, b, :], ACT.Identity, scale=scale_col))
                else:
                    wait("dve", t)
                    t = done("dve", dve.tensor_copy(dst, psum[:, b, :]) if scale_col is None
                             else dve.tensor_scalar(dst, psum[:, b, :], scale_col, None, ALU.mult))
                bank_free[b] = [t]
                tok.append(t)
            return tok

        def moe(n_exp, yt_ready, gate, gate_b, order, w1, b1, w2, b2, weights_in, residual=None):
            log = small[:, 0, 0:NT * n_exp].rearrange("p (i e) -> p i e", e=n_exp)
            eq = small[:, 1, 0:NT * n_exp].rearrange("p (i e) -> p i e", e=n_exp)
            hot = small[:, 2, 0:NT * n_exp].rearrange("p (i e) -> p i e", e=n_exp)
            best = small[:, 3, 0:NT]
            best2 = small[:, 4, 0:NT]
            hot_t = hidden[1][0:n_exp, 0, :]
            wait("pe", weights_in, *bank_free[7])
            for i in range(NT):
                wait("pe", yt_ready[i // GT])
                mm = pe.matmul(psum[:, 7, i * n_exp:(i + 1) * n_exp], YT[:, i * P:(i + 1) * P], gate[:],
                               start=True, stop=True)
            t = done("pe", mm)
            wait("dve", t, weights_in)
            t = done("dve", dve.tensor_tensor(log, psum[:, 7, 0:NT * n_exp].rearrange("p (i e) -> p i e", e=n_exp),
                                              gate_b[:].unsqueeze(1).broadcast_to([P, NT, n_exp]), ALU.add))
            bank_free[7] = [t]
            wait("dve", t)
            t = done("dve", dve.tensor_reduce(best, log, AX.X, ALU.max))
            wait("dve", t)
            t = done("dve", dve.tensor_tensor(eq, log, bcast(best, n_exp), ALU.is_ge))
            wait("dve", t)
            t = done("dve", dve.tensor_tensor(eq, eq, order[:].unsqueeze(1).broadcast_to([P, NT, n_exp]), ALU.mult))
            wait("dve", t)
            t = done("dve", dve.tensor_reduce(best2, eq, AX.X, ALU.max))
            wait("dve", t)
            t_hot = done("dve", dve.tensor_tensor(hot, eq, bcast(best2, n_exp), ALU.is_equal))

            def output_bias():
                wait("pe", t_hot)
                acc_tok = []
                for g in range(NG):
                    wait("pe", *bank_free[7])
                    for i in range(GT):
                        mm = pe.transpose(psum[0:n_exp, 7, i * P:(i + 1) * P], hot[:, GT * g + i, :], ident[:])
                    t = done("pe", mm)
                    wait("dve", t)
                    t = done("dve", dve.tensor_copy(hot_t, psum[0:n_exp, 7, :]))
                    wait("pe", t)
                    for i in range(GT):
                        mm = pe.matmul(psum[:, 7, i * P:(i + 1) * P],
                                       hot_t[:, i * P:(i + 1) * P], b2[:], start=True, stop=True)
                    t = done("pe", mm)
                    hid_free[1] = t
                    wait("dve", t)
                    dst = ACC[:, GT * g:GT * g + GT, :]
                    bias = psum[:, 7, :].rearrange("p (i d) -> p i d", i=GT)
                    t = done("dve", dve.tensor_copy(dst, bias) if residual is None else
                             dve.tensor_tensor(dst, bias, residual[:, GT * g:GT * g + GT, :], ALU.add))
                    bank_free[7] = [t]
                    acc_tok.append(t)
                return acc_tok

            units = [(e, g) for e in range(n_exp) for g in range(NG)]
            hid_ready, hid_free, acc_tok = {}, [None, None], None

            def layer1(u):
                e, g = units[u]
                hid = hidden[u % 2]
                toks = []
                for c in range(HC):
                    wait("pe", yt_ready[g], *bank_free[c])
                    t = done("pe", pe.matmul(psum[:, c, :], w1[:, e, c * P:(c + 1) * P], YT[:, g * GW:(g + 1) * GW],
                                             start=True, stop=True))
                    col = b1[:, e * HC + c:e * HC + c + 1]
                    if c % 2 == 0:
                        wait("act", t, hid_free[u % 2])
                        t = done("act", act.activation(hid[:, c, :], psum[:, c, :], ACT.Relu, bias=col))
                    else:
                        wait("dve", t, hid_free[u % 2])
                        t = done("dve", dve.tensor_scalar(hid[:, c, :], psum[:, c, :], col, 0.0, ALU.add, ALU.max))
                    bank_free[c] = [t]
                    toks.append(t)
                hid_ready[u] = toks

            def layer2(u):
                e, g = units[u]
                hid, b = hidden[u % 2], 4 + u % 2
                wait("pe", *hid_ready[u], *bank_free[b])
                for i in range(GT):
                    for c in range(HC):
                        mm = pe.matmul(psum[:, b, i * P:(i + 1) * P], hid[:, c, i * P:(i + 1) * P], w2[:, e, c, :],
                                       start=(c == 0), stop=(c == HC - 1))
                t = done("pe", mm)
                hid_free[u % 2] = t
                wait("dve", t)
                for i in range(GT):
                    n = GT * g + i
                    wait("dve", acc_tok[n])
                    acc_tok[n] = done("dve", dve.scalar_tensor_tensor(
                        out=ACC[:, n, :], in0=psum[:, b, i * P:(i + 1) * P], scalar=hot[:, n, e:e + 1],
                        in1=ACC[:, n, :], op0=ALU.mult, op1=ALU.add))
                bank_free[b] = [acc_tok[GT * g + GT - 1]]

            layer1(0)
            acc_tok = [t for t in output_bias() for _ in range(GT)]
            for u in range(len(units)):
                if u + 1 < len(units):
                    layer1(u + 1)
                layer2(u)
            return acc_tok

        def add_half(ready):
            tok = []
            for g in range(NG):
                wait("dve", *ready[GT * g:GT * g + GT])
                s = slice(GT * g, GT * g + GT)
                tok.append(done("dve", dve.scalar_tensor_tensor(out=X[:, s, :], in0=ACC[:, s, :], scalar=0.5,
                                                                in1=X[:, s, :], op0=ALU.mult, op1=ALU.add)))
            return tok

        def macaron_ffn(name, x_ready):
            core.stage(name)
            y = layer_norm(x_ready)
            yt = feature_major(Y, y)
            acc = moe(NE0, yt, gate0, gateb0, order0, w1_0, b1_0, w2_0, b2_0, moe0_in)
            tok = add_half(acc)
            barrier()
            return tok

        def split3(src, dst, rest, is_query, ready, free):
            def slot(k):
                return dst[:, :, k * HD:(k + 1) * HD]

            where = ((0, 1, 2), (3, 4), (5,)) if is_query else ((0, 3, 5), (1, 4), (2,))
            wait("dve", ready, *free)
            wait("act", *free)
            part = src
            toks = []
            for k in range(3):
                t = done("dve", dve.tensor_copy(slot(where[k][0]), part))
                for other in where[k][1:]:
                    wait("act", t)
                    toks.append(done("act", act.activation(slot(other), slot(where[k][0]), ACT.Copy)))
                if k < 2:
                    wait("dve", t)
                    t = done("dve", dve.tensor_tensor(rest, part, slot(where[k][0]), ALU.subtract))
                    wait("dve", t)
                    part = rest
            return [t, toks[-1]]

        def to_rows(src, n_tiles, dst_of, ready, banks, engine_of):
            toks = []
            for i in range(n_tiles):
                b = banks[i % len(banks)]
                half = psum[:, b, :].bitcast(BF16).rearrange("p (a t) -> p a t", a=8)
                wait("pe", *ready, *bank_free[b])
                for a in range(8):
                    mm = pe.transpose(half[:, a, :], src[:, i, a * P:(a + 1) * P], identb[:])
                t = done("pe", mm)
                e = engine_of(i)
                wait(e, t)
                t = done(e, act.activation(dst_of(i), half, ACT.Copy) if e == "act" else dve.tensor_copy(dst_of(i), half))
                bank_free[b] = [t]
                toks.append(t)
            return toks

        def windowed_attention(name, x_ready):
            core.stage(name)
            y_ready = layer_norm(x_ready)
            yt_ready = feature_major(Y, y_ready)
            SC = INV_SQRT_HD
            K = 256
            keys = take(0, 8 * (T + W) // 2, BF16).rearrange("p (a t) -> p a t", a=8)
            queries = take(33 * K, 8 * T // 2, BF16).rearrange("p (a t) -> p a t", a=8)
            split_q = take(65 * K, GT * NH * SLOT // 2, BF16).rearrange("p (n s) -> p n s", s=SLOT)
            split_k = take(73 * K, GT * NH * SLOT // 2, BF16).rearrange("p (n s) -> p n s", s=SLOT)
            v_own = take(81 * K, NT * D).rearrange("p (i d) -> p i d", i=NT)
            v_prev = take(89 * K, NT * D).rearrange("p (i d) -> p i d", i=NT)
            raw = take(97 * K, 2 * GT * D).rearrange("p (k i d) -> p k i d", k=2, i=GT)
            sq = take(101 * K, 2 * GT * D).rearrange("p (k i d) -> p k i d", k=2, i=GT)
            rest = take(105 * K, GT * D).rearrange("p (n d) -> p n d", d=HD)
            bqkv = take(107 * K, 3 * D)
            wait("sp", *core.last.values())
            for n, b in enumerate(("L0_attn_bq", "L0_attn_bk", "L0_attn_bv")):
                t_b = dma("sp", name + "_bias", bqkv[:, n * D:(n + 1) * D], on_all(ins[b], 0, D))
            wait("pool", *x_ready)
            wait("dve", t_b)
            wait("dve", const_in)
            wait("pe", const_in)
            t_pad = done("pool", pool.memset(keys[:, :, 0:W], 0.0))
            done("pool", pool.memset(split_q[:, :, 48:64], 0.0))
            t_pad = done("pool", pool.memset(split_k[:, :, 48:64], 0.0))
            r_norm = small[:, 0, 0:2 * GT * NH]
            q_tok, k_tok, v_tok = [], [], []
            free_raw, free_q, free_k = [], [], []
            for g in range(NG):
                for i in range(GT):
                    n, b = GT * g + i, i % 4
                    wait("pe", yt_ready[g], *bank_free[b])
                    t = done("pe", pe.matmul(psum[:, b, 0:3 * D], YT[:, n * P:(n + 1) * P], wqkv[:], start=True, stop=True))
                    wait("dve", t, *free_raw)
                    t_raw = done("dve", dve.tensor_tensor(raw[:, :, i, :], psum[:, b, 0:2 * D].rearrange("p (k d) -> p k d", k=2),
                                                          bqkv[:, 0:2 * D].rearrange("p (k d) -> p k d", k=2), ALU.add))
                    t_v = done("dve", dve.tensor_tensor(v_own[:, n, :], psum[:, b, 2 * D:3 * D], bqkv[:, 2 * D:3 * D], ALU.add))
                    bank_free[b] = [t_v]
                v_tok.append(t_v)
                flat = raw.rearrange("p k i (h e) -> p (k i h) e", e=HD)
                flat_sq = sq.rearrange("p k i (h e) -> p (k i h) e", e=HD)
                wait("act", t_raw)
                t = done("act", act.activation(flat_sq, flat, ACT.Square))
                wait("dve", t)
                t = done("dve", dve.tensor_reduce(r_norm, flat_sq, AX.X, ALU.add))
                t = rsqrt(r_norm, r_norm, 1.0 / HD, EPS_F32, t)
                wait("dve", t)
                t = done("dve", dve.tensor_tensor(flat, flat, bcast(r_norm, HD), ALU.mult))
                wait("dve", t)
                for k in range(2):
                    rows = raw[:, k, :, :].rearrange("p i (h e) -> p (i h) e", e=HD)
                    t = done("dve", dve.tensor_tensor(rows, rows, qk_w[:, k, :].unsqueeze(1).broadcast_to([P, GT * NH, HD]), ALU.mult))
                t_q = split3(raw[:, 0].rearrange("p i (h e) -> p (i h) e", e=HD), split_q, rest, True, t, free_q + [t_pad])
                t_k = split3(raw[:, 1].rearrange("p i (h e) -> p (i h) e", e=HD), split_k, rest, False, t_q[0], free_k)
                free_raw = [t_k[0]]
                base = g * GW
                eng = lambda i: "act" if i % 2 else "dve"
                tq = to_rows(split_q.rearrange("p (i h) s -> p i (h s)", i=GT), GT,
                             lambda i: queries[:, :, base + i * P:base + (i + 1) * P], t_q, (4, 5), eng)
                tk = to_rows(split_k.rearrange("p (i h) s -> p i (h s)", i=GT), GT,
                             lambda i: keys[:, :, W + base + i * P:W + base + (i + 1) * P], t_k, (6, 7), eng)
                free_q, free_k = tq, tk
                q_tok.append(tq)
                k_tok.append(tk)
            wait("sp", *v_tok)
            wait("pool", core.last["pool"])
            t_pad = done("pool", pool.memset(v_prev[0:W, 0:1, :], 0.0))
            wait("pool", t_pad)
            dma("sp", name + "_shift", v_prev[W:P, :, :], v_own[0:P - W, :, :])
            t_vp = dma("sp", name + "_shift", v_prev[0:W, 1:NT, :], v_own[P - W:P, 0:NT - 1, :])
            barrier()

            score = [take((65 + 4 * i) * K, NH * 2 * W).rearrange("p (h w) -> p h w", h=NH) for i in range(3)]
            prob = [YT[:, i * NH * 2 * W:(i + 1) * NH * 2 * W].rearrange("p (h w) -> p h w", h=NH) for i in range(2)]
            prob_t = [take((97 + 4 * i) * K, NH * 2 * W).rearrange("p (h w) -> p h w", h=NH) for i in range(2)]
            per_row = lambda k: take((104 + k) * K, NT * NH).rearrange("p (i h) -> p i h", i=NT)
            mx, ln_, rl, th = per_row(1), per_row(2), per_row(3), per_row(4)
            exp_tok, pt_tok, tanh_tok = {}, {}, {}
            score_free, prob_free, pt_free = {}, {}, {}
            u_tok, th_tok = [], []

            def scores(n):
                sc, b = score[n % 3], 2 * (n % 2)
                wait("pe", *bank_free[b])
                for h in range(NH):
                    r = SLOT * (h % 2)
                    for j in range(4):
                        t0 = n * P + j * W
                        mm = pe.matmul(psum[W * j:W * j + W, b + h % 2, (h // 2) * 2 * W:(h // 2 + 1) * 2 * W],
                                       queries[r:r + SLOT, h // 2, t0:t0 + W], keys[r:r + SLOT, h // 2, t0:t0 + 2 * W],
                                       start=True, stop=True)
                t = done("pe", mm)
                wait("dve", t, *score_free.get(n - 3, []))
                both = psum[:, b:b + 2, :].rearrange("p k (h w) -> p (k h) w", w=2 * W)
                t = done("dve", dve.tensor_tensor(sc, both, window_mask[:, min(n, 1), :].unsqueeze(1).broadcast_to([P, NH, 2 * W]), ALU.add))
                bank_free[b] = [t]
                wait("dve", t)
                t = done("dve", dve.tensor_reduce(mx[:, n, :], sc, AX.X, ALU.max))
                wait("dve", t)
                t = done("dve", dve.tensor_tensor(sc, sc, bcast(mx[:, n, :], 2 * W), ALU.subtract))
                wait("act", t)
                exp_tok[n] = done("act", act.activation(sc, sc, ACT.Exp, scale=SC))

            def normalised(n):
                sc, pt, pr = score[n % 3], prob_t[n % 2], prob[n % 2]
                wait("dve", exp_tok[n])
                t = done("dve", dve.tensor_reduce(ln_[:, n, :], sc, AX.X, ALU.add))
                wait("dve", t)
                t = done("dve", dve.reciprocal(rl[:, n, :], ln_[:, n, :]))
                wait("dve", *pt_free.get(n - 2, []))
                pt_tok[n] = done("dve", dve.transpose(pt.rearrange("p h w -> p (h w)"), sc.rearrange("p h w -> p (h w)")))
                wait("pool", t, *prob_free.get(n - 2, []))
                t_p = done("pool", pool.tensor_tensor(pr, sc, bcast(rl[:, n, :], 2 * W), ALU.mult))
                score_free[n] = [t_p, pt_tok[n]]
                wait("act", t_p)
                tanh_tok[n] = done("act", act.activation(pr, pr, ACT.Tanh, scale=0.5))

            def weighted_values(n):
                pt, ob = prob_t[n % 2], 4 + n % 2
                wait("pe", pt_tok[n], t_vp, t_pad, *bank_free[ob])
                for h in range(NH):
                    s = (h % 2) * 8 + h // 2
                    for k, vals in enumerate((v_prev, v_own)):
                        for j in range(4):
                            q = slice(W * j, W * j + W)
                            mm = pe.matmul(psum[q, ob, h * HD:(h + 1) * HD], pt[q, s, k * W:(k + 1) * W],
                                           vals[q, n, h * HD:(h + 1) * HD], start=(k == 0), stop=(k == 1),
                                           skip_group_check=True)
                t = done("pe", mm)
                pt_free[n] = [t]
                wait("act", t)
                t = done("act", act.activation(ACC[:, n, :], psum[:, ob, 0:D], ACT.Copy))
                bank_free[ob] = [t]
                u_tok.append(t)

            def tanh_sum(n):
                wait("dve", tanh_tok[n])
                t = done("dve", dve.tensor_reduce(th[:, n, :], prob[n % 2], AX.X, ALU.add))
                prob_free[n] = [t]
                th_tok.append(t)

            for n in range(NT + 3):
                if n < NT:
                    scores(n)
                if n >= 3:
                    tanh_sum(n - 3)
                if 1 <= n <= NT:
                    normalised(n - 1)
                if 2 <= n <= NT + 1:
                    weighted_values(n - 2)
            den, inv, fit, shift = th, per_row(5), per_row(6), per_row(7)
            sums = rstd
            wait("dve", th_tok[-1])
            t = done("dve", dve.tensor_scalar(den, th, 0.5 / T, 1.0, ALU.mult, ALU.add))
            wait("dve", t)
            t = done("dve", dve.reciprocal(inv, den))
            wait("dve", t)
            t = done("dve", dve.tensor_reduce(sums[:, :], inv.rearrange("p i h -> p h i"), AX.X, ALU.add))
            wait("pe", t, *bank_free[6])
            t = done("pe", pe.matmul(psum[:, 6, 0:NH], ones[:], sums[:, :], start=True, stop=True))
            wait("dve", t)
            t = done("dve", dve.tensor_tensor(fit, den, psum[:, 6, 0:NH].unsqueeze(1).broadcast_to([P, NT, NH]), ALU.mult))
            bank_free[6] = [t]
            wait("dve", t)
            t = done("dve", dve.reciprocal(fit, fit))
            wait("act", t)
            t_fit = done("act", act.activation(fit, fit, ACT.Ln))
            wait("dve", t_fit)
            t = done("dve", dve.scalar_tensor_tensor(out=inv, in0=mx, scalar=SC, in1=fit, op0=ALU.mult, op1=ALU.add))
            t2 = done("dve", dve.tensor_scalar(mx, mx, SC, None, ALU.mult))
            wait("dve", t2)
            t = done("dve", dve.tensor_tensor(shift, mx, fit, ALU.add))
            wait("dve", t)
            t = done("dve", dve.tensor_tensor(shift, shift, inv, ALU.subtract))
            wait("act", t)
            t = done("act", act.activation(shift, shift, ACT.Exp))
            wait("dve", t)
            t = done("dve", dve.tensor_tensor(ln_, ln_, shift, ALU.mult))
            wait("dve", t)
            t = done("dve", dve.reciprocal(ln_, ln_))
            wait("dve", t)
            t = done("dve", dve.tensor_tensor(ln_, ln_, shift, ALU.mult))
            tok = []
            wait("dve", t)
            for n in range(NT):
                a = ACC[:, n, :].rearrange("p (a k d) -> p k a d", k=2, d=HD)
                f = ln_[:, n, :].rearrange("p (k a) -> p k a", k=2)
                wait("dve", u_tok[n])
                tok.append(done("dve", dve.tensor_tensor(a, a, bcast(f, HD), ALU.mult)))
            wait("pool", *x_ready)
            t_x = done("pool", pool.tensor_tensor(X[:, :, :], X[:, :, :], bo[:].unsqueeze(1).broadcast_to([P, NT, D]), ALU.add))
            return project_out(tok, wo0, X, [t_x] * NG)

        def project_out(att_ready, w, dst, dst_ready):
            at = feature_major(ACC, att_ready)
            tok = []
            for g in range(NG):
                b = 4 + g % 2
                wait("pe", at[g], *bank_free[b])
                for i in range(GT):
                    n = GT * g + i
                    mm = pe.matmul(psum[:, b, i * P:(i + 1) * P], YT[:, n * P:(n + 1) * P], w[:], start=True, stop=True)
                t = done("pe", mm)
                wait("dve", t, dst_ready[g])
                d = dst[:, GT * g:GT * g + GT, :]
                t = done("dve", dve.tensor_tensor(d, psum[:, b, :].rearrange("p (i d) -> p i d", i=GT), d, ALU.add))
                bank_free[b] = [t]
                tok.append(t)
            barrier()
            return tok

        def latent_block(name, x_ready, during_moe=None):
            core.stage(name)
            K = 256
            keys = take(0, 8 * T // 2, BF16).rearrange("p (a t) -> p a t", a=8)
            split_q = [take((32 + 8 * i) * K, GT * NH * SLOT // 2, BF16).rearrange("p (n s) -> p n s", s=SLOT) for i in range(2)]
            plain_q = [take((48 + 8 * i) * K, 8 * GW // 2, BF16).rearrange("p (a t) -> p a t", a=8) for i in range(2)]
            shift_q = [take((64 + 8 * i) * K, 8 * GW // 2, BF16).rearrange("p (a t) -> p a t", a=8) for i in range(2)]
            prob = [take((80 + 4 * i) * K, 2 * GW).rearrange("p (k t) -> p k t", k=2) for i in range(4)]
            split_k = take(92 * K, GT * NH * SLOT // 2, BF16).rearrange("p (n s) -> p n s", s=SLOT)
            values = take(100 * K, NT * NH * 9).rearrange("p (i h d) -> p i h d", i=NT, h=NH)
            lat = take(64 * K, NT * KV).rearrange("p (i d) -> p i d", i=NT)
            lat_t = take(68 * K, T)[0:KV, :]
            raw = take(109 * K, GT * D).rearrange("p (n d) -> p n d", d=HD)
            rest = small[:, 0:4, :].rearrange("p a (n d) -> p (a n) d", d=HD)
            turned = small[:, 4:8, :].rearrange("p a (n d) -> p (a n) d", d=HD)

            y_ready = layer_norm(x_ready)
            t_r = rms_stats(Y, y_ready)
            wait("dve", t_r)
            h_ready = [done("dve", dve.tensor_scalar(ACC[:, i, :], Y[:, i, :], rstd[:, i:i + 1], None, ALU.mult))
                       for i in range(NT)]
            ht = feature_major(ACC, h_ready, norm_w[:, 0:1])
            for half in range(2):
                wait("pe", *bank_free[half])
                for i in range(8):
                    n = 8 * half + i
                    wait("pe", ht[n // GT])
                    mm = pe.matmul(psum[:, half, i * KV:(i + 1) * KV], YT[:, n * P:(n + 1) * P], wqd[:, D:D + KV],
                                   start=True, stop=True)
                t = done("pe", mm)
                wait("act", t)
                t = done("act", act.activation(lat[:, 8 * half:8 * half + 8, :],
                                               psum[:, half, :].rearrange("p (i d) -> p i d", i=8), ACT.Copy))
                bank_free[half] = [t]
                wait("dve", t)
                for n in range(8 * half, 8 * half + 8):
                    t = done("dve", dve.bn_stats(stats[:, n, :], lat[:, n, :]))
            wait("dve", t)
            for n in range(NT):
                t = done("dve", dve.bn_aggr(meanvar[:, n, :], stats[:, n, :]))
            t = rsqrt(meanvar[:, :, 1], rstd[:, :], 1.0, EPS_LN, t)
            wait("dve", t)
            for n in range(NT):
                t_l = done("dve", dve.tensor_scalar(lat[:, n, :], lat[:, n, :], meanvar[:, n, 0:1], rstd[:, n:n + 1],
                                                    ALU.subtract, ALU.mult))
            wait("pe", t_l)
            lt = []
            for g in range(NG):
                b = 2 + g % 2
                wait("pe", *bank_free[b])
                for i in range(GT):
                    mm = pe.transpose(psum[0:KV, b, i * P:(i + 1) * P], lat[:, GT * g + i, :], ident[:])
                t = done("pe", mm)
                wait("dve", t)
                t = done("dve", dve.tensor_scalar(lat_t[:, g * GW:(g + 1) * GW], psum[0:KV, b, :], ln_gb[:, 0:1],
                                                  ln_gb[:, 1:2], ALU.mult, ALU.add))
                bank_free[b] = [t]
                lt.append(t)

            t = done("pool", pool.memset(split_k[:, :, 48:64], 0.0))
            wait("pool", t)
            done("pool", pool.memset(split_k[:, :, 48:51], 1.0))
            done("pool", pool.memset(split_q[0][:, :, 48:64], 0.0))
            done("pool", pool.memset(split_q[1][:, :, 48:64], 0.0))
            t_sp = done("pool", pool.memset(values[:, :, :, 8:9], 1.0))

            def rotate(g, src, ready):
                view = lambda t: t.rearrange("p (i h) d -> p i h d", i=GT)
                table = lambda k, a, b: rope[:, k, GT * g:GT * g + GT, a:b].unsqueeze(2).broadcast_to([P, GT, NH, b - a])
                half = HD // 2
                s, d, r = view(src), view(turned), view(rest)
                wait("dve", ready)
                done("dve", dve.tensor_tensor(d, s, table(0, 0, HD), ALU.mult))
                done("dve", dve.tensor_tensor(r[:, :, :, 0:half], s[:, :, :, half:HD], table(1, 0, half), ALU.mult))
                t = done("dve", dve.tensor_tensor(r[:, :, :, half:HD], s[:, :, :, 0:half], table(1, half, HD), ALU.mult))
                wait("dve", t)
                t = done("dve", dve.tensor_tensor(turned, turned, rest, ALU.add))
                return t

            free_raw, free_k, k_tok, v_tok = [], [], [], []
            for g in range(NG):
                for i in range(GT):
                    n, b = GT * g + i, i % 4
                    wait("pe", lt[g], *bank_free[b])
                    t = done("pe", pe.matmul(psum[:, b, 0:2 * D], lat_t[:, n * P:(n + 1) * P], wukv[:], start=True, stop=True))
                    wait("dve", t, t_sp, *free_raw)
                    t_raw = done("dve", dve.tensor_copy(raw[:, i * NH:(i + 1) * NH, :],
                                                        psum[:, b, 0:D].rearrange("p (h d) -> p h d", h=NH)))
                    t_v = done("dve", dve.tensor_copy(values[:, n, :, 0:HD],
                                                      psum[:, b, D:2 * D].rearrange("p (h d) -> p h d", h=NH)))
                    bank_free[b] = [t_v]
                t = rotate(g, raw, t_raw)
                free_raw = [t]
                t_k = split3(turned, split_k, rest, False, t, free_k)
                free_k = to_rows(split_k.rearrange("p (i h) s -> p i (h s)", i=GT), GT,
                                 lambda i: keys[:, :, g * GW + i * P:g * GW + (i + 1) * P], t_k, (4, 5, 6, 7), lambda i: "act")
                k_tok.append(free_k)
                v_tok.append(t_v)

            work = [5, 6, 7]
            turn = [0]

            def work_bank():
                turn[0] += 1
                return work[turn[0] % 3]

            q_state = {}

            def prepare_q(g):
                nonlocal free_raw
                sq = split_q[g % 2]
                for i in range(GT):
                    n, b = GT * g + i, work_bank()
                    wait("pe", *bank_free[b])
                    t = done("pe", pe.matmul(psum[:, b, 0:D], YT[:, n * P:(n + 1) * P], wqd[:, 0:D], start=True, stop=True))
                    wait("act", t, *free_raw)
                    t = done("act", act.activation(raw[:, i * NH:(i + 1) * NH, :],
                                                   psum[:, b, 0:D].rearrange("p (h d) -> p h d", h=NH), ACT.Copy))
                    bank_free[b] = [t]
                t = rotate(g, raw, t)
                free_raw = [t]
                wait("pool", t_sp, *q_state.get(("done", g - 2), []))
                t_0 = done("pool", pool.memset(sq[:, :, 48:51], 0.0))
                t_q = split3(turned, sq, rest, True, t, [t_0] + q_state.get(("done", g - 2), [])) + [t_0]
                toks = []
                for i in range(GT):
                    b = work_bank()
                    toks += to_rows(sq[:, i * NH:(i + 1) * NH, :].rearrange("p (i h) s -> p i (h s)", i=1), 1,
                                    lambda _: plain_q[g % 2][:, :, i * P:(i + 1) * P], t_q, (b,), lambda _: "act")
                q_state[g] = toks

            row_max = take(111 * K, 64).rearrange("p (n c) -> p n c", c=4)
            shift = take(111 * K + 64, GT * 4)
            part = take(111 * K + 80, GT * 4)
            inv_flat = take(111 * K + 96, GT * 4)

            def max_items(g, hq):
                items = []
                pq, sq, fq = plain_q[g % 2], split_q[g % 2], shift_q[(4 * g + hq) % 2]
                toks = {}

                def one(i, hh, c):
                    h, n = 4 * hq + hh, GT * g + i
                    r, w = 64 * (h % 2), min(GW, (n + 1) * P - c * GW)
                    diag = (c * GW + w) == (n + 1) * P
                    b = work_bank()
                    wait("pe", q_state[g][i], *k_tok[min(c, NG - 1)], *bank_free[b])
                    mm = pe.matmul(psum[:, b, 0:w], pq[r:r + SLOT, h // 2, i * P:(i + 1) * P],
                                   keys[r:r + SLOT, h // 2, c * GW:c * GW + w], start=True, stop=not diag)
                    if diag:
                        mm = pe.matmul(psum[:, b, w - P:w], identb[:], mask_q[:], start=False, stop=True)
                    t = done("pe", mm)
                    wait("dve", t, *q_state.get("max_free", []))
                    t = done("dve", dve.tensor_reduce(row_max[:, i * 4 + hh, c:c + 1], psum[:, b, 0:w], AX.X, ALU.max))
                    bank_free[b] = [t]
                    toks["last"] = t

                for i in range(GT):
                    for hh in range(4):
                        for c in range(g + 1):
                            items.append(lambda i=i, hh=hh, c=c: one(i, hh, c))

                def finish():
                    wait("dve", toks["last"])
                    t = done("dve", dve.tensor_reduce(shift, row_max[:, :, 0:g + 1], AX.X, ALU.max, negate=True))
                    q_state["max_free"] = [t]
                    heads = sq.rearrange("p (i h) s -> p i h s", i=GT)[:, :, 4 * hq:4 * hq + 4, :]
                    s3 = shift.rearrange("p (i h) -> p i h", i=GT)
                    p3 = part.rearrange("p (i h) -> p i h", i=GT)
                    src = s3
                    for k in range(3):
                        wait("dve", t)
                        t = done("dve", dve.tensor_copy(heads[:, :, :, 48 + k], src))
                        if k < 2:
                            wait("dve", t)
                            t = done("dve", dve.tensor_tensor(p3, src, heads[:, :, :, 48 + k], ALU.subtract))
                            src = p3
                    b = work_bank()
                    half = psum[:, b, :].bitcast(BF16).rearrange("p (a t) -> p a t", a=8)
                    wait("pe", t, *bank_free[b])
                    for a in range(2):
                        for i in range(GT):
                            mm = pe.transpose(half[:, a * GT + i, :],
                                              sq[:, i * NH + 4 * hq + 2 * a:i * NH + 4 * hq + 2 * a + 2, :].rearrange("p h s -> p (h s)"),
                                              identb[:])
                    t = done("pe", mm)
                    q_state[("done", g)] = [t]
                    wait("dve", t, *q_state.get(("pv", 4 * g + hq - 2), []))
                    t = done("dve", dve.tensor_copy(fq[:, 0:2, :], psum[:, b, :].bitcast(BF16).rearrange("p (a t) -> p a t", a=2)))
                    bank_free[b] = [t]
                    q_state[("shift", 4 * g + hq)] = t

                items.append(finish)
                return items

            prob_free = [[], [], [], []]
            prob_turn = [0]
            ot = take(96 * K, GW)
            O_BANK = 4
            wait("dve", *bank_free[O_BANK])
            t_o = done("dve", dve.memset(psum[:, O_BANK, :], 0.0))
            bank_free[O_BANK] = [t_o]
            att_tok = {}
            ot_free = [[]]

            def exp_steps(g, hq):
                u = 4 * g + hq
                fq = shift_q[u % 2]
                n_keys = GT * g + GT
                pending = []

                def score(j):
                    off = P * max(0, j - GT * g)
                    got = []
                    for a in range(2):
                        for r in range(2):
                            b = 2 * a + r
                            wait("pe", q_state[("shift", u)], k_tok[j // GT][j % GT], *bank_free[b])
                            rows = slice(SLOT * r, SLOT * r + SLOT)
                            mm = pe.matmul(psum[:, b, off:GW], keys[rows, 2 * hq + a, j * P:(j + 1) * P],
                                           fq[rows, a, off:GW], start=True, stop=(j < GT * g))
                        if j >= GT * g:
                            for r in range(2):
                                mm = pe.matmul(psum[:, 2 * a + r, off:off + P], identb[:], mask_k[:], start=False, stop=True)
                        t = done("pe", mm)
                        pr = prob_turn[0] % 4
                        prob_turn[0] += 1
                        wait("act", t, *prob_free[pr])
                        t = done("act", act.activation(prob[pr][:, :, off:GW], psum[:, 2 * a:2 * a + 2, off:GW], ACT.Exp,
                                                       scale=INV_SQRT_HD))
                        bank_free[2 * a] = [t]
                        bank_free[2 * a + 1] = [t]
                        got.append((pr, t))
                    return off, got

                def values_of(j, off, got):
                    wait("pe", *(t for _, t in got), *v_tok)
                    if j == 0:
                        wait("pe", *bank_free[O_BANK])
                    for a in range(2):
                        for r in range(2):
                            hh = 2 * a + r
                            mm = pe.matmul(psum[32 * hh:32 * hh + 9, O_BANK, off:GW], values[:, j, 4 * hq + hh, :],
                                           prob[got[a][0]][:, r, off:GW], start=(j == 0), stop=(j == n_keys - 1),
                                           skip_group_check=True)
                        t = done("pe", mm)
                        prob_free[got[a][0]] = [t]
                    return t

                def step(j):
                    got = score(j)
                    if pending:
                        values_of(*pending.pop())
                    pending.append((j, *got))

                def finish():
                    t = values_of(*pending.pop())
                    q_state[("pv", u)] = [t]
                    wait("dve", t, *ot_free[0])
                    t = done("dve", dve.tensor_copy(ot, psum[:, O_BANK, :]))
                    bank_free[O_BANK] = [t]
                    b = work_bank()
                    wait("pe", t, *bank_free[b])
                    for i in range(GT):
                        mm = pe.transpose(psum[:, b, i * P:(i + 1) * P], ot[:, i * P:(i + 1) * P], ident[:])
                    t = done("pe", mm)
                    ot_free[0] = [t]
                    back_ = psum[:, b, :].rearrange("p (i h s) -> p i h s", i=GT, h=4)
                    inv_sum = inv_flat.rearrange("p (i h) -> p i h", i=GT)
                    wait("dve", t, *q_state.get("inv", []))
                    t = done("dve", dve.reciprocal(inv_sum, back_[:, :, :, 8]))
                    wait("dve", t)
                    dst = ACC[:, GT * g:GT * g + GT, 4 * hq * HD:(4 * hq + 4) * HD].rearrange("p i (h d) -> p i h d", h=4)
                    t = done("dve", dve.tensor_tensor(dst, back_[:, :, :, 0:HD], bcast(inv_sum, HD), ALU.mult))
                    q_state["inv"] = [t]
                    bank_free[b] = [t]
                    att_tok[g] = t

                return [lambda j=j: step(j) for j in range(n_keys)] + [finish]

            units = [(g, hq) for g in range(NG) for hq in range(4)]
            prepare_q(0)
            for item in max_items(*units[0]):
                item()
            for k, unit in enumerate(units):
                nxt = []
                if k + 1 < len(units):
                    if units[k + 1][1] == 0:
                        prepare_q(units[k + 1][0])
                    nxt = max_items(*units[k + 1])
                steps = exp_steps(*unit)
                given = 0
                for s, step in enumerate(steps):
                    step()
                    upto_item = (s + 1) * len(nxt) // len(steps)
                    for item in nxt[given:upto_item]:
                        item()
                    given = upto_item
            y2 = project_out([att_tok[i // GT] for i in range(NT)], wo1, Y, [att_tok[g] for g in range(NG)])
            if during_moe is not None:
                during_moe()
            t_r = rms_stats(Y, [y2[i // GT] for i in range(NT)])
            wait("dve", t_r)
            h_ready = [done("dve", dve.tensor_scalar(ACC[:, i, :], Y[:, i, :], rstd[:, i:i + 1], None, ALU.mult))
                       for i in range(NT)]
            ht = feature_major(ACC, h_ready, norm_w[:, 1:2])
            acc = moe(NE1, ht, gate1, gateb1, order1, w1_1, b1_1, w2_1, b2_1, const_in, residual=Y)
            tok = add_half(acc)
            barrier()
            return tok

        toep = take(0, D * P).rearrange("p (m x) -> p m x", m=D)
        b_in = take(64 * 256, D * NS).rearrange("p (m n) -> p m n", m=D)
        decay = sb("decay", [P, 64])
        taps = nc.dram_tensor("taps", (D, 2 * P), F32).ap()

        def ssm_far_table():
            core.stage("tab")
            wait("act", const_in)
            wait("dve", const_in)
            wait("pool", const_in)
            back = arena[:, T + P:T + 2 * P + 1]
            wait("sp", *core.last.values())
            t_back = dma("sp", "ld_back", back, ins["back"])
            t1 = done("act", act.activation(logdt_pair[:], logdt_pair[:], ACT.Exp))
            t2 = done("act", act.activation(alog_col[:], alog_col[:], ACT.Exp))
            wait("dve", t1, t2)
            t = done("dve", dve.tensor_scalar(logdt_pair[:], logdt_pair[:], alog_col[:, 0:1], -1.0, ALU.mult, ALU.mult))
            wait("act", t, t_back)
            far = []
            for a in range(64):
                far.append(done("act", act.activation(E_far[:, a, :], back, ACT.Exp, scale=logdt_pair[:, a:a + 1])))
            wait("dve", far[-1])
            t = done("dve", dve.tensor_copy(decay[:], E_far[:, :, 0]))
            wait("dve", t)
            mul = []
            for q in range(4):
                s = slice(16 * q, 16 * q + 16)
                mul.append(done("dve", dve.tensor_tensor(E_far[:, s, :], E_far[:, s, :], bcast(c_pair[:, s], P + 1), ALU.mult)))
            for b in range(4):
                wait("pe", *bank_free[b])
            wait("pe", *mul)
            for a in range(64):
                slot, q = a // 4, a % 4
                mm = pe.matmul(psum[32 * q:32 * q + 32, slot // 4, (slot % 4) * P:(slot % 4 + 1) * P], pairs2[:],
                               E_far[:, a, 1:P + 1], start=True, stop=True)
            t = done("pe", mm)
            k_rev = arena[:, 0:T].rearrange("p (b x) -> p b x", b=4)
            zero = arena[:, T:T + P]
            wait("dve", t)
            tk = done("dve", dve.tensor_copy(k_rev, psum[:, 0:4, :]))
            for b in range(4):
                bank_free[b] = [tk]
            tz = done("dve", dve.memset(zero, 0.0))
            wait("sp", tk, tz)
            for q in range(4):
                dma("sp", "st_taps", bass.AP(tensor=taps.tensor, offset=2 * q * 2 * P, ap=[[2 * P, 2], [8 * 2 * P, 16], [1, P]]),
                    arena[32 * q:32 * q + 2, 0:T].rearrange("p (s x) -> p s x", s=16))
            t_taps = dma("sp", "st_taps", taps[:, P:2 * P], zero)
            for e in ("sp", "pe", "dve", "act", "pool"):
                wait(e, t_taps)
            barrier()

        def ssm_near_tables():
            core.stage("near")
            wait("sp", *core.last.values())
            step = D // 8
            for m in range(0, D, step):
                t_toep[0] = dma("sp" if (m // step) % 2 else "act", "ld_toep", toep[:, m:m + step, :],
                                bass.AP(tensor=taps.tensor, offset=m * 2 * P, ap=[[1, P], [2 * P, step], [1, P]]))
            t_l = dma("sp", "ld_dt", logdt_all, on_all(ins["L1_attn_log_dt"], 0, D))
            t_l = dma("sp", "ld_dt", alog_all, on_all(ins["L1_attn_A_log"], 0, NS))
            wait("act", t_l)
            t1 = done("act", act.activation(logdt_all, logdt_all, ACT.Exp))
            t2 = done("act", act.activation(alog_all, alog_all, ACT.Exp))
            wait("pool", t1, t2)
            t = done("pool", pool.tensor_tensor(b_in, bcast(logdt_all, NS), alog_all.unsqueeze(1).broadcast_to([P, D, NS]), ALU.mult))
            tn = done("dve", dve.tensor_scalar(neg_back[:], back_col[:], -1.0, None, ALU.mult))
            wait("act", t, tn)
            t_bin[0] = done("act", act.activation(b_in, b_in, ACT.Exp, scale=neg_back[:, 0:1]))

        neg_back = sb("neg_back", [P, 1])
        t_toep, t_bin = [None], [None]

        def ssm(name, x_ready):
            core.stage(name)
            C17 = NT + 1
            state_in = take(96 * 256, 64 * C17)
            states = take(101 * 256, 64 * C17)
            mult = take(106 * 256, 64 * C17)
            v3 = lambda t: t.rearrange("p (a c) -> p a c", a=64)
            y_ready = layer_norm(x_ready)
            tz = done("pool", pool.memset(v3(state_in)[:, :, 0:1], 0.0))
            done("pool", pool.memset(v3(mult)[:, :, 0:1], 0.0))
            t_mult = done("pool", pool.tensor_copy(v3(mult)[:, :, 1:C17], bcast(decay[:], NT)))
            for n in range(NT):
                wait("pool", y_ready[n])
            t = done("pool", pool.tensor_tensor(ACC[:, :, :], Y[:, :, :], skip_d[:].unsqueeze(1).broadcast_to([P, NT, D]), ALU.mult))
            wait("pool", t)
            t_skip = done("pool", pool.tensor_tensor(X[:, :, :], X[:, :, :], ACC[:, :, :], ALU.add))
            wait("pe", t_bin[0], *y_ready, *bank_free[0], *bank_free[1])
            for a in range(64):
                for r in range(2):
                    mm = pe.matmul(psum[64 * r:64 * r + 64, a // 32, (a % 32) * NT:(a % 32 + 1) * NT],
                                   b_in[:, 2 * a + r, :], Y[:, :, 2 * a + r], start=True, stop=True)
            t = done("pe", mm)
            wait("dve", t, tz)
            t = done("dve", dve.tensor_copy(v3(state_in)[:, :, 1:C17], psum[:, 0:2, :].rearrange("p b (a c) -> p (b a) c", c=NT)))
            bank_free[0] = bank_free[1] = [t]
            wait("dve", t, t_mult)
            t_st = done("dve", dve.tensor_tensor_scan(states, mult, state_in, 0.0, ALU.mult, ALU.add))
            st3 = v3(states)
            rows_free, tok = [], None
            banks = (0, 1, 2, 3)
            for b in banks:
                wait("dve", *bank_free[b])
                t = done("dve", dve.memset(psum[:, b, :], 0.0))
                bank_free[b] = [t]
            ysb = [ACC[:, 4 * i:4 * i + 4, :] for i in range(4)]
            wait("act", t_skip)
            wait("pe", t_toep[0])
            ysb_free = [[], [], [], []]
            for grp in range(8):
                b = grp % 4
                wait("pe", *bank_free[b])
                for qd in range(4):
                    for q in range(4):
                        m = 16 * grp + 4 * qd + q
                        o = psum[32 * q:32 * q + NT, b, qd * P:(qd + 1) * P]
                        pe.matmul(o, Y[:, :, m], toep[:, m, :], start=True, stop=False, skip_group_check=True)
                    if qd == 0 and grp == 0:
                        wait("pe", t_st)
                    for q in range(4):
                        m = 16 * grp + 4 * qd + q
                        r = 64 * (m % 2)
                        o = psum[32 * q:32 * q + NT, b, qd * P:(qd + 1) * P]
                        mm = pe.matmul(o, st3[r:r + 64, m // 2, 0:NT], E_far[r:r + 64, m // 2, 0:P], start=False,
                                       stop=True, skip_group_check=True)
                t = done("pe", mm)
                ys = ysb[grp % 4]
                wait("act", t, *ysb_free[grp % 4])
                t = done("act", act.activation(ys, psum[:, b, :].rearrange("p (k x) -> p k x", k=4)[:, :, ::-1], ACT.Copy))
                bank_free[b] = [t]
                tb = 4 + grp % 2
                wait("pe", t, *bank_free[tb])
                for qd in range(4):
                    mm = pe.transpose(psum[:, tb, qd * P:(qd + 1) * P], ys[:, qd, :], ident[:])
                t = done("pe", mm)
                ysb_free[grp % 4] = [t]
                wait("dve", t, t_skip)
                add = psum[:, tb, :].rearrange("p (m c) -> p c m", c=32)[:, 0:NT, :]
                dst = X[:, :, 16 * grp:16 * grp + 16]
                tok = done("dve", dve.tensor_tensor(dst, add, dst, ALU.add))
                bank_free[tb] = [tok]
            barrier()
            return [tok] * NG

        ready = macaron_ffn("ffa", x_in)
        if upto >= 2:
            ready = windowed_attention("win", ready)
        if upto >= 3:
            ready = macaron_ffn("ffb", ready)
        if upto >= 4:
            ssm_far_table()
            ready = latent_block("la", ready, during_moe=ssm_near_tables)
            wait("sp", t_toep[0])
        if upto >= 5:
            ready = ssm("ssm", ready)
        if upto >= 6:
            ready = latent_block("lb", ready)
        core.stage("end")
        out_view = out[0].rearrange("(i p) f -> p i f", p=P)
        for g in range(NG):
            wait("sp", ready[g])
            t = dma("sp", "st_out", out_view[:, GT * g:GT * g + GT, :], X[:, GT * g:GT * g + GT, :])
        wait("sp", t, const_in)


_RAW = ["L0_attn_x", "L0_attn_bq", "L0_attn_bk", "L0_attn_bv", "L0_attn_wo", "L0_attn_bo", "L0_attn_qn_w",
        "L0_attn_kn_w", "L0_ffn_gate_b", "L0_ffn_b2", "L1_attn_A_log", "L1_attn_D", "L1_attn_log_dt",
        "L1_ffn_gate_b", "L1_ffn_b2"]


def kernel(**inputs):
    import numpy as np
    import concourse.bacc as _bacc
    from concourse.bass_utils import run_bass_kernel_spmd as _run

    a = {n: np.ascontiguousarray(inputs[n]) for n in _RAW}
    g = {n: np.asarray(v) for n, v in inputs.items()}

    def lay(name, value):
        a[name] = np.ascontiguousarray(value)

    lay("gate0", g["L0_ffn_gate_w"].T)
    lay("gate1", g["L1_ffn_gate_w"].T)
    for k, (w1, b1, w2, ne) in enumerate((("L0_ffn_w1", "L0_ffn_b1", "L0_ffn_w2", NE0), ("L1_ffn_W1", "L1_ffn_b1", "L1_ffn_W2", NE1))):
        lay(f"w1_{k}", g[w1].transpose(2, 0, 1))
        lay(f"b1_{k}", g[b1].reshape(ne * HC, P).T)
        lay(f"w2_{k}", g[w2].reshape(ne, D, HC, P).transpose(3, 0, 2, 1))
    lay("wqkv", np.concatenate([g["L0_attn_wq"], g["L0_attn_wk"], g["L0_attn_wv"]], axis=1))
    lay("wqd", np.concatenate([g["L1_ffn_Wq"].T, g["L1_ffn_Wdkv"].T], axis=1))
    lay("wukv", np.concatenate([g["L1_ffn_Wuk"].T, g["L1_ffn_Wuv"].T], axis=1))
    lay("wo1", g["L1_ffn_Wo"].T)
    lay("norm_w", np.stack([g["L1_ffn_norm1_w"], g["L1_ffn_norm2_w"]], axis=1))
    lay("ln_gb", np.stack([g["L1_ffn_ln_g"], g["L1_ffn_ln_b"]], axis=1))
    lay("c_pair", g["L1_attn_C_re"].reshape(64, 2 * NS).T)

    lay("logdt_pair", g["L1_attn_log_dt"].reshape(64, 2).T)
    lay("alog_col", g["L1_attn_A_log"][:, None])

    f = np.float32
    lay("order0", np.tile(np.arange(NE0, 0, -1, dtype=f), (P, 1)))
    lay("order1", np.tile(np.arange(NE1, 0, -1, dtype=f), (P, 1)))
    row, col = np.arange(P)[:, None] % W, np.arange(2 * W)[None, :]
    ok = (col <= row + W) & (col > row)
    first = ok & ((np.arange(P)[:, None] >= W) | (col >= W))
    lay("window_mask", np.stack([np.where(first, 0, MASKED), np.where(ok, 0, MASKED)], axis=1).astype(f))
    half = HD // 2
    inv_freq = (f(1.0) / f(10000.0) ** (np.arange(half, dtype=f) / f(half))).astype(f)
    ang = np.arange(T, dtype=f)[:, None] * inv_freq[None, :]
    sin, cos = np.sin(ang).astype(f), np.cos(ang).astype(f)
    table = np.stack([np.concatenate([cos, cos], 1), np.concatenate([-sin, sin], 1)])
    lay("rope", table.reshape(2, NT, P, HD).transpose(2, 0, 1, 3))
    lay("back", np.tile(np.arange(P, -1, -1, dtype=f), (P, 1)))
    lay("back_col", np.arange(P - 1, -1, -1, dtype=f)[:, None])

    nc = _bacc.Bacc("TRN2", target_bir_lowering=False, num_devices=1)
    arrays = {f"in_{n}": v for n, v in a.items()}
    ins = {n: nc.dram_tensor(f"in_{n}", v.shape, mybir.dt.from_np(v.dtype), kind="ExternalInput").ap() for n, v in a.items()}
    out = nc.dram_tensor("out_0", (1, T, D), F32, kind="ExternalOutput").ap()
    build(nc, ins, out, UPTO)
    r = _run(nc, [arrays], core_ids=[0])
    return r.results[0]["out_0"]


UPTO = 6
```

```python
from contextlib import ExitStack

import concourse.bass as bass
from concourse import mybir

F32 = mybir.dt.float32
BF16 = mybir.dt.bfloat16
ALU = mybir.AluOpType
ACT = mybir.ActivationFunctionType
AX = mybir.AxisListType

P = 128
T = 2048
NT = T // P
D = 128
NH = 16
HD = D // NH
W = 32
HID = 512
HC = HID // P
NE0, NE1 = 8, 4
KV = 64
NS = 64
GT = 4
NG = NT // GT
GW = GT * P
SLOT = 64
MASKED = -1e30
EPS_LN, EPS_RMS = 1e-5, 1e-6
EPS_F32 = 1.1920928955078125e-07
INV_SQRT_HD = 1.0 / HD ** 0.5


class Core:

    def __init__(self, nc, ctx):
        self.nc, self.ctx = nc, ctx
        self.eng = {"pe": nc.tensor, "dve": nc.vector, "act": nc.scalar, "pool": nc.gpsimd, "sp": nc.sync}
        self.seen = {e: {} for e in self.eng}
        self.last = {}
        self.count = {}
        self.sems = {}
        self.stage_name = ""

    def stage(self, name):
        self.stage_name = name

    def sem(self, name):
        if name not in self.sems:
            self.sems[name] = self.ctx.enter_context(self.nc.semaphore(name))
            self.count[name] = 0
        return self.sems[name]

    def wait(self, engine, *tokens):
        for token in tokens:
            if token is None:
                continue
            name, value = token
            if self.seen[engine].get(name, 0) < value:
                self.seen[engine][name] = value
                self.eng[engine].wait_ge(self.sems[name], value)

    def done(self, engine, instruction):
        name = f"{self.stage_name}_{engine}"
        instruction.then_inc(self.sem(name), 1)
        self.count[name] += 1
        self.last[engine] = (name, self.count[name])
        return self.last[engine]

    def dma(self, engine, name, out, in_):
        sem = self.sem(name)
        self.eng[engine].dma_start(out, in_).then_inc(sem, 16)
        self.count[name] += 16
        return name, self.count[name]

    def barrier(self):
        for engine in ("pe", "dve", "act", "pool"):
            self.wait(engine, *self.last.values())


def bcast(ap, n):
    return ap.unsqueeze(len(ap.shape)).broadcast_to(list(ap.shape) + [n])


def on_all(ap, offset, n):
    return bass.AP(tensor=ap.tensor, offset=offset, ap=[[0, P], [1, n]])


def build(nc, ins, out, upto=6):
    with ExitStack() as ctx:
        core = Core(nc, ctx)
        wait, done, dma, barrier = core.wait, core.done, core.dma, core.barrier
        pe, dve, act, pool = nc.tensor, nc.vector, nc.scalar, nc.gpsimd

        def sb(name, shape, dt=F32):
            return ctx.enter_context(nc.sbuf_tensor(name, shape, dt))

        psum = ctx.enter_context(nc.psum_tensor("psum", [P, 8, GW], F32))
        bank_free = [[] for _ in range(8)]

        X = sb("X", [P, NT, D])
        Y = sb("Y", [P, NT, D])
        YT = sb("YT", [P, T])
        ACC = sb("ACC", [P, NT, D])
        ident = sb("ident", [P, P])
        identb = sb("identb", [P, P], BF16)
        stats = sb("stats", [P, NT, 6])
        meanvar = sb("meanvar", [P, NT, 2])
        rstd = sb("rstd", [P, NT])
        small = sb("small", [P, 8, P])

        big_w = sb("big_w", [P, 64 * 129])
        w1_0 = big_w[:, 0:NE0 * HID].rearrange("p (e h) -> p e h", e=NE0)
        w2_0 = big_w[:, NE0 * HID:2 * NE0 * HID].rearrange("p (e c d) -> p e c d", e=NE0, c=HC)
        E_far = big_w[:, :].rearrange("p (a x) -> p a x", a=64)
        w4 = sb("w4", [P, 2 * NE1 * HID])
        w1_1 = w4[:, 0:NE1 * HID].rearrange("p (e h) -> p e h", e=NE1)
        w2_1 = w4[:, NE1 * HID:2 * NE1 * HID].rearrange("p (e c d) -> p e c d", e=NE1, c=HC)

        ARENA = 112 * 256
        arena = sb("arena", [P, ARENA])

        def take(start, n, dt=F32):
            part = arena[:, start:start + n]
            return part if dt is F32 else part.bitcast(dt)

        hidden = [take(96 * 256 + i * 8 * 256, HC * GW).rearrange("p (c t) -> p c t", c=HC) for i in range(2)]

        def load(name, shape, src, dt=F32, engine="sp", group="ld_const"):
            t = sb(name, shape, dt)
            return t, dma(engine, group, t[:], src)

        x_view = ins["L0_attn_x"][0].rearrange("(i p) f -> p i f", p=P)
        x_in = [dma("sp", f"ld_x{g}", X[:, GT * g:GT * g + GT, :], x_view[:, GT * g:GT * g + GT, :]) for g in range(NG)]
        small_group = "ld_moe0"
        gate0, _ = load("gate0", [P, NE0], ins["gate0"], group=small_group, engine="act")
        gateb0, _ = load("gateb0", [P, NE0], on_all(ins["L0_ffn_gate_b"], 0, NE0), group=small_group, engine="act")
        b1_0, _ = load("b1_0", [P, NE0 * HC], ins["b1_0"], group=small_group, engine="act")
        b2_0, _ = load("b2_0", [NE0, D], ins["L0_ffn_b2"], group=small_group, engine="act")
        order0, _ = load("order0", [P, NE0], ins["order0"], group=small_group, engine="act")
        dma("act", small_group, w1_0, ins["w1_0"])
        moe0_in = dma("act", small_group, w2_0, ins["w2_0"])

        wqkv, _ = load("wqkv", [P, 3 * D], ins["wqkv"])
        qk_w = sb("qk_w", [P, 2, HD])
        dma("sp", "ld_const", qk_w[:, 0, :], on_all(ins["L0_attn_qn_w"], 0, HD))
        dma("sp", "ld_const", qk_w[:, 1, :], on_all(ins["L0_attn_kn_w"], 0, HD))
        wo0, _ = load("wo0", [P, D], ins["L0_attn_wo"])
        bo, _ = load("bo", [P, D], on_all(ins["L0_attn_bo"], 0, D))
        window_mask, _ = load("window_mask", [P, 2, 2 * W], ins["window_mask"])
        gate1, _ = load("gate1", [P, NE1], ins["gate1"])
        gateb1, _ = load("gateb1", [P, NE1], on_all(ins["L1_ffn_gate_b"], 0, NE1))
        b1_1, _ = load("b1_1", [P, NE1 * HC], ins["b1_1"])
        b2_1, _ = load("b2_1", [NE1, D], ins["L1_ffn_b2"])
        order1, _ = load("order1", [P, NE1], ins["order1"])
        norm_w, _ = load("norm_w", [P, 2], ins["norm_w"])
        ln_gb, _ = load("ln_gb", [KV, 2], ins["ln_gb"])
        wqd, _ = load("wqd", [P, D + KV], ins["wqd"])
        wukv, _ = load("wukv", [KV, 2 * D], ins["wukv"])
        wo1, _ = load("wo1", [P, D], ins["wo1"])
        rope, _ = load("rope", [P, 2, NT, HD], ins["rope"])
        skip_d, _ = load("skip_d", [P, D], on_all(ins["L1_attn_D"], 0, D))
        c_pair, _ = load("c_pair", [P, 64], ins["c_pair"])
        logdt_pair = sb("logdt_pair", [P, 64])
        for r in range(2):
            dma("sp", "ld_const", logdt_pair[64 * r:64 * r + 64, :],
                bass.AP(tensor=ins["logdt_pair"].tensor, offset=64 * r, ap=[[0, 64], [1, 64]]))
        alog_col = sb("alog_col", [P, 1])
        for r in range(2):
            dma("sp", "ld_const", alog_col[64 * r:64 * r + 64, :], ins["alog_col"])
        logdt_all, alog_all = small[:, 5, :], small[:, 6, 0:NS]
        back_col, _ = load("back_col", [P, 1], ins["back_col"])
        dma("sp", "ld_const", w1_1, ins["w1_1"])
        const_in = dma("sp", "ld_const", w2_1, ins["w2_1"])

        core.stage("setup")
        ones = sb("ones", [P, P])
        mask_q = sb("mask_q", [P, P], BF16)
        mask_k = sb("mask_k", [P, P], BF16)
        pairs2 = sb("pairs2", [P, 32])
        t_z = done("pool", pool.memset(ident[:], 0.0))
        wait("pool", t_z)
        t_id = done("pool", pool.affine_select(out=ident[:], in_=ident[:], compare_op=ALU.not_equal, fill=1.0,
                                               base=0, pattern=[[-1, P]], channel_multiplier=1))
        wait("pool", t_id)
        t_idb = done("pool", pool.tensor_copy(identb[:], ident[:]))
        t_m = done("pool", pool.memset(mask_q[:], 0.0))
        t_m2 = done("pool", pool.memset(mask_k[:], 0.0))
        t_ones = done("pool", pool.memset(ones[:], 1.0))
        t_p = done("pool", pool.memset(pairs2[:], 0.0))
        wait("pool", t_p)
        done("pool", pool.affine_select(out=mask_q[:], in_=mask_q[:], compare_op=ALU.is_ge, fill=MASKED,
                                        base=0, pattern=[[-1, P]], channel_multiplier=1))
        done("pool", pool.affine_select(out=mask_k[:], in_=mask_k[:], compare_op=ALU.is_ge, fill=MASKED,
                                        base=0, pattern=[[1, P]], channel_multiplier=-1))
        for r in range(2):
            wait("pool", core.last["pool"])
            t_setup = done("pool", pool.memset(pairs2[64 * r:64 * r + 64, r:r + 1], 1.0))
        wait("pe", t_setup)

        def layer_norm(ready):
            tok = []
            for i in range(NT):
                wait("dve", ready[i // GT])
                tok.append(done("dve", dve.bn_stats(stats[:, i, :], X[:, i, :])))
            for i in range(NT):
                wait("dve", tok[i])
                t = done("dve", dve.bn_aggr(meanvar[:, i, :], stats[:, i, :]))
            t = rsqrt(meanvar[:, :, 1], rstd[:, :], 1.0, EPS_LN, t)
            wait("dve", t)
            return [done("dve", dve.tensor_scalar(Y[:, i, :], X[:, i, :], meanvar[:, i, 0:1], rstd[:, i:i + 1],
                                                  ALU.subtract, ALU.mult)) for i in range(NT)]

        def rsqrt(src, dst, scale, eps, ready):
            wait("dve", ready)
            t = done("dve", dve.tensor_scalar(dst, src, scale, eps, ALU.mult, ALU.add))
            wait("act", t)
            t = done("act", act.activation(dst, dst, ACT.Sqrt))
            wait("dve", t)
            return done("dve", dve.reciprocal(dst, dst))

        def rms_stats(src, ready):
            for i in range(NT):
                wait("act", ready[i])
                t = done("act", act.activation(ACC[:, i, :], src[:, i, :], ACT.Square,
                                               accum_out=rstd[:, i:i + 1]))
            return rsqrt(rstd[:, :], rstd[:, :], 1.0 / D, EPS_RMS, t)

        def feature_major(src, ready, scale_col=None, banks=(6, 7)):
            tok = []
            for g in range(NG):
                b = banks[g % 2]
                wait("pe", *bank_free[b])
                for i in range(GT):
                    wait("pe", ready[GT * g + i])
                    mm = pe.transpose(psum[:, b, i * P:(i + 1) * P], src[:, GT * g + i, :], ident[:])
                t = done("pe", mm)
                dst = YT[:, g * GW:(g + 1) * GW]
                if g % 2:
                    wait("act", t)
                    t = done("act", act.activation(dst, psum[:, b, :], ACT.Copy) if scale_col is None
                             else act.activation(dst, psum[:, b, :], ACT.Identity, scale=scale_col))
                else:
                    wait("dve", t)
                    t = done("dve", dve.tensor_copy(dst, psum[:, b, :]) if scale_col is None
                             else dve.tensor_scalar(dst, psum[:, b, :], scale_col, None, ALU.mult))
                bank_free[b] = [t]
                tok.append(t)
            return tok

        def moe(n_exp, yt_ready, gate, gate_b, order, w1, b1, w2, b2, weights_in, residual=None, beside=()):
            beside = list(beside)
            log = small[:, 0, 0:NT * n_exp].rearrange("p (i e) -> p i e", e=n_exp)
            eq = small[:, 1, 0:NT * n_exp].rearrange("p (i e) -> p i e", e=n_exp)
            hot = small[:, 2, 0:NT * n_exp].rearrange("p (i e) -> p i e", e=n_exp)
            best = small[:, 3, 0:NT]
            best2 = small[:, 4, 0:NT]
            hot_t = hidden[1][0:n_exp, 0, :]
            wait("pe", weights_in, *bank_free[7])
            for i in range(NT):
                wait("pe", yt_ready[i // GT])
                mm = pe.matmul(psum[:, 7, i * n_exp:(i + 1) * n_exp], YT[:, i * P:(i + 1) * P], gate[:],
                               start=True, stop=True)
            t = done("pe", mm)
            wait("dve", t, weights_in)
            t = done("dve", dve.tensor_tensor(log, psum[:, 7, 0:NT * n_exp].rearrange("p (i e) -> p i e", e=n_exp),
                                              gate_b[:].unsqueeze(1).broadcast_to([P, NT, n_exp]), ALU.add))
            bank_free[7] = [t]
            wait("dve", t)
            t = done("dve", dve.tensor_reduce(best, log, AX.X, ALU.max))
            wait("dve", t)
            t = done("dve", dve.tensor_tensor(eq, log, bcast(best, n_exp), ALU.is_ge))
            wait("dve", t)
            t = done("dve", dve.tensor_tensor(eq, eq, order[:].unsqueeze(1).broadcast_to([P, NT, n_exp]), ALU.mult))
            wait("dve", t)
            t = done("dve", dve.tensor_reduce(best2, eq, AX.X, ALU.max))
            wait("dve", t)
            t_hot = done("dve", dve.tensor_tensor(hot, eq, bcast(best2, n_exp), ALU.is_equal))

            def output_bias():
                wait("pe", t_hot)
                acc_tok = []
                for g in range(NG):
                    wait("pe", *bank_free[7])
                    for i in range(GT):
                        mm = pe.transpose(psum[0:n_exp, 7, i * P:(i + 1) * P], hot[:, GT * g + i, :], ident[:])
                    t = done("pe", mm)
                    wait("dve", t)
                    t = done("dve", dve.tensor_copy(hot_t, psum[0:n_exp, 7, :]))
                    wait("pe", t)
                    for i in range(GT):
                        mm = pe.matmul(psum[:, 7, i * P:(i + 1) * P],
                                       hot_t[:, i * P:(i + 1) * P], b2[:], start=True, stop=True)
                    t = done("pe", mm)
                    hid_free[1] = t
                    wait("dve", t)
                    dst = ACC[:, GT * g:GT * g + GT, :]
                    bias = psum[:, 7, :].rearrange("p (i d) -> p i d", i=GT)
                    t = done("dve", dve.tensor_copy(dst, bias) if residual is None else
                             dve.tensor_tensor(dst, bias, residual[:, GT * g:GT * g + GT, :], ALU.add))
                    bank_free[7] = [t]
                    acc_tok.append(t)
                return acc_tok

            units = [(e, g) for e in range(n_exp) for g in range(NG)]
            hid_ready, hid_free, acc_tok = {}, [None, None], None

            def layer1(u):
                e, g = units[u]
                hid = hidden[u % 2]
                toks = []
                for c in range(HC):
                    wait("pe", yt_ready[g], *bank_free[c])
                    t = done("pe", pe.matmul(psum[:, c, :], w1[:, e, c * P:(c + 1) * P], YT[:, g * GW:(g + 1) * GW],
                                             start=True, stop=True))
                    col = b1[:, e * HC + c:e * HC + c + 1]
                    if c % 2 == 0:
                        wait("act", t, hid_free[u % 2])
                        t = done("act", act.activation(hid[:, c, :], psum[:, c, :], ACT.Relu, bias=col))
                    else:
                        wait("dve", t, hid_free[u % 2])
                        t = done("dve", dve.tensor_scalar(hid[:, c, :], psum[:, c, :], col, 0.0, ALU.add, ALU.max))
                    bank_free[c] = [t]
                    toks.append(t)
                hid_ready[u] = toks

            def layer2(u):
                e, g = units[u]
                hid, b = hidden[u % 2], 4 + u % 2
                wait("pe", *hid_ready[u], *bank_free[b])
                for i in range(GT):
                    for c in range(HC):
                        mm = pe.matmul(psum[:, b, i * P:(i + 1) * P], hid[:, c, i * P:(i + 1) * P], w2[:, e, c, :],
                                       start=(c == 0), stop=(c == HC - 1))
                t = done("pe", mm)
                hid_free[u % 2] = t
                wait("dve", t)
                for i in range(GT):
                    n = GT * g + i
                    wait("dve", acc_tok[n])
                    acc_tok[n] = done("dve", dve.scalar_tensor_tensor(
                        out=ACC[:, n, :], in0=psum[:, b, i * P:(i + 1) * P], scalar=hot[:, n, e:e + 1],
                        in1=ACC[:, n, :], op0=ALU.mult, op1=ALU.add))
                bank_free[b] = [acc_tok[GT * g + GT - 1]]

            layer1(0)
            acc_tok = [t for t in output_bias() for _ in range(GT)]
            for u in range(len(units)):
                if u + 1 < len(units):
                    layer1(u + 1)
                layer2(u)
                if beside:
                    beside.pop(0)()
            return acc_tok

        def add_half(ready):
            tok = []
            for g in range(NG):
                wait("dve", *ready[GT * g:GT * g + GT])
                s = slice(GT * g, GT * g + GT)
                tok.append(done("dve", dve.scalar_tensor_tensor(out=X[:, s, :], in0=ACC[:, s, :], scalar=0.5,
                                                                in1=X[:, s, :], op0=ALU.mult, op1=ALU.add)))
            return tok

        def macaron_ffn(name, x_ready):
            core.stage(name)
            y = layer_norm(x_ready)
            yt = feature_major(Y, y)
            acc = moe(NE0, yt, gate0, gateb0, order0, w1_0, b1_0, w2_0, b2_0, moe0_in)
            tok = add_half(acc)
            barrier()
            return tok

        def split3(src, dst, rest, is_query, ready, free):
            def slot(k):
                return dst[:, :, k * HD:(k + 1) * HD]

            where = ((0, 1, 2), (3, 4), (5,)) if is_query else ((0, 3, 5), (1, 4), (2,))
            wait("dve", ready, *free)
            wait("act", *free)
            part = src
            toks = []
            for k in range(3):
                t = done("dve", dve.tensor_copy(slot(where[k][0]), part))
                for other in where[k][1:]:
                    wait("act", t)
                    toks.append(done("act", act.activation(slot(other), slot(where[k][0]), ACT.Copy)))
                if k < 2:
                    wait("dve", t)
                    t = done("dve", dve.tensor_tensor(rest, part, slot(where[k][0]), ALU.subtract))
                    wait("dve", t)
                    part = rest
            return [t, toks[-1]]

        def to_rows(src, n_tiles, dst_of, ready, banks, engine_of):
            toks = []
            for i in range(n_tiles):
                b = banks[i % len(banks)]
                half = psum[:, b, :].bitcast(BF16).rearrange("p (a t) -> p a t", a=8)
                wait("pe", *ready, *bank_free[b])
                for a in range(8):
                    mm = pe.transpose(half[:, a, :], src[:, i, a * P:(a + 1) * P], identb[:])
                t = done("pe", mm)
                e = engine_of(i)
                wait(e, t)
                t = done(e, act.activation(dst_of(i), half, ACT.Copy) if e == "act" else dve.tensor_copy(dst_of(i), half))
                bank_free[b] = [t]
                toks.append(t)
            return toks

        def windowed_attention(name, x_ready):
            core.stage(name)
            y_ready = layer_norm(x_ready)
            yt_ready = feature_major(Y, y_ready)
            SC = INV_SQRT_HD
            K = 256
            keys = take(0, 8 * (T + W) // 2, BF16).rearrange("p (a t) -> p a t", a=8)
            queries = take(33 * K, 8 * T // 2, BF16).rearrange("p (a t) -> p a t", a=8)
            split_q = take(65 * K, GT * NH * SLOT // 2, BF16).rearrange("p (n s) -> p n s", s=SLOT)
            split_k = take(73 * K, GT * NH * SLOT // 2, BF16).rearrange("p (n s) -> p n s", s=SLOT)
            v_own = take(81 * K, NT * D).rearrange("p (i d) -> p i d", i=NT)
            v_prev = take(89 * K, NT * D).rearrange("p (i d) -> p i d", i=NT)
            raw = take(97 * K, 2 * GT * D).rearrange("p (k i d) -> p k i d", k=2, i=GT)
            sq = take(101 * K, 2 * GT * D).rearrange("p (k i d) -> p k i d", k=2, i=GT)
            rest = take(105 * K, GT * D).rearrange("p (n d) -> p n d", d=HD)
            bqkv = take(107 * K, 3 * D)
            wait("sp", *core.last.values())
            for n, b in enumerate(("L0_attn_bq", "L0_attn_bk", "L0_attn_bv")):
                t_b = dma("sp", name + "_bias", bqkv[:, n * D:(n + 1) * D], on_all(ins[b], 0, D))
            wait("pool", *x_ready)
            wait("dve", t_b)
            wait("dve", const_in)
            wait("pe", const_in)
            t_pad = done("pool", pool.memset(keys[:, :, 0:W], 0.0))
            done("pool", pool.memset(split_q[:, :, 48:64], 0.0))
            t_pad = done("pool", pool.memset(split_k[:, :, 48:64], 0.0))
            r_norm = small[:, 0, 0:2 * GT * NH]
            q_tok, k_tok, v_tok = [], [], []
            free_raw, free_q, free_k = [], [], []
            for g in range(NG):
                for i in range(GT):
                    n, b = GT * g + i, i % 4
                    wait("pe", yt_ready[g], *bank_free[b])
                    t = done("pe", pe.matmul(psum[:, b, 0:3 * D], YT[:, n * P:(n + 1) * P], wqkv[:], start=True, stop=True))
                    wait("dve", t, *free_raw)
                    t_raw = done("dve", dve.tensor_tensor(raw[:, :, i, :], psum[:, b, 0:2 * D].rearrange("p (k d) -> p k d", k=2),
                                                          bqkv[:, 0:2 * D].rearrange("p (k d) -> p k d", k=2), ALU.add))
                    t_v = done("dve", dve.tensor_tensor(v_own[:, n, :], psum[:, b, 2 * D:3 * D], bqkv[:, 2 * D:3 * D], ALU.add))
                    bank_free[b] = [t_v]
                v_tok.append(t_v)
                flat = raw.rearrange("p k i (h e) -> p (k i h) e", e=HD)
                flat_sq = sq.rearrange("p k i (h e) -> p (k i h) e", e=HD)
                wait("act", t_raw)
                t = done("act", act.activation(flat_sq, flat, ACT.Square))
                wait("dve", t)
                t = done("dve", dve.tensor_reduce(r_norm, flat_sq, AX.X, ALU.add))
                t = rsqrt(r_norm, r_norm, 1.0 / HD, EPS_F32, t)
                wait("dve", t)
                t = done("dve", dve.tensor_tensor(flat, flat, bcast(r_norm, HD), ALU.mult))
                wait("dve", t)
                for k in range(2):
                    rows = raw[:, k, :, :].rearrange("p i (h e) -> p (i h) e", e=HD)
                    t = done("dve", dve.tensor_tensor(rows, rows, qk_w[:, k, :].unsqueeze(1).broadcast_to([P, GT * NH, HD]), ALU.mult))
                t_q = split3(raw[:, 0].rearrange("p i (h e) -> p (i h) e", e=HD), split_q, rest, True, t, free_q + [t_pad])
                t_k = split3(raw[:, 1].rearrange("p i (h e) -> p (i h) e", e=HD), split_k, rest, False, t_q[0], free_k)
                free_raw = [t_k[0]]
                base = g * GW
                eng = lambda i: "act" if i % 2 else "dve"
                tq = to_rows(split_q.rearrange("p (i h) s -> p i (h s)", i=GT), GT,
                             lambda i: queries[:, :, base + i * P:base + (i + 1) * P], t_q, (4, 5), eng)
                tk = to_rows(split_k.rearrange("p (i h) s -> p i (h s)", i=GT), GT,
                             lambda i: keys[:, :, W + base + i * P:W + base + (i + 1) * P], t_k, (6, 7), eng)
                free_q, free_k = tq, tk
                q_tok.append(tq)
                k_tok.append(tk)
            wait("sp", *v_tok)
            wait("pool", core.last["pool"])
            t_pad = done("pool", pool.memset(v_prev[0:W, 0:1, :], 0.0))
            wait("pool", t_pad)
            dma("sp", name + "_shift", v_prev[W:P, :, :], v_own[0:P - W, :, :])
            t_vp = dma("sp", name + "_shift", v_prev[0:W, 1:NT, :], v_own[P - W:P, 0:NT - 1, :])
            barrier()

            score = [take((65 + 4 * i) * K, NH * 2 * W).rearrange("p (h w) -> p h w", h=NH) for i in range(3)]
            prob = [YT[:, i * NH * 2 * W:(i + 1) * NH * 2 * W].rearrange("p (h w) -> p h w", h=NH) for i in range(2)]
            prob_t = [take((97 + 4 * i) * K, NH * 2 * W).rearrange("p (h w) -> p h w", h=NH) for i in range(2)]
            per_row = lambda k: take((104 + k) * K, NT * NH).rearrange("p (i h) -> p i h", i=NT)
            mx, ln_, rl, th = per_row(1), per_row(2), per_row(3), per_row(4)
            exp_tok, pt_tok, tanh_tok = {}, {}, {}
            score_free, prob_free, pt_free = {}, {}, {}
            u_tok, th_tok = [], []

            def scores(n):
                sc, b = score[n % 3], 2 * (n % 2)
                wait("pe", *bank_free[b])
                for h in range(NH):
                    r = SLOT * (h % 2)
                    for j in range(4):
                        t0 = n * P + j * W
                        mm = pe.matmul(psum[W * j:W * j + W, b + h % 2, (h // 2) * 2 * W:(h // 2 + 1) * 2 * W],
                                       queries[r:r + SLOT, h // 2, t0:t0 + W], keys[r:r + SLOT, h // 2, t0:t0 + 2 * W],
                                       start=True, stop=True)
                t = done("pe", mm)
                wait("dve", t, *score_free.get(n - 3, []))
                both = psum[:, b:b + 2, :].rearrange("p k (h w) -> p (k h) w", w=2 * W)
                t = done("dve", dve.tensor_tensor(sc, both, window_mask[:, min(n, 1), :].unsqueeze(1).broadcast_to([P, NH, 2 * W]), ALU.add))
                bank_free[b] = [t]
                wait("dve", t)
                t = done("dve", dve.tensor_reduce(mx[:, n, :], sc, AX.X, ALU.max))
                wait("dve", t)
                t = done("dve", dve.tensor_tensor(sc, sc, bcast(mx[:, n, :], 2 * W), ALU.subtract))
                wait("act", t)
                exp_tok[n] = done("act", act.activation(sc, sc, ACT.Exp, scale=SC))

            def normalised(n):
                sc, pt, pr = score[n % 3], prob_t[n % 2], prob[n % 2]
                wait("dve", exp_tok[n])
                t = done("dve", dve.tensor_reduce(ln_[:, n, :], sc, AX.X, ALU.add))
                wait("dve", t)
                t = done("dve", dve.reciprocal(rl[:, n, :], ln_[:, n, :]))
                wait("dve", *pt_free.get(n - 2, []))
                pt_tok[n] = done("dve", dve.transpose(pt.rearrange("p h w -> p (h w)"), sc.rearrange("p h w -> p (h w)")))
                wait("pool", t, *prob_free.get(n - 2, []))
                t_p = done("pool", pool.tensor_tensor(pr, sc, bcast(rl[:, n, :], 2 * W), ALU.mult))
                score_free[n] = [t_p, pt_tok[n]]
                wait("act", t_p)
                tanh_tok[n] = done("act", act.activation(pr, pr, ACT.Tanh, scale=0.5))

            def weighted_values(n):
                pt, ob = prob_t[n % 2], 4 + n % 2
                wait("pe", pt_tok[n], t_vp, t_pad, *bank_free[ob])
                for h in range(NH):
                    s = (h % 2) * 8 + h // 2
                    for k, vals in enumerate((v_prev, v_own)):
                        for j in range(4):
                            q = slice(W * j, W * j + W)
                            mm = pe.matmul(psum[q, ob, h * HD:(h + 1) * HD], pt[q, s, k * W:(k + 1) * W],
                                           vals[q, n, h * HD:(h + 1) * HD], start=(k == 0), stop=(k == 1),
                                           skip_group_check=True)
                t = done("pe", mm)
                pt_free[n] = [t]
                wait("act", t)
                t = done("act", act.activation(ACC[:, n, :], psum[:, ob, 0:D], ACT.Copy))
                bank_free[ob] = [t]
                u_tok.append(t)

            def tanh_sum(n):
                wait("dve", tanh_tok[n])
                t = done("dve", dve.tensor_reduce(th[:, n, :], prob[n % 2], AX.X, ALU.add))
                prob_free[n] = [t]
                th_tok.append(t)

            for n in range(NT + 3):
                if n < NT:
                    scores(n)
                if n >= 3:
                    tanh_sum(n - 3)
                if 1 <= n <= NT:
                    normalised(n - 1)
                if 2 <= n <= NT + 1:
                    weighted_values(n - 2)
            den, inv, fit, shift = th, per_row(5), per_row(6), per_row(7)
            sums = rstd
            wait("dve", th_tok[-1])
            t = done("dve", dve.tensor_scalar(den, th, 0.5 / T, 1.0, ALU.mult, ALU.add))
            wait("dve", t)
            t = done("dve", dve.reciprocal(inv, den))
            wait("dve", t)
            t = done("dve", dve.tensor_reduce(sums[:, :], inv.rearrange("p i h -> p h i"), AX.X, ALU.add))
            wait("pe", t, *bank_free[6])
            t = done("pe", pe.matmul(psum[:, 6, 0:NH], ones[:], sums[:, :], start=True, stop=True))
            wait("dve", t)
            t = done("dve", dve.tensor_tensor(fit, den, psum[:, 6, 0:NH].unsqueeze(1).broadcast_to([P, NT, NH]), ALU.mult))
            bank_free[6] = [t]
            wait("dve", t)
            t = done("dve", dve.reciprocal(fit, fit))
            wait("act", t)
            t_fit = done("act", act.activation(fit, fit, ACT.Ln))
            wait("dve", t_fit)
            t = done("dve", dve.scalar_tensor_tensor(out=inv, in0=mx, scalar=SC, in1=fit, op0=ALU.mult, op1=ALU.add))
            t2 = done("dve", dve.tensor_scalar(mx, mx, SC, None, ALU.mult))
            wait("dve", t2)
            t = done("dve", dve.tensor_tensor(shift, mx, fit, ALU.add))
            wait("dve", t)
            t = done("dve", dve.tensor_tensor(shift, shift, inv, ALU.subtract))
            wait("act", t)
            t = done("act", act.activation(shift, shift, ACT.Exp))
            wait("dve", t)
            t = done("dve", dve.tensor_tensor(ln_, ln_, shift, ALU.mult))
            wait("dve", t)
            t = done("dve", dve.reciprocal(ln_, ln_))
            wait("dve", t)
            t = done("dve", dve.tensor_tensor(ln_, ln_, shift, ALU.mult))
            tok = []
            wait("dve", t)
            for n in range(NT):
                a = ACC[:, n, :].rearrange("p (a k d) -> p k a d", k=2, d=HD)
                f = ln_[:, n, :].rearrange("p (k a) -> p k a", k=2)
                wait("dve", u_tok[n])
                tok.append(done("dve", dve.tensor_tensor(a, a, bcast(f, HD), ALU.mult)))
            wait("pool", *x_ready)
            t_x = done("pool", pool.tensor_tensor(X[:, :, :], X[:, :, :], bo[:].unsqueeze(1).broadcast_to([P, NT, D]), ALU.add))
            return project_out(tok, wo0, X, [t_x] * NG)

        def project_out(att_ready, w, dst, dst_ready):
            at = feature_major(ACC, att_ready)
            tok = []
            for g in range(NG):
                b = 4 + g % 2
                wait("pe", at[g], *bank_free[b])
                for i in range(GT):
                    n = GT * g + i
                    mm = pe.matmul(psum[:, b, i * P:(i + 1) * P], YT[:, n * P:(n + 1) * P], w[:], start=True, stop=True)
                t = done("pe", mm)
                wait("dve", t, dst_ready[g])
                d = dst[:, GT * g:GT * g + GT, :]
                t = done("dve", dve.tensor_tensor(d, psum[:, b, :].rearrange("p (i d) -> p i d", i=GT), d, ALU.add))
                bank_free[b] = [t]
                tok.append(t)
            barrier()
            return tok

        def latent_block(name, x_ready, during_attention=None, during_moe=None):
            core.stage(name)
            K = 256
            keys = take(0, 8 * T // 2, BF16).rearrange("p (a t) -> p a t", a=8)
            split_q = [take((32 + 8 * i) * K, GT * NH * SLOT // 2, BF16).rearrange("p (n s) -> p n s", s=SLOT) for i in range(2)]
            padded = lambda k: take(k * K, 4 * GW // 2, BF16).rearrange("p (r a t) -> p r a t", r=2, a=2)
            plain_q = [padded(48), padded(52)]
            shift_q = [padded(56), padded(60)]
            N_PROB, LAG, AHEAD, SPARE = 6, 3, 6, 2.5
            prob = [take((64 + 4 * i) * K, 2 * GW).rearrange("p (k t) -> p k t", k=2) for i in range(N_PROB)]
            split_k = take(92 * K, GT * NH * SLOT // 2, BF16).rearrange("p (n s) -> p n s", s=SLOT)
            values = take(100 * K, NT * NH * 9).rearrange("p (i h d) -> p i h d", i=NT, h=NH)
            lat = take(64 * K, NT * KV).rearrange("p (i d) -> p i d", i=NT)
            lat_t = take(68 * K, T)[0:KV, :]
            raw = take(109 * K, GT * D).rearrange("p (n d) -> p n d", d=HD)
            rest = small[:, 0:4, :].rearrange("p a (n d) -> p (a n) d", d=HD)
            turned = small[:, 4:8, :].rearrange("p a (n d) -> p (a n) d", d=HD)

            y_ready = layer_norm(x_ready)
            t_r = rms_stats(Y, y_ready)
            wait("dve", t_r)
            h_ready = [done("dve", dve.tensor_scalar(ACC[:, i, :], Y[:, i, :], rstd[:, i:i + 1], None, ALU.mult))
                       for i in range(NT)]
            ht = feature_major(ACC, h_ready, norm_w[:, 0:1])
            for half in range(2):
                wait("pe", *bank_free[half])
                for i in range(8):
                    n = 8 * half + i
                    wait("pe", ht[n // GT])
                    mm = pe.matmul(psum[:, half, i * KV:(i + 1) * KV], YT[:, n * P:(n + 1) * P], wqd[:, D:D + KV],
                                   start=True, stop=True)
                t = done("pe", mm)
                wait("act", t)
                t = done("act", act.activation(lat[:, 8 * half:8 * half + 8, :],
                                               psum[:, half, :].rearrange("p (i d) -> p i d", i=8), ACT.Copy))
                bank_free[half] = [t]
                wait("dve", t)
                for n in range(8 * half, 8 * half + 8):
                    t = done("dve", dve.bn_stats(stats[:, n, :], lat[:, n, :]))
            wait("dve", t)
            for n in range(NT):
                t = done("dve", dve.bn_aggr(meanvar[:, n, :], stats[:, n, :]))
            t = rsqrt(meanvar[:, :, 1], rstd[:, :], 1.0, EPS_LN, t)
            wait("dve", t)
            for n in range(NT):
                t_l = done("dve", dve.tensor_scalar(lat[:, n, :], lat[:, n, :], meanvar[:, n, 0:1], rstd[:, n:n + 1],
                                                    ALU.subtract, ALU.mult))
            wait("pe", t_l)
            lt = []
            for g in range(NG):
                b = 2 + g % 2
                wait("pe", *bank_free[b])
                for i in range(GT):
                    mm = pe.transpose(psum[0:KV, b, i * P:(i + 1) * P], lat[:, GT * g + i, :], ident[:])
                t = done("pe", mm)
                wait("dve", t)
                t = done("dve", dve.tensor_scalar(lat_t[:, g * GW:(g + 1) * GW], psum[0:KV, b, :], ln_gb[:, 0:1],
                                                  ln_gb[:, 1:2], ALU.mult, ALU.add))
                bank_free[b] = [t]
                lt.append(t)

            t = done("pool", pool.memset(split_k[:, :, 48:64], 0.0))
            wait("pool", t)
            done("pool", pool.memset(split_k[:, :, 48:51], 1.0))
            done("pool", pool.memset(split_q[0][:, :, 48:64], 0.0))
            done("pool", pool.memset(split_q[1][:, :, 48:64], 0.0))
            t_pad = done("pool", pool.memset(take(48 * K, 16 * K), 0.0))
            t_sp = done("pool", pool.memset(values[:, :, :, 8:9], 1.0))

            def rotate(g, src, ready):
                view = lambda t: t.rearrange("p (i h) d -> p i h d", i=GT)
                table = lambda k, a, b: rope[:, k, GT * g:GT * g + GT, a:b].unsqueeze(2).broadcast_to([P, GT, NH, b - a])
                half = HD // 2
                s, d, r = view(src), view(turned), view(rest)
                wait("dve", ready)
                done("dve", dve.tensor_tensor(d, s, table(0, 0, HD), ALU.mult))
                done("dve", dve.tensor_tensor(r[:, :, :, 0:half], s[:, :, :, half:HD], table(1, 0, half), ALU.mult))
                t = done("dve", dve.tensor_tensor(r[:, :, :, half:HD], s[:, :, :, 0:half], table(1, half, HD), ALU.mult))
                wait("dve", t)
                t = done("dve", dve.tensor_tensor(turned, turned, rest, ALU.add))
                return t

            free_raw, free_k, k_tok, v_tok = [], [], [], []
            for g in range(NG):
                for i in range(GT):
                    n, b = GT * g + i, i % 4
                    wait("pe", lt[g], *bank_free[b])
                    t = done("pe", pe.matmul(psum[:, b, 0:2 * D], lat_t[:, n * P:(n + 1) * P], wukv[:], start=True, stop=True))
                    wait("dve", t, t_sp, *free_raw)
                    t_raw = done("dve", dve.tensor_copy(raw[:, i * NH:(i + 1) * NH, :],
                                                        psum[:, b, 0:D].rearrange("p (h d) -> p h d", h=NH)))
                    t_v = done("dve", dve.tensor_copy(values[:, n, :, 0:HD],
                                                      psum[:, b, D:2 * D].rearrange("p (h d) -> p h d", h=NH)))
                    bank_free[b] = [t_v]
                t = rotate(g, raw, t_raw)
                free_raw = [t]
                t_k = split3(turned, split_k, rest, False, t, free_k)
                free_k = to_rows(split_k.rearrange("p (i h) s -> p i (h s)", i=GT), GT,
                                 lambda i: keys[:, :, g * GW + i * P:g * GW + (i + 1) * P], t_k, (4, 5, 6, 7), lambda i: "act")
                k_tok.append(free_k)
                v_tok.append(t_v)

            work = [5, 6, 7]
            turn = [0]

            def work_bank():
                turn[0] += 1 if work[(turn[0] + 1) % 3] != state.get("held") else 2
                return work[turn[0] % 3]

            state = {}
            eng_of = {"dve": dve, "pool": pool}

            def prepare_q(g, i, e):
                n, b, v = GT * g + i, work_bank(), eng_of[e]
                s, r, d = (t[:, i * NH:(i + 1) * NH, :] for t in (raw, rest, turned))
                sq = split_q[g % 2][:, i * NH:(i + 1) * NH, :]
                table = lambda k, lo, hi: rope[:, k, n, lo:hi].unsqueeze(1).broadcast_to([P, NH, hi - lo])
                half = HD // 2
                wait("pe", *bank_free[b])
                t = done("pe", pe.matmul(psum[:, b, 0:D], YT[:, n * P:(n + 1) * P], wqd[:, 0:D], start=True, stop=True))
                wait("act", t, state.get(("raw", i), t_k[0]), *free_raw)
                t = done("act", act.activation(s, psum[:, b, 0:D].rearrange("p (h d) -> p h d", h=NH), ACT.Copy))
                bank_free[b] = [t]
                wait(e, t, t_sp, state.get(("raw", i)), *free_raw, *t_k, *state.get(("turned", g - 2), []))
                done(e, v.tensor_tensor(d, s, table(0, 0, HD), ALU.mult))
                done(e, v.tensor_tensor(r[:, :, 0:half], s[:, :, half:HD], table(1, 0, half), ALU.mult))
                t = done(e, v.tensor_tensor(r[:, :, half:HD], s[:, :, 0:half], table(1, half, HD), ALU.mult))
                wait(e, t)
                t = done(e, v.tensor_tensor(d, d, r, ALU.add))
                done(e, v.memset(sq[:, :, 48:51], 0.0))
                part = d
                for lo, copies in ((0, 3), (3, 2), (5, 1)):
                    wait(e, t)
                    dst = sq[:, :, lo * HD:(lo + copies) * HD].rearrange("p h (k d) -> p h k d", k=copies)
                    t = done(e, v.tensor_copy(dst, part.unsqueeze(2).broadcast_to([P, NH, copies, HD])))
                    if lo < 5:
                        wait(e, t)
                        t = done(e, v.tensor_tensor(r, part, sq[:, :, lo * HD:(lo + 1) * HD], ALU.subtract))
                        part = r
                state[("raw", i)] = t
                state[("split", g, i)] = t

            row_max = take(111 * K, 64).rearrange("p (n c) -> p n c", c=4)
            shift = take(111 * K + 64, GT * 4)
            part_ = take(111 * K + 80, GT * 4)
            inv_flat = take(111 * K + 96, GT * 4)

            def turn_queries(g, hq, dst, before, free):
                b = work_bank()
                half = psum[:, b, :].bitcast(BF16).rearrange("p (a t) -> p a t", a=2)
                wait("pe", *before, *bank_free[b])
                for a in range(2):
                    for i in range(GT):
                        pair = split_q[g % 2][:, i * NH + 4 * hq + 2 * a:i * NH + 4 * hq + 2 * a + 2, :]
                        mm = pe.transpose(half[:, a, i * P:(i + 1) * P], pair.rearrange("p h s -> p (h s)"), identb[:])
                t = done("pe", mm)
                wait("act", t, t_pad, *free)
                for r in range(2):
                    rows = slice(SLOT * r, SLOT * r + SLOT)
                    t2 = done("act", act.activation(dst[rows, r], half[rows], ACT.Copy))
                bank_free[b] = [t2]
                return t, t2

            def max_items(g, hq):
                u = 4 * g + hq
                sq, plain = split_q[g % 2], plain_q[u % 2]

                def first():
                    _, state[("plain", u)] = turn_queries(g, hq, plain, [state[("split", g, i)] for i in range(GT)],
                                                          [state.get(("maxed", u - 2))])

                def one(i, hh, c):
                    n, a, r = GT * g + i, hh // 2, hh % 2
                    w = min(GW, (n + 1) * P - c * GW)
                    diag = c == g
                    b = work_bank()
                    wait("pe", state[("plain", u)], *k_tok[c], *bank_free[b])
                    mm = pe.matmul(psum[:, b, 0:w], plain[:, r, a, i * P:(i + 1) * P],
                                   keys[:, 2 * hq + a, c * GW:c * GW + w], start=True, stop=not diag)
                    if diag:
                        mm = pe.matmul(psum[:, b, w - P:w], identb[:], mask_q[:], start=False, stop=True)
                    t = done("pe", mm)
                    wait("dve", t, state.get("max_free"))
                    t = done("dve", dve.tensor_reduce(row_max[:, i * 4 + hh, c:c + 1], psum[:, b, 0:w], AX.X, ALU.max))
                    bank_free[b] = [t]
                    state[("maxed", u)] = t

                def finish():
                    wait("dve", state[("maxed", u)])
                    t = done("dve", dve.tensor_reduce(shift, row_max[:, :, 0:g + 1], AX.X, ALU.max, negate=True))
                    state["max_free"] = t
                    heads = sq.rearrange("p (i h) s -> p i h s", i=GT)[:, :, 4 * hq:4 * hq + 4, :]
                    src, rem = (v.rearrange("p (i h) -> p i h", i=GT) for v in (shift, part_))
                    wait("dve", state[("plain", u)])
                    for k in range(3):
                        wait("dve", t)
                        t = done("dve", dve.tensor_copy(heads[:, :, :, 48 + k], src))
                        if k < 2:
                            wait("dve", t)
                            t = done("dve", dve.tensor_tensor(rem, src, heads[:, :, :, 48 + k], ALU.subtract))
                            src = rem
                    state[("chained", u)] = t

                def turn_shifted():
                    t_pe, state[("shift", u)] = turn_queries(g, hq, shift_q[u % 2], [state[("chained", u)]],
                                                             [state.get(("scored", u - 2))])
                    state.setdefault(("turned", g), []).append(t_pe)

                tiles = [lambda i=i, hh=hh, c=c: one(i, hh, c) for i in range(GT) for hh in range(4) for c in range(g + 1)]
                return first, tiles, finish, turn_shifted

            prob_free = [None] * N_PROB
            prob_turn = [0]
            ot = take(88 * K, GW)
            O_BANK = 4
            wait("dve", *bank_free[O_BANK])
            bank_free[O_BANK] = [done("dve", dve.memset(psum[:, O_BANK, :], 0.0))]
            att_tok = {}

            def score(u, j, a):
                g, hq = u // 4, u % 4
                off = P * max(0, j - GT * g)
                for r in range(2):
                    b = 2 * a + r
                    wait("pe", state[("shift", u)], k_tok[j // GT][j % GT], *bank_free[b])
                    mm = pe.matmul(psum[:, b, off:GW], keys[:, 2 * hq + a, j * P:(j + 1) * P],
                                   shift_q[u % 2][:, r, a, off:GW], start=True, stop=(j < GT * g))
                if j >= GT * g:
                    for r in range(2):
                        mm = pe.matmul(psum[:, 2 * a + r, off:off + P], identb[:], mask_k[:], start=False, stop=True)
                t = done("pe", mm)
                state[("scored", u)] = t
                pr = prob_turn[0] % N_PROB
                prob_turn[0] += 1
                wait("act", t, prob_free[pr])
                t = done("act", act.activation(prob[pr][:, :, off:GW], psum[:, 2 * a:2 * a + 2, off:GW], ACT.Exp,
                                               scale=INV_SQRT_HD))
                bank_free[2 * a] = [t]
                bank_free[2 * a + 1] = [t]
                return pr, off, t

            def weigh(u, j, a, pr, off, t_exp):
                g, hq = u // 4, u % 4
                wait("pe", t_exp, *v_tok)
                if j == 0:
                    wait("pe", *bank_free[O_BANK])
                for r in range(2):
                    hh = 2 * a + r
                    mm = pe.matmul(psum[32 * hh:32 * hh + 9, O_BANK, off:GW], values[:, j, 4 * hq + hh, :],
                                   prob[pr][:, r, off:GW], start=(j == 0), stop=(j == GT * g + GT - 1),
                                   skip_group_check=True)
                t = done("pe", mm)
                prob_free[pr] = t
                state["weighed"] = t

            def take_out():
                wait("act", state["weighed"], state.get("ot_free"))
                state["ot"] = done("act", act.activation(ot, psum[:, O_BANK, :], ACT.Copy))
                bank_free[O_BANK] = [state["ot"]]

            def turn_out():
                b = state["held"] = work_bank()
                wait("pe", state["ot"], *bank_free[b])
                for i in range(GT):
                    mm = pe.transpose(psum[:, b, i * P:(i + 1) * P], ot[:, i * P:(i + 1) * P], ident[:])
                state["ot_free"] = done("pe", mm)

            def normalise(u):
                g, hq, b, t = u // 4, u % 4, state.pop("held"), state["ot_free"]
                back_ = psum[:, b, :].rearrange("p (i h s) -> p i h s", i=GT, h=4)
                inv_sum = inv_flat.rearrange("p (i h) -> p i h", i=GT)
                wait("dve", t, state.get("inv_free"))
                t = done("dve", dve.reciprocal(inv_sum, back_[:, :, :, 8]))
                wait("dve", t)
                dst = ACC[:, GT * g:GT * g + GT, 4 * hq * HD:(4 * hq + 4) * HD].rearrange("p i (h d) -> p i h d", h=4)
                t = done("dve", dve.tensor_tensor(dst, back_[:, :, :, 0:HD], bcast(inv_sum, HD), ALU.mult))
                state["inv_free"] = t
                bank_free[b] = [t]
                att_tok[g] = t

            n_units = 4 * NG
            side, mark = [], []
            parts = [max_items(u // 4, u % 4) for u in range(n_units)]
            for u in range(n_units):
                first, tiles, finish, turn_shifted = parts[u]
                mine = ([first] if u == 0 else []) + tiles[0 if u == 0 else AHEAD:]
                if u + 1 < n_units:
                    g = (u + 1) // 4
                    mine.insert(len(mine) // 2 if g == u // 4 else len(mine) - 4, parts[u + 1][0])
                if u in (0, 5, 9):
                    for i in range(GT):
                        mine.insert(1 + (i + 1) * len(mine) // 6, lambda g=u // 4 + 1, i=i: prepare_q(g, i, "pool"))
                if u == 8 and during_attention is not None:
                    others = during_attention(work_bank)
                    for k, piece in enumerate(others):
                        mine.insert(1 + k + (k + 1) * (len(mine) - k - 2) // len(others), piece)
                side += mine + [finish] + (parts[u + 1][1][:AHEAD] if u + 1 < n_units else []) + [turn_shifted]
                mark.append(len(side))
            for i in range(GT):
                prepare_q(0, i, "dve")
            given = 0

            def give(target):
                nonlocal given
                while given < min(target, len(side)):
                    side[given]()
                    given += 1

            give(mark[0])
            later = []
            out_steps = []

            def catch_up(lag, most):
                while len(later) > lag and most:
                    u, j, *_ = later[0]
                    weigh(*later.pop(0))
                    most -= 1
                    if not later or later[0][0] != u:
                        take_out()
                        out_steps.extend([turn_out, lambda u=u: normalise(u)])
                        return

            for u in range(n_units):
                steps = [(j, a) for j in range(GT * (u // 4) + GT) for a in range(2)]
                begin = given
                span = 1 - SPARE / len(steps)
                for s, (j, a) in enumerate(steps):
                    got = score(u, j, a)
                    later.append((u, j, a, *got))
                    frac = (s + 1) / len(steps)
                    if out_steps:
                        out_steps.pop(0)()
                    if u + 1 < n_units:
                        give(round(begin + (mark[u + 1] - begin) * min(1, frac / span)))
                        if frac > span and u + 2 < n_units:
                            give(round(mark[u + 1] + (mark[u + 2] - mark[u + 1]) * (frac - span)))
                    if len(out_steps) != 2 or len(later) >= N_PROB - 1:
                        catch_up(LAG, 2)
            catch_up(0, len(later))
            for f in out_steps:
                f()
            y2 = project_out([att_tok[i // GT] for i in range(NT)], wo1, Y, [att_tok[g] for g in range(NG)])
            t_r = rms_stats(Y, [y2[i // GT] for i in range(NT)])
            wait("dve", t_r)
            h_ready = [done("dve", dve.tensor_scalar(ACC[:, i, :], Y[:, i, :], rstd[:, i:i + 1], None, ALU.mult))
                       for i in range(NT)]
            ht = feature_major(ACC, h_ready, norm_w[:, 1:2])
            acc = moe(NE1, ht, gate1, gateb1, order1, w1_1, b1_1, w2_1, b2_1, const_in, residual=Y,
                      beside=[] if during_moe is None else during_moe())
            tok = add_half(acc)
            barrier()
            return tok

        toep = take(0, D * P).rearrange("p (m x) -> p m x", m=D)
        b_in = take(64 * 256, D * NS).rearrange("p (m n) -> p m n", m=D)
        decay = sb("decay", [P, 64])
        taps = nc.dram_tensor("taps", (D, 2 * P), F32).ap()

        def ssm_far_table(work_bank):
            back = take(111 * 256 + 112, P + 1)
            zero = take(90 * 256, P)
            k_rev = take(92 * 256, T).rearrange("p (b x) -> p b x", b=4)
            tok = {}

            def rates():
                wait("sp", *core.last.values())
                t_back = dma("sp", "ld_back", back, ins["back"])
                wait("act", const_in)
                t1 = done("act", act.activation(logdt_pair[:], logdt_pair[:], ACT.Exp))
                t2 = done("act", act.activation(alog_col[:], alog_col[:], ACT.Exp))
                wait("pool", t1, t2, const_in, *core.last.values())
                t = done("pool", pool.tensor_scalar(logdt_pair[:], logdt_pair[:], alog_col[:, 0:1], -1.0, ALU.mult, ALU.mult))
                done("pool", pool.memset(zero, 0.0))
                wait("act", t, t_back)

            def powers(a):
                for k in range(a, a + 4):
                    tok["exp"] = done("act", act.activation(E_far[:, k, :], back, ACT.Exp, scale=logdt_pair[:, k:k + 1]))

            def times_c(q):
                s = slice(16 * q, 16 * q + 16)
                wait("pool", tok["exp"])
                t = done("pool", pool.tensor_copy(decay[:, s], E_far[:, s, 0]))
                wait("pool", t)
                tok["mul", q] = done("pool", pool.tensor_tensor(E_far[:, s, :], E_far[:, s, :], bcast(c_pair[:, s], P + 1), ALU.mult))

            def sum_states(bank):
                b = work_bank()
                wait("pe", tok["mul", bank], *bank_free[b])
                for a in range(16 * bank, 16 * bank + 16):
                    q, k = a % 4, a // 4 % 4
                    mm = pe.matmul(psum[32 * q:32 * q + 32, b, k * P:(k + 1) * P], pairs2[:], E_far[:, a, 1:P + 1],
                                   start=True, stop=True)
                t = done("pe", mm)
                wait("act", t)
                tok["k"] = done("act", act.activation(k_rev[:, bank, :], psum[:, b, :], ACT.Copy))
                bank_free[b] = [tok["k"]]

            def store():
                wait("sp", tok["k"], tok["mul", 3])
                for q in range(4):
                    dma("sp", "st_taps", bass.AP(tensor=taps.tensor, offset=2 * q * 2 * P, ap=[[2 * P, 2], [8 * 2 * P, 16], [1, P]]),
                        take(92 * 256, T)[32 * q:32 * q + 2, :].rearrange("p (s x) -> p s x", s=16))
                t_taps[0] = dma("sp", "st_taps", taps[:, P:2 * P], zero)

            pieces = [rates]
            for q in range(4):
                pieces += [lambda a=a: powers(a) for a in range(16 * q, 16 * q + 16, 4)] + [lambda q=q: times_c(q)]
            return pieces + [lambda b=b: sum_states(b) for b in range(4)] + [store]

        def ssm_near_tables():
            step = D // 8
            for e in ("act", "dve", "pool"):
                wait(e, t_taps[0])

            def blocks():
                wait("sp", t_taps[0], *core.last.values())
                wait("act", t_taps[0], *core.last.values())
                dma("sp", "ld_dt", logdt_all, on_all(ins["L1_attn_log_dt"], 0, D))
                t_dt[0] = dma("sp", "ld_dt", alog_all, on_all(ins["L1_attn_A_log"], 0, NS))
                for m in range(0, D, step):
                    t_toep[0] = dma("sp" if (m // step) % 2 else "act", "ld_toep", toep[:, m:m + step, :],
                                    bass.AP(tensor=taps.tensor, offset=m * 2 * P, ap=[[1, P], [2 * P, step], [1, P]]))

            def rates():
                wait("act", t_dt[0])
                t1 = done("act", act.activation(logdt_all, logdt_all, ACT.Exp))
                t2 = done("act", act.activation(alog_all, alog_all, ACT.Exp))
                done("pool", pool.tensor_scalar(neg_back[:], back_col[:], -1.0, None, ALU.mult))
                wait("pool", t1, t2)
                t_dt[0] = done("pool", pool.tensor_tensor(b_in, bcast(logdt_all, NS),
                                                          alog_all.unsqueeze(1).broadcast_to([P, D, NS]), ALU.mult))

            def powers(m):
                wait("act", t_dt[0])
                t_bin[0] = done("act", act.activation(b_in[:, m:m + step, :], b_in[:, m:m + step, :], ACT.Exp,
                                                      scale=neg_back[:, 0:1]))

            idle = lambda: None
            return [blocks, rates, idle, idle, idle, idle] + [lambda m=m: powers(m) for m in range(0, D, step)]

        neg_back = sb("neg_back", [P, 1])
        t_taps, t_toep, t_dt, t_bin = [None], [None], [None], [None]

        def ssm(name, x_ready):
            core.stage(name)
            C17 = NT + 1
            state_in = take(96 * 256, 64 * C17)
            states = take(101 * 256, 64 * C17)
            mult = take(106 * 256, 64 * C17)
            v3 = lambda t: t.rearrange("p (a c) -> p a c", a=64)
            y_ready = layer_norm(x_ready)
            tz = done("pool", pool.memset(v3(state_in)[:, :, 0:1], 0.0))
            done("pool", pool.memset(v3(mult)[:, :, 0:1], 0.0))
            t_mult = done("pool", pool.tensor_copy(v3(mult)[:, :, 1:C17], bcast(decay[:], NT)))
            for n in range(NT):
                wait("pool", y_ready[n])
            t = done("pool", pool.tensor_tensor(ACC[:, :, :], Y[:, :, :], skip_d[:].unsqueeze(1).broadcast_to([P, NT, D]), ALU.mult))
            wait("pool", t)
            t_skip = done("pool", pool.tensor_tensor(X[:, :, :], X[:, :, :], ACC[:, :, :], ALU.add))
            wait("pe", t_bin[0], *y_ready, *bank_free[0], *bank_free[1])
            for a in range(64):
                for r in range(2):
                    mm = pe.matmul(psum[64 * r:64 * r + 64, a // 32, (a % 32) * NT:(a % 32 + 1) * NT],
                                   b_in[:, 2 * a + r, :], Y[:, :, 2 * a + r], start=True, stop=True)
            t = done("pe", mm)
            wait("dve", t, tz)
            t = done("dve", dve.tensor_copy(v3(state_in)[:, :, 1:C17], psum[:, 0:2, :].rearrange("p b (a c) -> p (b a) c", c=NT)))
            bank_free[0] = bank_free[1] = [t]
            wait("dve", t, t_mult)
            t_st = done("dve", dve.tensor_tensor_scan(states, mult, state_in, 0.0, ALU.mult, ALU.add))
            st3 = v3(states)
            rows_free, tok = [], None
            banks = (0, 1, 2, 3)
            for b in banks:
                wait("dve", *bank_free[b])
                t = done("dve", dve.memset(psum[:, b, :], 0.0))
                bank_free[b] = [t]
            ysb = [ACC[:, 4 * i:4 * i + 4, :] for i in range(4)]
            wait("act", t_skip)
            wait("pe", t_toep[0])
            ysb_free = [[], [], [], []]
            for grp in range(8):
                b = grp % 4
                wait("pe", *bank_free[b])
                for qd in range(4):
                    for q in range(4):
                        m = 16 * grp + 4 * qd + q
                        o = psum[32 * q:32 * q + NT, b, qd * P:(qd + 1) * P]
                        pe.matmul(o, Y[:, :, m], toep[:, m, :], start=True, stop=False, skip_group_check=True)
                    if qd == 0 and grp == 0:
                        wait("pe", t_st)
                    for q in range(4):
                        m = 16 * grp + 4 * qd + q
                        r = 64 * (m % 2)
                        o = psum[32 * q:32 * q + NT, b, qd * P:(qd + 1) * P]
                        mm = pe.matmul(o, st3[r:r + 64, m // 2, 0:NT], E_far[r:r + 64, m // 2, 0:P], start=False,
                                       stop=True, skip_group_check=True)
                t = done("pe", mm)
                ys = ysb[grp % 4]
                wait("act", t, *ysb_free[grp % 4])
                t = done("act", act.activation(ys, psum[:, b, :].rearrange("p (k x) -> p k x", k=4)[:, :, ::-1], ACT.Copy))
                bank_free[b] = [t]
                tb = 4 + grp % 2
                wait("pe", t, *bank_free[tb])
                for qd in range(4):
                    mm = pe.transpose(psum[:, tb, qd * P:(qd + 1) * P], ys[:, qd, :], ident[:])
                t = done("pe", mm)
                ysb_free[grp % 4] = [t]
                wait("dve", t, t_skip)
                add = psum[:, tb, :].rearrange("p (m c) -> p c m", c=32)[:, 0:NT, :]
                dst = X[:, :, 16 * grp:16 * grp + 16]
                tok = done("dve", dve.tensor_tensor(dst, add, dst, ALU.add))
                bank_free[tb] = [tok]
            barrier()
            return [tok] * NG

        ready = macaron_ffn("ffa", x_in)
        if upto >= 2:
            ready = windowed_attention("win", ready)
        if upto >= 3:
            ready = macaron_ffn("ffb", ready)
        if upto >= 4:
            ready = latent_block("la", ready, during_attention=ssm_far_table, during_moe=ssm_near_tables)
            wait("sp", t_toep[0])
        if upto >= 5:
            ready = ssm("ssm", ready)
        if upto >= 6:
            ready = latent_block("lb", ready)
        core.stage("end")
        out_view = out[0].rearrange("(i p) f -> p i f", p=P)
        for g in range(NG):
            wait("sp", ready[g])
            t = dma("sp", "st_out", out_view[:, GT * g:GT * g + GT, :], X[:, GT * g:GT * g + GT, :])
        wait("sp", t, const_in)


_RAW = ["L0_attn_x", "L0_attn_bq", "L0_attn_bk", "L0_attn_bv", "L0_attn_wo", "L0_attn_bo", "L0_attn_qn_w",
        "L0_attn_kn_w", "L0_ffn_gate_b", "L0_ffn_b2", "L1_attn_A_log", "L1_attn_D", "L1_attn_log_dt",
        "L1_ffn_gate_b", "L1_ffn_b2"]


def kernel(**inputs):
    import numpy as np
    import concourse.bacc as _bacc
    from concourse.bass_utils import run_bass_kernel_spmd as _run

    a = {n: np.ascontiguousarray(inputs[n]) for n in _RAW}
    g = {n: np.asarray(v) for n, v in inputs.items()}

    def lay(name, value):
        a[name] = np.ascontiguousarray(value)

    lay("gate0", g["L0_ffn_gate_w"].T)
    lay("gate1", g["L1_ffn_gate_w"].T)
    for k, (w1, b1, w2, ne) in enumerate((("L0_ffn_w1", "L0_ffn_b1", "L0_ffn_w2", NE0), ("L1_ffn_W1", "L1_ffn_b1", "L1_ffn_W2", NE1))):
        lay(f"w1_{k}", g[w1].transpose(2, 0, 1))
        lay(f"b1_{k}", g[b1].reshape(ne * HC, P).T)
        lay(f"w2_{k}", g[w2].reshape(ne, D, HC, P).transpose(3, 0, 2, 1))
    lay("wqkv", np.concatenate([g["L0_attn_wq"], g["L0_attn_wk"], g["L0_attn_wv"]], axis=1))
    lay("wqd", np.concatenate([g["L1_ffn_Wq"].T, g["L1_ffn_Wdkv"].T], axis=1))
    lay("wukv", np.concatenate([g["L1_ffn_Wuk"].T, g["L1_ffn_Wuv"].T], axis=1))
    lay("wo1", g["L1_ffn_Wo"].T)
    lay("norm_w", np.stack([g["L1_ffn_norm1_w"], g["L1_ffn_norm2_w"]], axis=1))
    lay("ln_gb", np.stack([g["L1_ffn_ln_g"], g["L1_ffn_ln_b"]], axis=1))
    lay("c_pair", g["L1_attn_C_re"].reshape(64, 2 * NS).T)

    lay("logdt_pair", g["L1_attn_log_dt"].reshape(64, 2).T)
    lay("alog_col", g["L1_attn_A_log"][:, None])

    f = np.float32
    lay("order0", np.tile(np.arange(NE0, 0, -1, dtype=f), (P, 1)))
    lay("order1", np.tile(np.arange(NE1, 0, -1, dtype=f), (P, 1)))
    row, col = np.arange(P)[:, None] % W, np.arange(2 * W)[None, :]
    ok = (col <= row + W) & (col > row)
    first = ok & ((np.arange(P)[:, None] >= W) | (col >= W))
    lay("window_mask", np.stack([np.where(first, 0, MASKED), np.where(ok, 0, MASKED)], axis=1).astype(f))
    half = HD // 2
    inv_freq = (f(1.0) / f(10000.0) ** (np.arange(half, dtype=f) / f(half))).astype(f)
    ang = np.arange(T, dtype=f)[:, None] * inv_freq[None, :]
    sin, cos = np.sin(ang).astype(f), np.cos(ang).astype(f)
    table = np.stack([np.concatenate([cos, cos], 1), np.concatenate([-sin, sin], 1)])
    lay("rope", table.reshape(2, NT, P, HD).transpose(2, 0, 1, 3))
    lay("back", np.tile(np.arange(P, -1, -1, dtype=f), (P, 1)))
    lay("back_col", np.arange(P - 1, -1, -1, dtype=f)[:, None])

    nc = _bacc.Bacc("TRN2", target_bir_lowering=False, num_devices=1)
    arrays = {f"in_{n}": v for n, v in a.items()}
    ins = {n: nc.dram_tensor(f"in_{n}", v.shape, mybir.dt.from_np(v.dtype), kind="ExternalInput").ap() for n, v in a.items()}
    out = nc.dram_tensor("out_0", (1, T, D), F32, kind="ExternalOutput").ap()
    build(nc, ins, out, UPTO)
    r = _run(nc, [arrays], core_ids=[0])
    return r.results[0]["out_0"]


UPTO = 6
```

```python
from contextlib import ExitStack

import concourse.bass as bass
from concourse import mybir

F32 = mybir.dt.float32
BF16 = mybir.dt.bfloat16
ALU = mybir.AluOpType
ACT = mybir.ActivationFunctionType
AX = mybir.AxisListType

P = 128
T = 2048
NT = T // P
D = 128
NH = 16
HD = D // NH
W = 32
HID = 512
HC = HID // P
NE0, NE1 = 8, 4
KV = 64
NS = 64
GT = 4
NG = NT // GT
GW = GT * P
SLOT = 64
MASKED = -1e30
EPS_LN, EPS_RMS = 1e-5, 1e-6
EPS_F32 = 1.1920928955078125e-07
INV_SQRT_HD = 1.0 / HD ** 0.5


class Core:

    def __init__(self, nc, ctx):
        self.nc, self.ctx = nc, ctx
        self.eng = {"pe": nc.tensor, "dve": nc.vector, "act": nc.scalar, "pool": nc.gpsimd, "sp": nc.sync}
        self.seen = {e: {} for e in self.eng}
        self.last = {}
        self.count = {}
        self.sems = {}
        self.stage_name = ""

    def stage(self, name):
        self.stage_name = name

    def sem(self, name):
        if name not in self.sems:
            self.sems[name] = self.ctx.enter_context(self.nc.semaphore(name))
            self.count[name] = 0
        return self.sems[name]

    def wait(self, engine, *tokens):
        for token in tokens:
            if token is None:
                continue
            name, value = token
            if self.seen[engine].get(name, 0) < value:
                self.seen[engine][name] = value
                self.eng[engine].wait_ge(self.sems[name], value)

    def done(self, engine, instruction):
        name = f"{self.stage_name}_{engine}"
        instruction.then_inc(self.sem(name), 1)
        self.count[name] += 1
        self.last[engine] = (name, self.count[name])
        return self.last[engine]

    def dma(self, engine, name, out, in_):
        sem = self.sem(name)
        self.eng[engine].dma_start(out, in_).then_inc(sem, 16)
        self.count[name] += 16
        return name, self.count[name]

    def barrier(self):
        for engine in ("pe", "dve", "act", "pool"):
            self.wait(engine, *self.last.values())


def bcast(ap, n):
    return ap.unsqueeze(len(ap.shape)).broadcast_to(list(ap.shape) + [n])


def on_all(ap, offset, n):
    return bass.AP(tensor=ap.tensor, offset=offset, ap=[[0, P], [1, n]])


def build(nc, ins, out, upto=6):
    with ExitStack() as ctx:
        core = Core(nc, ctx)
        wait, done, dma, barrier = core.wait, core.done, core.dma, core.barrier
        pe, dve, act, pool = nc.tensor, nc.vector, nc.scalar, nc.gpsimd

        def sb(name, shape, dt=F32):
            return ctx.enter_context(nc.sbuf_tensor(name, shape, dt))

        psum = ctx.enter_context(nc.psum_tensor("psum", [P, 8, GW], F32))
        bank_free = [[] for _ in range(8)]

        X = sb("X", [P, NT, D])
        Y = sb("Y", [P, NT, D])
        YT = sb("YT", [P, T])
        ACC = sb("ACC", [P, NT, D])
        ident = sb("ident", [P, P])
        identb = sb("identb", [P, P], BF16)
        stats = sb("stats", [P, NT, 6])
        meanvar = sb("meanvar", [P, NT, 2])
        rstd = sb("rstd", [P, NT])
        small = sb("small", [P, 8, P])

        big_w = sb("big_w", [P, 64 * 129])
        w1_0 = big_w[:, 0:NE0 * HID].rearrange("p (e h) -> p e h", e=NE0)
        w2_0 = big_w[:, NE0 * HID:2 * NE0 * HID].rearrange("p (e c d) -> p e c d", e=NE0, c=HC)
        E_far = big_w[:, :].rearrange("p (a x) -> p a x", a=64)
        w4 = sb("w4", [P, 2 * NE1 * HID])
        w1_1 = w4[:, 0:NE1 * HID].rearrange("p (e h) -> p e h", e=NE1)
        w2_1 = w4[:, NE1 * HID:2 * NE1 * HID].rearrange("p (e c d) -> p e c d", e=NE1, c=HC)

        ARENA = 112 * 256
        arena = sb("arena", [P, ARENA])

        def take(start, n, dt=F32):
            part = arena[:, start:start + n]
            return part if dt is F32 else part.bitcast(dt)

        hidden_flat = take(96 * 256, 4096)
        SLOTS = (NT + NE0 - 1) * P
        sorted_rows = nc.dram_tensor("sorted_rows", (SLOTS, D), F32).ap()
        made_rows = nc.dram_tensor("made_rows", (T + SLOTS, D), F32).ap()
        slot_row = nc.dram_tensor("slot_row", (SLOTS, 1), mybir.dt.uint32).ap()
        numbers_view = slot_row.rearrange("(p s) o -> p (s o)", p=P)
        number_place = sb("number_place", [P, 2, NT], mybir.dt.uint32)
        row_of_slot = sb("row_of_slot", [P, NT + NE0 - 1], mybir.dt.uint32)
        slot = sb("slot", [P, NT], mybir.dt.uint32)
        tile_expert = sb("tile_expert", [P, NT + NE0 - 1], mybir.dt.int32)

        def dma_indirect(name, out_, out_offset, in_, in_offset):
            sem = core.sem(name)
            pool.indirect_dma_start(out_, out_offset, in_, in_offset).then_inc(sem, 16)
            core.count[name] += 16
            return name, core.count[name]

        def load(name, shape, src, dt=F32, engine="sp", group="ld_const"):
            t = sb(name, shape, dt)
            return t, dma(engine, group, t[:], src)

        x_view = ins["L0_attn_x"][0].rearrange("(i p) f -> p i f", p=P)
        x_in = [dma("sp", f"ld_x{g}", X[:, GT * g:GT * g + GT, :], x_view[:, GT * g:GT * g + GT, :]) for g in range(NG)]
        small_group = "ld_moe0"
        gate0, _ = load("gate0", [P, NE0], ins["gate0"], group=small_group, engine="act")
        gateb0, _ = load("gateb0", [P, NE0], on_all(ins["L0_ffn_gate_b"], 0, NE0), group=small_group, engine="act")
        tile_start, _ = load("tile_start", [P, NT + NE0 - 1], ins["tile_start"], group=small_group, engine="act")
        order0, _ = load("order0", [P, NE0], ins["order0"], group=small_group, engine="act")
        dma("act", small_group, w1_0, ins["w1_0"])
        moe0_in = dma("act", small_group, w2_0, ins["w2_0"])

        wqkv, _ = load("wqkv", [P, 3 * D], ins["wqkv"])
        qk_w = sb("qk_w", [P, 2, HD])
        dma("sp", "ld_const", qk_w[:, 0, :], on_all(ins["L0_attn_qn_w"], 0, HD))
        dma("sp", "ld_const", qk_w[:, 1, :], on_all(ins["L0_attn_kn_w"], 0, HD))
        wo0, _ = load("wo0", [P, D], ins["L0_attn_wo"])
        bo, _ = load("bo", [P, D], on_all(ins["L0_attn_bo"], 0, D))
        window_mask, _ = load("window_mask", [P, 2, 2 * W], ins["window_mask"])
        gate1, _ = load("gate1", [P, NE1], ins["gate1"])
        gateb1, _ = load("gateb1", [P, NE1], on_all(ins["L1_ffn_gate_b"], 0, NE1))
        order1, _ = load("order1", [P, NE1], ins["order1"])
        norm_w, _ = load("norm_w", [P, 2], ins["norm_w"])
        ln_gb, _ = load("ln_gb", [KV, 2], ins["ln_gb"])
        wqd, _ = load("wqd", [P, D + KV], ins["wqd"])
        wukv, _ = load("wukv", [KV, 2 * D], ins["wukv"])
        wo1, _ = load("wo1", [P, D], ins["wo1"])
        rope, _ = load("rope", [P, 2, NT, HD], ins["rope"])
        skip_d, _ = load("skip_d", [P, D], on_all(ins["L1_attn_D"], 0, D))
        c_pair, _ = load("c_pair", [P, 64], ins["c_pair"])
        logdt_pair = sb("logdt_pair", [P, 64])
        for r in range(2):
            dma("sp", "ld_const", logdt_pair[64 * r:64 * r + 64, :],
                bass.AP(tensor=ins["logdt_pair"].tensor, offset=64 * r, ap=[[0, 64], [1, 64]]))
        alog_col = sb("alog_col", [P, 1])
        for r in range(2):
            dma("sp", "ld_const", alog_col[64 * r:64 * r + 64, :], ins["alog_col"])
        logdt_all, alog_all = window_mask[:].rearrange("p k w -> p (k w)"), bo[:, 0:NS]
        back_col, _ = load("back_col", [P, 1], ins["back_col"])
        dma("sp", "ld_const", w1_1, ins["w1_1"])
        const_in = dma("sp", "ld_const", w2_1, ins["w2_1"])

        core.stage("setup")
        ones = sb("ones", [P, P])
        mask_q = sb("mask_q", [P, P], BF16)
        mask_k = sb("mask_k", [P, P], BF16)
        pairs2 = sb("pairs2", [P, 32])
        t_z = done("pool", pool.memset(ident[:], 0.0))
        wait("pool", t_z)
        t_id = done("pool", pool.affine_select(out=ident[:], in_=ident[:], compare_op=ALU.not_equal, fill=1.0,
                                               base=0, pattern=[[-1, P]], channel_multiplier=1))
        wait("pool", t_id)
        t_idb = done("pool", pool.tensor_copy(identb[:], ident[:]))
        t_m = done("pool", pool.memset(mask_q[:], 0.0))
        t_m2 = done("pool", pool.memset(mask_k[:], 0.0))
        numbers = sb("numbers", [P, 2 * NT + NE0 - 1], mybir.dt.uint32)
        done("pool", pool.iota(numbers[:], pattern=[[P, 2 * NT + NE0 - 1]], base=0, channel_multiplier=1))
        token_number, no_token = numbers[:, 0:NT], numbers[:, NT:2 * NT + NE0 - 1]
        above = sb("above", [P, P])
        done("pool", pool.memset(above[:], 1.0))
        t_ones = done("pool", pool.memset(ones[:], 1.0))
        blank = take(64 * 256, D)
        t = done("dve", dve.memset(blank, 0.0))
        wait("sp", t)
        t_sorted0 = dma("sp", "st_blank", sorted_rows.rearrange("(s p) d -> p s d", p=P),
                        blank.unsqueeze(1).broadcast_to([P, NT + NE0 - 1, D]))
        t_p = done("pool", pool.memset(pairs2[:], 0.0))
        wait("pool", t_p)
        done("pool", pool.affine_select(out=above[:], in_=above[:], compare_op=ALU.is_ge, fill=0.0,
                                        base=-1, pattern=[[1, P]], channel_multiplier=-1))
        done("pool", pool.affine_select(out=mask_q[:], in_=mask_q[:], compare_op=ALU.is_ge, fill=MASKED,
                                        base=0, pattern=[[-1, P]], channel_multiplier=1))
        done("pool", pool.affine_select(out=mask_k[:], in_=mask_k[:], compare_op=ALU.is_ge, fill=MASKED,
                                        base=0, pattern=[[1, P]], channel_multiplier=-1))
        for r in range(2):
            wait("pool", core.last["pool"])
            t_setup = done("pool", pool.memset(pairs2[64 * r:64 * r + 64, r:r + 1], 1.0))
        wait("pe", t_setup)

        def settle(ready, g):
            if callable(ready[g]):
                ready[g] = ready[g]()
            return ready[g]

        def layer_norm(ready):
            tok, root = [], {}
            pipeline([lambda g: root.update({g: group_statistics(g, ready)}), lambda g: tok.extend(group_normed(g, root[g]))])
            return tok

        def pipeline(steps, last=lambda g: None):
            for k in range(NG + len(steps) - 1):
                for j in reversed(range(len(steps))):
                    if 0 <= k - j < NG:
                        steps[j](k - j)
                if 0 <= k - len(steps) + 1:
                    last(k - len(steps) + 1)

        def root_of(g, src, scale, eps, ready):
            s = slice(GT * g, GT * g + GT)
            wait("dve", ready)
            t = done("dve", dve.tensor_scalar(rstd[:, s], src, scale, eps, ALU.mult, ALU.add))
            wait("act", t)
            return done("act", act.activation(rstd[:, s], rstd[:, s], ACT.Sqrt))

        def group_statistics(g, x_ready):
            wait("dve", settle(x_ready, g))
            tiles = range(GT * g, GT * g + GT)
            for n in tiles:
                t = done("dve", dve.bn_stats(stats[:, n, :], X[:, n, :]))
            wait("dve", t)
            for n in tiles:
                t = done("dve", dve.bn_aggr(meanvar[:, n, :], stats[:, n, :]))
            return root_of(g, meanvar[:, GT * g:GT * g + GT, 1], 1.0, EPS_LN, t)

        def invert_root(g, ready):
            s = slice(GT * g, GT * g + GT)
            wait("dve", ready)
            wait("dve", done("dve", dve.reciprocal(rstd[:, s], rstd[:, s])))

        def group_normed(g, root):
            invert_root(g, root)
            return [done("dve", dve.tensor_scalar(Y[:, n, :], X[:, n, :], meanvar[:, n, 0:1], rstd[:, n:n + 1],
                                                  ALU.subtract, ALU.mult)) for n in range(GT * g, GT * g + GT)]

        def rsqrt(src, dst, scale, eps, ready):
            wait("dve", ready)
            t = done("dve", dve.tensor_scalar(dst, src, scale, eps, ALU.mult, ALU.add))
            wait("act", t)
            t = done("act", act.activation(dst, dst, ACT.Sqrt))
            wait("dve", t)
            return done("dve", dve.reciprocal(dst, dst))

        def feature_major(src, ready, scale_col=None, banks=(6, 7), then=lambda g, t: None):
            tok = []
            for g in range(NG):
                b = banks[g % 2]
                wait("pe", *bank_free[b])
                for i in range(GT):
                    wait("pe", ready[GT * g + i])
                    mm = pe.transpose(psum[:, b, i * P:(i + 1) * P], src[:, GT * g + i, :], ident[:])
                t = done("pe", mm)
                if g:
                    then(g - 1, tok[g - 1])
                dst = YT[:, g * GW:(g + 1) * GW]
                wait("act", t)
                t = done("act", act.activation(dst, psum[:, b, :], ACT.Copy) if scale_col is None
                         else act.activation(dst, psum[:, b, :], ACT.Identity, scale=scale_col))
                bank_free[b] = [t]
                tok.append(t)
            then(NG - 1, tok[NG - 1])
            return tok

        def gate_logits(n_exp, gate):
            def of_group(g, yt_ready):
                wait("pe", yt_ready, const_in if n_exp == NE1 else moe0_in, *bank_free[5])
                for i in range(GT * g, GT * g + GT):
                    mm = pe.matmul(psum[:, 5, i * n_exp:(i + 1) * n_exp], YT[:, i * P:(i + 1) * P], gate[:],
                                   start=True, stop=True)
                t_gate[0] = done("pe", mm)
            return of_group

        t_gate = [None]

        def moe(n_exp, gate_b, order, w1, load_bias, w2, weights_in, rows, rows_ready,
                scale_col=None, beside=()):
            beside = list(beside)
            n_tiles = NT + n_exp - 1
            stage = core.stage_name
            wait("sp", *core.last.values())
            t_no_token = dma("sp", "no_token", numbers_view, no_token)
            log = small[:, 0, 0:NT * n_exp].rearrange("p (i e) -> p i e", e=n_exp)
            eq = small[:, 1, 0:NT * n_exp].rearrange("p (i e) -> p i e", e=n_exp)
            hot = small[:, 2, 0:NT * n_exp].rearrange("p (i e) -> p i e", e=n_exp)
            best = small[:, 3, 0:NT]
            best2 = small[:, 4, 0:NT]
            t = t_gate[0]
            b1, b2, t_bias = load_bias(t)
            wait("dve", t, weights_in)
            t = done("dve", dve.tensor_tensor(log, psum[:, 5, 0:NT * n_exp].rearrange("p (i e) -> p i e", e=n_exp),
                                              gate_b[:].unsqueeze(1).broadcast_to([P, NT, n_exp]), ALU.add))
            bank_free[5] = [t]
            wait("dve", t)
            t = done("dve", dve.tensor_reduce(best, log, AX.X, ALU.max))
            wait("dve", t)
            t = done("dve", dve.tensor_tensor(eq, log, bcast(best, n_exp), ALU.is_ge))
            wait("dve", t)
            t = done("dve", dve.tensor_tensor(eq, eq, order[:].unsqueeze(1).broadcast_to([P, NT, n_exp]), ALU.mult))
            wait("dve", t)
            t = done("dve", dve.tensor_reduce(best2, eq, AX.X, ALU.max))
            wait("dve", t)
            t_hot = done("dve", dve.tensor_tensor(hot, eq, bcast(best2, n_exp), ALU.is_equal))

            NE_T = NT * n_exp
            wait("pe", t_hot, *bank_free[6], *bank_free[7])
            flat_hot = small[:, 2, 0:NE_T]
            t_tot = done("pe", pe.matmul(psum[:, 6, 0:NE_T], ones[:], flat_hot, start=True, stop=True))
            t_above = done("pe", pe.matmul(psum[:, 7, 0:NE_T], above[:], flat_hot, start=True, stop=True))
            tot = small[:, 0, 0:NE_T]
            run = small[:, 1, 0:NE_T]
            e_i = lambda v: v.rearrange("p (e i) -> p e i", e=n_exp)
            count, padded, end, start, before = (small[:, 3, 16 * k:16 * k + n_exp] for k in range(5))
            wait("dve", t_tot)
            t = done("dve", dve.tensor_copy(e_i(tot), psum[:, 6, 0:NE_T].rearrange("p (i e) -> p e i", e=n_exp)))
            bank_free[6] = [t]
            wait("dve", t)
            t1 = done("dve", dve.tensor_tensor_scan(run, ones[:, 0:NE_T], tot, 0.0, ALU.mult, ALU.add))
            t2 = done("dve", dve.tensor_reduce(count, e_i(tot), AX.X, ALU.add))
            wait("dve", t2)
            below = small[:, 5, 0:NE_T].rearrange("p (e s) -> p e s", e=n_exp)
            t = done("dve", dve.tensor_tensor(below, bcast(count, NT), tile_start[:, 0:NT].unsqueeze(1).broadcast_to([P, n_exp, NT]),
                                              ALU.is_gt))
            wait("dve", t)
            t = done("dve", dve.tensor_reduce(padded, below, AX.X, ALU.add))
            wait("dve", t)
            t = done("dve", dve.tensor_scalar(padded, padded, float(P), None, ALU.mult))
            wait("dve", t)
            t = done("dve", dve.tensor_tensor_scan(end, ones[:, 0:n_exp], padded, 0.0, ALU.mult, ALU.add))
            wait("dve", t, t1)
            done("dve", dve.tensor_tensor(start, end, padded, ALU.subtract))
            t = done("dve", dve.tensor_tensor(before, e_i(run)[:, :, NT - 1], count, ALU.subtract))
            wait("dve", t)
            t = done("dve", dve.tensor_tensor(start, start, before, ALU.subtract))
            t1 = done("dve", dve.tensor_tensor(run, run, tot, ALU.subtract))
            wait("dve", t, t1)
            t = done("dve", dve.tensor_tensor(e_i(run), e_i(run), bcast(start, NT), ALU.add))
            wait("dve", t, t_above)
            i_e = e_i(run).rearrange("p e i -> p i e")
            place = tot.rearrange("p (i e) -> p i e", e=n_exp)
            t = done("dve", dve.tensor_tensor(place, psum[:, 7, 0:NE_T].rearrange("p (i e) -> p i e", e=n_exp), i_e, ALU.add))
            bank_free[7] = [t]
            wait("dve", t)
            t = done("dve", dve.tensor_tensor(place, place, hot, ALU.mult))
            wait("dve", t)
            t = done("dve", dve.tensor_reduce(best2, place, AX.X, ALU.add))
            wait("dve", t)
            t_slot = done("dve", dve.tensor_copy(slot[:], best2))
            wait("dve", t_slot)
            low, high = number_place[:, 0, :], number_place[:, 1, :]
            done("dve", dve.tensor_scalar(low, slot[:], P - 1, None, ALU.bitwise_and))
            t = done("dve", dve.tensor_scalar(high, slot[:], P.bit_length() - 1, None, ALU.logical_shift_right))
            wait("dve", t)
            t_place = done("dve", dve.scalar_tensor_tensor(out=low, in0=low, scalar=float(NT + NE0 - 1), in1=high,
                                                           op0=ALU.mult, op1=ALU.add))
            reached = small[:, 7, 0:n_tiles * (n_exp - 1)].rearrange("p (s e) -> p s e", e=n_exp - 1) \
                if n_tiles * (n_exp - 1) <= P else hidden_flat[:, 0:n_tiles * (n_exp - 1)].rearrange("p (s e) -> p s e", e=n_exp - 1)
            t = done("dve", dve.tensor_tensor(reached, bcast(tile_start[:, 0:n_tiles], n_exp - 1),
                                              end[:, 0:n_exp - 1].unsqueeze(1).broadcast_to([P, n_tiles, n_exp - 1]), ALU.is_ge))
            wait("dve", t)
            t = done("dve", dve.tensor_reduce(small[:, 4, 32:32 + n_tiles], reached, AX.X, ALU.add))
            wait("dve", t)
            t_exp = done("dve", dve.tensor_copy(tile_expert[:, 0:n_tiles], small[:, 4, 32:32 + n_tiles]))

            wait("pool", t_slot, t_sorted0, t_exp)
            for i in range(NT):
                wait("pool", rows_ready[i])
                t_scat = dma_indirect("rows_out", sorted_rows, bass.IndirectOffsetOnAxis(slot[:, i:i + 1], 0), rows[:, i, :], None)
            wait("pool", t_no_token, t_place)
            for i in range(NT):
                t_rows = dma_indirect("numbers_out", slot_row, bass.IndirectOffsetOnAxis(number_place[:, 0, i:i + 1], 0),
                                      token_number[:, i:i + 1], None)
            more = hidden_flat[:, 0:(n_tiles - NT) * D].rearrange("p (s d) -> p s d", d=D)
            x_tile = lambda s: ACC[:, s, :] if s < NT else more[:, s - NT, :]
            xt = [hidden_flat[:, 1024 + GW * k:1024 + GW * k + GW] for k in range(2)]
            pre = [hidden_flat[:, 2048 + GW * k:2048 + GW * k + GW] for k in range(2)]
            hid = [small[:, 4 * k:4 * k + 4, :] for k in range(2)]
            made = [hidden_flat[:, 3072 + GW * k:3072 + GW * k + GW].rearrange("p (s d) -> p s d", d=D) for k in range(2)]
            sorted_view = sorted_rows.rearrange("(s p) d -> p s d", p=P)
            made_view = made_rows[0:T, :].rearrange("(s p) d -> p s d", p=P)
            x_in_ = []
            wait("sp", t_scat, t_exp)
            n_chunks = -(-n_tiles // GT)
            for q in range(n_chunks):
                lo, hi = GT * q, min(GT * q + GT, n_tiles)
                dst = ACC[:, lo:hi, :] if hi <= NT else more[:, lo - NT:hi - NT, :]
                x_in_.append(dma("sp", f"{stage}_x{q}", dst, sorted_view[:, lo:hi, :]))
            wait("sp", t_rows)
            t_back = dma("sp", "numbers_back", row_of_slot[:], numbers_view)
            flat1 = w1.rearrange("p e h -> p (e h)")
            flat2 = w2.rearrange("p e c d -> p (e c d)")
            state = {}

            def turn_rows(q):
                lo, hi = GT * q, min(GT * q + GT, n_tiles)
                wait("pe", x_in_[q], *bank_free[6])
                for s in range(lo, hi):
                    mm = pe.transpose(psum[:, 6, (s - lo) * P:(s - lo + 1) * P], x_tile(s), ident[:])
                t = done("pe", mm)
                wait("act", t, state.get(("layer1", GT * (q - 1) - 1)))
                dst, src = xt[q % 2][:, 0:(hi - lo) * P], psum[:, 6, 0:(hi - lo) * P]
                t = done("act", act.activation(dst, src, ACT.Copy) if scale_col is None
                         else act.activation(dst, src, ACT.Identity, scale=scale_col))
                bank_free[6] = [t]
                state[("xt", q)] = t

            def layer1(s):
                if s % GT == 0:
                    turn_rows(s // GT)
                q, k, b = s // GT, s % GT, s % 2
                wait("pe", state[("xt", q)], t_exp, *bank_free[b])
                e = pe.value_load(tile_expert[0:1, s:s + 1], min_val=0, max_val=n_exp - 1)
                state[("pe_e", s)] = e
                t = done("pe", pe.matmul(psum[:, b, :], xt[q % 2][:, k * P:(k + 1) * P], flat1[:, bass.ds(e * HID, HID)],
                                         start=True, stop=True))
                state[("layer1", s)] = t
                wait("dve", t, t_bias, state.get(("turned", s - 2)))
                e = dve.value_load(tile_expert[0:1, s:s + 1], min_val=0, max_val=n_exp - 1)
                state[("dve_e", s)] = e
                t = done("dve", dve.tensor_tensor(pre[s % 2], psum[:, b, :], b1[:, bass.ds(e * HID, HID)], ALU.add))
                bank_free[b] = [t]
                state[("pre", s)] = t

            def turn_hidden(s):
                b = 2 + s % 2
                wait("pe", state[("pre", s)], *bank_free[b])
                for c in range(HC):
                    mm = pe.transpose(psum[:, b, c * P:(c + 1) * P], pre[s % 2][:, c * P:(c + 1) * P], ident[:])
                t = done("pe", mm)
                state[("turned", s)] = t
                wait("act", t, state.get(("layer2", s - 2)), t_scat)
                t = done("act", act.activation(hid[s % 2], psum[:, b, :].rearrange("p (c t) -> p c t", c=HC), ACT.Relu))
                bank_free[b] = [t]
                state[("hid", s)] = t

            def layer2(s):
                b, q, e = 4 + s % 2, s // GT, state[("pe_e", s)]
                wait("pe", state[("hid", s)], *bank_free[b])
                for c in range(HC):
                    mm = pe.matmul(psum[:, b, 0:D], hid[s % 2][:, c, :], flat2[:, bass.ds(e * HID + c * P, D)],
                                   start=(c == 0), stop=(c == HC - 1))
                t = done("pe", mm)
                state[("layer2", s)] = t
                wait("dve", t, state.get(("made", q - 2)))
                t = done("dve", dve.tensor_tensor(made[q % 2][:, s % GT, :], psum[:, b, 0:D],
                                                  b2[:, bass.ds(state[("dve_e", s)] * D, D)], ALU.add))
                bank_free[b] = [t]
                wait("pool", t, t_back)
                state[("made", q)] = dma_indirect(f"rows_made{q % 2}", made_rows,
                                                  bass.IndirectOffsetOnAxis(row_of_slot[:, s:s + 1], 0),
                                                  made[q % 2][:, s % GT, :], None)

            for s in range(n_tiles + 2):
                if s < n_tiles:
                    layer1(s)
                if 0 <= s - 1 < n_tiles:
                    turn_hidden(s - 1)
                if 0 <= s - 2:
                    layer2(s - 2)
                if beside:
                    beside.pop(0)()
            for piece in beside:
                piece()
            for e in ("sp", "act", "dve", "pe", "pool"):
                wait(e, state[("made", n_chunks - 1)], state[("made", n_chunks - 2)])
            wait("sp", state[("turned", n_tiles - 1)], state[("xt", n_chunks - 1)])
            return [dma("sp", f"ld_made{g}", ACC[:, GT * g:GT * g + GT, :], made_view[:, GT * g:GT * g + GT, :])
                    for g in range(NG)]

        def add_half(ready):
            def piece(g):
                wait("dve", ready[g], core.last["dve"])
                s = slice(GT * g, GT * g + GT)
                return done("dve", dve.scalar_tensor_tensor(out=X[:, s, :], in0=ACC[:, s, :], scalar=0.5,
                                                            in1=X[:, s, :], op0=ALU.mult, op1=ALU.add))
            return [lambda g=g: piece(g) for g in range(NG)]

        def macaron_ffn(name, x_ready):
            core.stage(name)
            y = layer_norm(x_ready)
            b1, b2 = take(0, NE0 * HID), take(NE0 * HID, NE0 * D)
            dma("act", "ld_bias", b1, on_all(ins["L0_ffn_b1"], 0, NE0 * HID))
            t_bias = dma("act", "ld_bias", b2, on_all(ins["L0_ffn_b2"], 0, NE0 * D))
            feature_major(Y, y, then=gate_logits(NE0, gate0))
            back = moe(NE0, gateb0, order0, w1_0, lambda _: (b1, b2, t_bias), w2_0, moe0_in, Y, y)
            barrier()
            return add_half(back)

        def split3(src, dst, rest, is_query, ready, free, copier="act"):
            def slot(k):
                return dst[:, :, k * HD:(k + 1) * HD]

            where = ((0, 1, 2), (3, 4), (5,)) if is_query else ((0, 3, 5), (1, 4), (2,))
            wait("dve", ready, *free)
            wait(copier, *free)
            part = src
            toks = []
            for k in range(3):
                t = done("dve", dve.tensor_copy(slot(where[k][0]), part))
                for other in where[k][1:]:
                    wait(copier, t)
                    toks.append(done(copier, act.activation(slot(other), slot(where[k][0]), ACT.Copy) if copier == "act"
                                     else pool.tensor_copy(slot(other), slot(where[k][0]))))
                if k < 2:
                    wait("dve", t)
                    t = done("dve", dve.tensor_tensor(rest, part, slot(where[k][0]), ALU.subtract))
                    wait("dve", t)
                    part = rest
            return [t, toks[-1]]

        def to_rows(src, n_tiles, dst_of, ready, banks, engine_of):
            toks = []
            for i in range(n_tiles):
                b = banks[i % len(banks)]
                half = psum[:, b, :].bitcast(BF16).rearrange("p (a t) -> p a t", a=8)
                wait("pe", *ready, *bank_free[b])
                for a in range(8):
                    mm = pe.transpose(half[:, a, :], src[:, i, a * P:(a + 1) * P], identb[:])
                t = t_read = done("pe", mm)
                e = engine_of(i)
                wait(e, t)
                t = done(e, act.activation(dst_of(i), half, ACT.Copy) if e == "act" else dve.tensor_copy(dst_of(i), half))
                bank_free[b] = [t]
                toks.append(t)
            return toks, [t_read]

        def windowed_attention(name, x_ready):
            core.stage(name)
            SC = INV_SQRT_HD
            K = 256
            keys = take(0, 8 * (T + W) // 2, BF16).rearrange("p (a t) -> p a t", a=8)
            queries = take(33 * K, 8 * T // 2, BF16).rearrange("p (a t) -> p a t", a=8)
            split_q = take(65 * K, GT * NH * SLOT // 2, BF16).rearrange("p (n s) -> p n s", s=SLOT)
            split_k = take(73 * K, GT * NH * SLOT // 2, BF16).rearrange("p (n s) -> p n s", s=SLOT)
            v_own = take(81 * K, NT * D).rearrange("p (i d) -> p i d", i=NT)
            v_prev = take(89 * K, NT * D).rearrange("p (i d) -> p i d", i=NT)
            raws = [take(k * K, 2 * GT * D).rearrange("p (k i d) -> p k i d", k=2, i=GT) for k in (97, 89)]
            sq = take(101 * K, 2 * GT * D).rearrange("p (k i d) -> p k i d", k=2, i=GT)
            rest = take(105 * K, GT * D).rearrange("p (n d) -> p n d", d=HD)
            bqkv = take(107 * K, 3 * D)
            wait("sp", *core.last.values())
            for n, b in enumerate(("L0_attn_bq", "L0_attn_bk", "L0_attn_bv")):
                t_b = dma("sp", name + "_bias", bqkv[:, n * D:(n + 1) * D], on_all(ins[b], 0, D))
            wait("pool", const_in)
            wait("act", const_in)
            wait("pe", const_in)
            t_pad = done("pool", pool.memset(keys[:, :, 0:W], 0.0))
            done("pool", pool.memset(split_q[:, :, 48:64], 0.0))
            t_pad = done("pool", pool.memset(split_k[:, :, 48:64], 0.0))
            r_norm = small[:, 0, 0:2 * GT * NH]
            q_tok, k_tok, v_tok, yt_ready, tok = [], [], [], [], {}
            free_q, free_k = [], []

            def statistics(g):
                tok["var", g] = group_statistics(g, x_ready)

            def normed(g):
                b = 6 + g % 2
                t = group_normed(g, tok["var", g])
                wait("pe", t[-1], *bank_free[b])
                for i in range(GT):
                    mm = pe.transpose(psum[:, b, i * P:(i + 1) * P], Y[:, GT * g + i, :], ident[:])
                wait("act", done("pe", mm))
                t = done("act", act.activation(YT[:, g * GW:(g + 1) * GW], psum[:, b, :], ACT.Copy))
                bank_free[b] = [t]
                yt_ready.append(t)

            def project(g):
                raw = raws[g % 2]
                wait("dve", t_b, const_in, tok.get(("split", g - 2)))
                for i in range(GT):
                    n, b = GT * g + i, i
                    wait("pe", yt_ready[g], *bank_free[b])
                    t = done("pe", pe.matmul(psum[:, b, 0:3 * D], YT[:, n * P:(n + 1) * P], wqkv[:], start=True, stop=True))
                    wait("dve", t)
                    t_raw = done("dve", dve.tensor_tensor(raw[:, :, i, :], psum[:, b, 0:2 * D].rearrange("p (k d) -> p k d", k=2),
                                                          bqkv[:, 0:2 * D].rearrange("p (k d) -> p k d", k=2), ALU.add))
                    t_v = done("dve", dve.tensor_tensor(v_own[:, n, :], psum[:, b, 2 * D:3 * D], bqkv[:, 2 * D:3 * D], ALU.add))
                    bank_free[b] = [t_v]
                v_tok.append(t_v)
                wait("act", t_raw, tok.get(("sums", g - 1)))
                tok["squares", g] = done("act", act.activation(sq.rearrange("p k i d -> p (k i d)"),
                                                               raw.rearrange("p k i d -> p (k i d)"), ACT.Square))

            def head_sums(g):
                wait("dve", tok["squares", g])
                t = done("dve", dve.tensor_reduce(r_norm, sq.rearrange("p k i (h e) -> p (k i h) e", e=HD), AX.X, ALU.add))
                tok["sums", g] = t
                wait("dve", t)
                t = done("dve", dve.tensor_scalar(r_norm, r_norm, 1.0 / HD, EPS_F32, ALU.mult, ALU.add))
                wait("act", t)
                tok["root", g] = done("act", act.activation(r_norm, r_norm, ACT.Sqrt))

            def head_normed(g):
                raw = raws[g % 2]
                flat = raw.rearrange("p k i (h e) -> p (k i h) e", e=HD)
                wait("dve", tok["root", g])
                t = done("dve", dve.reciprocal(r_norm, r_norm))
                wait("dve", t)
                t = done("dve", dve.tensor_tensor(flat, flat, bcast(r_norm, HD), ALU.mult))
                tok["scaled", g] = t
                for k, e in ((0, "dve"), (1, "pool")):
                    rows = raw[:, k, :, :].rearrange("p i (h e) -> p (i h) e", e=HD)
                    wait(e, t)
                    tok["weighed", g, k] = done(e, (dve if e == "dve" else pool).tensor_tensor(
                        rows, rows, qk_w[:, k, :].unsqueeze(1).broadcast_to([P, GT * NH, HD]), ALU.mult))

            def split(g):
                raw = raws[g % 2]
                t_q = split3(raw[:, 0].rearrange("p i (h e) -> p (i h) e", e=HD), split_q, rest, True, tok["weighed", g, 0],
                             free_q + [t_pad])
                wait("dve", tok["weighed", g, 1])
                t_k = split3(raw[:, 1].rearrange("p i (h e) -> p (i h) e", e=HD), split_k, rest, False, t_q[0], free_k)
                tok["split", g] = t_k[0]
                tok["split_q", g], tok["split_k", g] = t_q, t_k

            def turned(g):
                nonlocal free_q, free_k
                base = g * GW
                tq, free_q = to_rows(split_q.rearrange("p (i h) s -> p i (h s)", i=GT), GT,
                                     lambda i: queries[:, :, base + i * P:base + (i + 1) * P], tok["split_q", g], (4, 5),
                                     lambda i: "act")
                tk, free_k = to_rows(split_k.rearrange("p (i h) s -> p i (h s)", i=GT), GT,
                                     lambda i: keys[:, :, W + base + i * P:W + base + (i + 1) * P], tok["split_k", g], (4, 5),
                                     lambda i: "act")
                q_tok.append(tq)
                k_tok.append(tk)

            pipeline([statistics, normed, project, head_sums, lambda g: (head_normed(g), split(g))], turned)
            wait("sp", *v_tok, tok["split", NG - 1])
            wait("pool", core.last["pool"], tok["split", NG - 1])
            t_pad = done("pool", pool.memset(v_prev[0:W, 0:1, :], 0.0))
            wait("pool", t_pad)
            dma("sp", name + "_shift", v_prev[W:P, :, :], v_own[0:P - W, :, :])
            t_vp = dma("sp", name + "_shift", v_prev[0:W, 1:NT, :], v_own[P - W:P, 0:NT - 1, :])
            barrier()

            score = [take((65 + 4 * i) * K, NH * 2 * W).rearrange("p (h w) -> p h w", h=NH) for i in range(3)]
            prob = [YT[:, i * NH * 2 * W:(i + 1) * NH * 2 * W].rearrange("p (h w) -> p h w", h=NH) for i in range(2)]
            prob_t = [take((97 + 4 * i) * K, NH * 2 * W).rearrange("p (h w) -> p h w", h=NH) for i in range(2)]
            per_row = lambda k: take((104 + k) * K, NT * NH).rearrange("p (i h) -> p i h", i=NT)
            mx, ln_, rl, th = per_row(1), per_row(2), per_row(3), per_row(4)
            exp_tok, pt_tok, tanh_tok = {}, {}, {}
            score_free, prob_free, pt_free = {}, {}, {}
            u_tok, th_tok = [], []

            def scores(n):
                sc, b = score[n % 3], 2 * (n % 2)
                wait("pe", *bank_free[b])
                for h in range(NH):
                    r = SLOT * (h % 2)
                    for j in range(4):
                        t0 = n * P + j * W
                        mm = pe.matmul(psum[W * j:W * j + W, b + h % 2, (h // 2) * 2 * W:(h // 2 + 1) * 2 * W],
                                       queries[r:r + SLOT, h // 2, t0:t0 + W], keys[r:r + SLOT, h // 2, t0:t0 + 2 * W],
                                       start=True, stop=True)
                t = done("pe", mm)
                wait("dve", t, *score_free.get(n - 3, []))
                both = psum[:, b:b + 2, :].rearrange("p k (h w) -> p (k h) w", w=2 * W)
                t = done("dve", dve.tensor_tensor(sc, both, window_mask[:, min(n, 1), :].unsqueeze(1).broadcast_to([P, NH, 2 * W]), ALU.add))
                bank_free[b] = [t]
                wait("dve", t)
                t = done("dve", dve.tensor_reduce(mx[:, n, :], sc, AX.X, ALU.max))
                wait("dve", t)
                t = done("dve", dve.tensor_tensor(sc, sc, bcast(mx[:, n, :], 2 * W), ALU.subtract))
                wait("act", t)
                exp_tok[n] = done("act", act.activation(sc, sc, ACT.Exp, scale=SC))

            def normalised(n):
                sc, pt, pr = score[n % 3], prob_t[n % 2], prob[n % 2]
                wait("dve", exp_tok[n])
                t = done("dve", dve.tensor_reduce(ln_[:, n, :], sc, AX.X, ALU.add))
                wait("dve", t)
                t = done("dve", dve.reciprocal(rl[:, n, :], ln_[:, n, :]))
                wait("dve", *pt_free.get(n - 2, []))
                pt_tok[n] = done("dve", dve.transpose(pt.rearrange("p h w -> p (h w)"), sc.rearrange("p h w -> p (h w)")))
                wait("pool", t, *prob_free.get(n - 2, []))
                t_p = done("pool", pool.tensor_tensor(pr, sc, bcast(rl[:, n, :], 2 * W), ALU.mult))
                score_free[n] = [t_p, pt_tok[n]]
                wait("act", t_p)
                tanh_tok[n] = done("act", act.activation(pr, pr, ACT.Tanh, scale=0.5))

            def weighted_values(n):
                pt, ob = prob_t[n % 2], 4 + n % 2
                wait("pe", pt_tok[n], t_vp, t_pad, *bank_free[ob])
                for h in range(NH):
                    s = (h % 2) * 8 + h // 2
                    for k, vals in enumerate((v_prev, v_own)):
                        for j in range(4):
                            q = slice(W * j, W * j + W)
                            mm = pe.matmul(psum[q, ob, h * HD:(h + 1) * HD], pt[q, s, k * W:(k + 1) * W],
                                           vals[q, n, h * HD:(h + 1) * HD], start=(k == 0), stop=(k == 1),
                                           skip_group_check=True)
                t = done("pe", mm)
                pt_free[n] = [t]
                wait("act", t)
                t = done("act", act.activation(ACC[:, n, :], psum[:, ob, 0:D], ACT.Copy))
                bank_free[ob] = [t]
                u_tok.append(t)

            def tanh_sum(n):
                wait("dve", tanh_tok[n])
                t = done("dve", dve.tensor_reduce(th[:, n, :], prob[n % 2], AX.X, ALU.add))
                prob_free[n] = [t]
                th_tok.append(t)

            for n in range(NT + 3):
                if n < NT:
                    scores(n)
                if n >= 3:
                    tanh_sum(n - 3)
                if 1 <= n <= NT:
                    normalised(n - 1)
                if 2 <= n <= NT + 1:
                    weighted_values(n - 2)
            den, inv, fit, shift = th, per_row(5), per_row(6), per_row(7)
            sums = rstd
            wait("dve", th_tok[-1])
            t = done("dve", dve.tensor_scalar(den, th, 0.5 / T, 1.0, ALU.mult, ALU.add))
            wait("dve", t)
            t = done("dve", dve.reciprocal(inv, den))
            wait("dve", t)
            t = done("dve", dve.tensor_reduce(sums[:, :], inv.rearrange("p i h -> p h i"), AX.X, ALU.add))
            wait("pe", t, *bank_free[6])
            t = done("pe", pe.matmul(psum[:, 6, 0:NH], ones[:], sums[:, :], start=True, stop=True))
            wait("dve", t)
            t = done("dve", dve.tensor_tensor(fit, den, psum[:, 6, 0:NH].unsqueeze(1).broadcast_to([P, NT, NH]), ALU.mult))
            bank_free[6] = [t]
            wait("dve", t)
            t = done("dve", dve.reciprocal(fit, fit))
            wait("act", t)
            t_fit = done("act", act.activation(fit, fit, ACT.Ln))
            wait("dve", t_fit)
            t = done("dve", dve.scalar_tensor_tensor(out=inv, in0=mx, scalar=SC, in1=fit, op0=ALU.mult, op1=ALU.add))
            t2 = done("dve", dve.tensor_scalar(mx, mx, SC, None, ALU.mult))
            wait("dve", t2)
            t = done("dve", dve.tensor_tensor(shift, mx, fit, ALU.add))
            wait("dve", t)
            t = done("dve", dve.tensor_tensor(shift, shift, inv, ALU.subtract))
            wait("act", t)
            t = done("act", act.activation(shift, shift, ACT.Exp))
            wait("dve", t)
            t = done("dve", dve.tensor_tensor(ln_, ln_, shift, ALU.mult))
            wait("dve", t)
            t = done("dve", dve.reciprocal(ln_, ln_))
            wait("dve", t)
            t = done("dve", dve.tensor_tensor(ln_, ln_, shift, ALU.mult))
            tok = []
            wait("dve", t)
            for n in range(NT):
                a = ACC[:, n, :].rearrange("p (a k d) -> p k a d", k=2, d=HD)
                f = ln_[:, n, :].rearrange("p (k a) -> p k a", k=2)
                wait("dve", u_tok[n])
                tok.append(done("dve", dve.tensor_tensor(a, a, bcast(f, HD), ALU.mult)))
            wait("pool", *x_ready)
            t_x = done("pool", pool.tensor_tensor(X[:, :, :], X[:, :, :], bo[:].unsqueeze(1).broadcast_to([P, NT, D]), ALU.add))
            return project_out(tok, wo0, X, [t_x] * NG)

        def project_out(att_ready, w, dst, dst_ready):
            at = feature_major(ACC, att_ready)
            tok = []
            for g in range(NG):
                b = 4 + g % 2
                wait("pe", at[g], *bank_free[b])
                for i in range(GT):
                    n = GT * g + i
                    mm = pe.matmul(psum[:, b, i * P:(i + 1) * P], YT[:, n * P:(n + 1) * P], w[:], start=True, stop=True)
                t = done("pe", mm)
                wait("dve", t, dst_ready[g])
                d = dst[:, GT * g:GT * g + GT, :]
                t = done("dve", dve.tensor_tensor(d, psum[:, b, :].rearrange("p (i d) -> p i d", i=GT), d, ALU.add))
                bank_free[b] = [t]
                tok.append(t)
            barrier()
            return tok

        def latent_block(name, x_ready, during_attention=None, during_moe=None):
            core.stage(name)
            K = 256
            keys = take(0, 8 * T // 2, BF16).rearrange("p (a t) -> p a t", a=8)
            split_q = [take((32 + 8 * i) * K, GT * NH * SLOT // 2, BF16).rearrange("p (n s) -> p n s", s=SLOT) for i in range(2)]
            padded = lambda k: take(k * K, 4 * GW // 2, BF16).rearrange("p (r a t) -> p r a t", r=2, a=2)
            plain_q = [padded(48), padded(52)]
            shift_q = [padded(56), padded(60)]
            N_PROB, LAG, AHEAD, SPARE = 6, 3, 6, 2.5
            prob = [take((64 + 4 * i) * K, 2 * GW).rearrange("p (k t) -> p k t", k=2) for i in range(N_PROB)]
            split_k = take(92 * K, GT * NH * SLOT // 2, BF16).rearrange("p (n s) -> p n s", s=SLOT)
            values = take(100 * K, NT * NH * 9).rearrange("p (i h d) -> p i h d", i=NT, h=NH)
            lat = take(64 * K, NT * KV).rearrange("p (i d) -> p i d", i=NT)
            lat_t = take(68 * K, T)[0:KV, :]
            raw = take(109 * K, GT * D).rearrange("p (n d) -> p n d", d=HD)
            rest = small[:, 0:4, :].rearrange("p a (n d) -> p (a n) d", d=HD)
            turned = small[:, 4:8, :].rearrange("p a (n d) -> p (a n) d", d=HD)

            t = done("pool", pool.memset(split_k[:, :, 48:64], 0.0))
            wait("pool", t)
            done("pool", pool.memset(split_k[:, :, 48:51], 1.0))
            done("pool", pool.memset(split_q[0][:, :, 48:64], 0.0))
            done("pool", pool.memset(split_q[1][:, :, 48:64], 0.0))
            t_pad = done("pool", pool.memset(take(48 * K, 16 * K), 0.0))
            t_sp = done("pool", pool.memset(values[:, :, :, 8:9], 1.0))

            def rotate(g, src, ready):
                view = lambda t: t.rearrange("p (i h) d -> p i h d", i=GT)
                table = lambda k, a, b: rope[:, k, GT * g:GT * g + GT, a:b].unsqueeze(2).broadcast_to([P, GT, NH, b - a])
                half = HD // 2
                s, d, r = view(src), view(turned), view(rest)
                wait("dve", ready)
                done("dve", dve.tensor_tensor(d, s, table(0, 0, HD), ALU.mult))
                done("dve", dve.tensor_tensor(r[:, :, :, 0:half], s[:, :, :, half:HD], table(1, 0, half), ALU.mult))
                t = done("dve", dve.tensor_tensor(r[:, :, :, half:HD], s[:, :, :, 0:half], table(1, half, HD), ALU.mult))
                wait("dve", t)
                t = done("dve", dve.tensor_tensor(turned, turned, rest, ALU.add))
                return t

            y_ready, h_ready, ht, tok = [], [], [], {}
            k_tok, v_tok, free_raw, free_k = [], [], [], []
            tiles = lambda g: range(GT * g, GT * g + GT)

            def statistics(g):
                tok["var", g] = group_statistics(g, x_ready)

            def normed(g):
                y_ready.extend(group_normed(g, tok["var", g]))
                for n in tiles(g):
                    wait("act", y_ready[GT * g + GT - 1])
                    tok["squares", g] = done("act", act.activation(ACC[:, n, :], Y[:, n, :], ACT.Square,
                                                                   accum_out=rstd[:, n:n + 1]))

            def mean_square(g):
                tok["ms", g] = root_of(g, rstd[:, GT * g:GT * g + GT], 1.0 / D, EPS_RMS, tok["squares", g])

            def rms_normed(g):
                invert_root(g, tok["ms", g])
                b = 6 + g % 2
                wait("pe", *bank_free[b])
                for i, n in enumerate(tiles(g)):
                    h_ready.append(done("dve", dve.tensor_scalar(ACC[:, n, :], Y[:, n, :], rstd[:, n:n + 1], None, ALU.mult)))
                    wait("pe", h_ready[n])
                    mm = pe.transpose(psum[:, b, i * P:(i + 1) * P], ACC[:, n, :], ident[:])
                wait("act", done("pe", mm))
                t = done("act", act.activation(YT[:, g * GW:(g + 1) * GW], psum[:, b, :], ACT.Identity, scale=norm_w[:, 0:1]))
                bank_free[b] = [t]
                ht.append(t)

            def latent(g):
                b = 4 + g % 2
                wait("pe", ht[g], *bank_free[b])
                for i, n in enumerate(tiles(g)):
                    mm = pe.matmul(psum[:, b, i * KV:(i + 1) * KV], YT[:, n * P:(n + 1) * P], wqd[:, D:D + KV],
                                   start=True, stop=True)
                wait("act", done("pe", mm))
                s = slice(GT * g, GT * g + GT)
                t = done("act", act.activation(lat[:, s, :], psum[:, b, 0:GT * KV].rearrange("p (i d) -> p i d", i=GT), ACT.Copy))
                bank_free[b] = [t]
                wait("dve", t)
                for n in tiles(g):
                    t = done("dve", dve.bn_stats(stats[:, n, :], lat[:, n, :]))
                wait("dve", t)
                for n in tiles(g):
                    t = done("dve", dve.bn_aggr(meanvar[:, n, :], stats[:, n, :]))
                tok["lat", g] = root_of(g, meanvar[:, s, 1], 1.0, EPS_LN, t)

            def latent_normed(g):
                invert_root(g, tok["lat", g])
                b = 4 + g % 2
                wait("pe", *bank_free[b])
                for i, n in enumerate(tiles(g)):
                    t = done("dve", dve.tensor_scalar(lat[:, n, :], lat[:, n, :], meanvar[:, n, 0:1], rstd[:, n:n + 1],
                                                      ALU.subtract, ALU.mult))
                    wait("pe", t)
                    mm = pe.transpose(psum[0:KV, b, i * P:(i + 1) * P], lat[:, n, :], ident[:])
                wait("act", done("pe", mm))
                t = done("act", act.activation(lat_t[:, g * GW:(g + 1) * GW], psum[0:KV, b, :], ACT.Identity,
                                               bias=ln_gb[:, 1:2], scale=ln_gb[:, 0:1]))
                bank_free[b] = [t]
                tok["lat_t", g] = t

            def keys_of(g):
                for i, n in enumerate(tiles(g)):
                    b = i
                    wait("pe", tok["lat_t", g], *bank_free[b])
                    t = done("pe", pe.matmul(psum[:, b, 0:2 * D], lat_t[:, n * P:(n + 1) * P], wukv[:], start=True, stop=True))
                    e = ("act", "dve")[i % 2]
                    copy = (lambda out_, in_: act.activation(out_, in_, ACT.Copy)) if e == "act" else dve.tensor_copy
                    wait(e, t, t_sp, *free_raw)
                    done(e, copy(raw[:, i * NH:(i + 1) * NH, :], psum[:, b, 0:D].rearrange("p (h d) -> p h d", h=NH)))
                    t_v = done(e, copy(values[:, n, :, 0:HD], psum[:, b, D:2 * D].rearrange("p (h d) -> p h d", h=NH)))
                    bank_free[b] = [t_v]
                    v_tok.append(t_v)

            def keys_rotated(g):
                nonlocal free_raw
                wait("dve", v_tok[GT * g + GT - 2], *tok.get(("split", g - 1), []))
                tok["rotated", g] = rotate(g, raw, v_tok[GT * g + GT - 1])
                free_raw = [tok["rotated", g]]

            def keys_split(g):
                tok["split", g] = split3(turned, split_k, rest, False, tok["rotated", g], free_k)

            def keys_turned(g):
                nonlocal free_k
                ready, free_k = to_rows(split_k.rearrange("p (i h) s -> p i (h s)", i=GT), GT,
                                        lambda i: keys[:, :, g * GW + i * P:g * GW + (i + 1) * P], tok["split", g],
                                        (0, 1, 2, 3), lambda i: "dve" if i % 2 else "act")
                k_tok.append(ready)

            work = [5, 6, 7]
            turn = [0]

            def work_bank():
                turn[0] += 1 if work[(turn[0] + 1) % 3] != state.get("held") else 2
                return work[turn[0] % 3]

            state = {}
            eng_of = {"dve": dve, "pool": pool}

            def prepare_q(g, i, e):
                n, b, v = GT * g + i, work_bank(), eng_of[e]
                s, r, d = (t[:, i * NH:(i + 1) * NH, :] for t in ((raw, rest, turned) if g else early))
                sq = split_q[g % 2][:, i * NH:(i + 1) * NH, :]
                table = lambda k, lo, hi: rope[:, k, n, lo:hi].unsqueeze(1).broadcast_to([P, NH, hi - lo])
                half = HD // 2
                shared = state.get(("raw", i), []) + tok["split", NG - 1] + free_raw if g else []
                wait("pe", ht[g], *bank_free[b])
                t = done("pe", pe.matmul(psum[:, b, 0:D], YT[:, n * P:(n + 1) * P], wqd[:, 0:D], start=True, stop=True))
                wait("act", t, *shared)
                t = done("act", act.activation(s, psum[:, b, 0:D].rearrange("p (h d) -> p h d", h=NH), ACT.Copy))
                bank_free[b] = [t]
                wait(e, t, t_sp, *shared, *state.get(("turned", g - 2), []))
                done(e, v.tensor_tensor(d, s, table(0, 0, HD), ALU.mult))
                done(e, v.tensor_tensor(r[:, :, 0:half], s[:, :, half:HD], table(1, 0, half), ALU.mult))
                t = done(e, v.tensor_tensor(r[:, :, half:HD], s[:, :, 0:half], table(1, half, HD), ALU.mult))
                wait(e, t)
                t = done(e, v.tensor_tensor(d, d, r, ALU.add))
                done(e, v.memset(sq[:, :, 48:51], 0.0))
                part = d
                for lo, copies in ((0, 3), (3, 2), (5, 1)):
                    wait(e, t)
                    dst = sq[:, :, lo * HD:(lo + copies) * HD].rearrange("p h (k d) -> p h k d", k=copies)
                    t = done(e, v.tensor_copy(dst, part.unsqueeze(2).broadcast_to([P, NH, copies, HD])))
                    if lo < 5:
                        wait(e, t)
                        t = done(e, v.tensor_tensor(r, part, sq[:, :, lo * HD:(lo + 1) * HD], ALU.subtract))
                        part = r
                state[("raw", i)] = [t]
                state[("split", g, i)] = t

            early = [take((76 + 2 * k) * K, GT * D).rearrange("p (n d) -> p n d", d=HD) for k in range(3)]
            pipeline([statistics, normed, mean_square, rms_normed, latent, lambda i: prepare_q(0, i, "pool"),
                      latent_normed, keys_of, keys_rotated, keys_split, keys_turned])

            row_max = take(111 * K, 64).rearrange("p (n c) -> p n c", c=4)
            shift = take(111 * K + 64, GT * 4)
            part_ = take(111 * K + 80, GT * 4)
            inv_flat = take(111 * K + 96, GT * 4)

            def turn_queries(g, hq, dst, before, free):
                b = work_bank()
                half = psum[:, b, :].bitcast(BF16).rearrange("p (a t) -> p a t", a=2)
                wait("pe", *before, *bank_free[b])
                for a in range(2):
                    for i in range(GT):
                        pair = split_q[g % 2][:, i * NH + 4 * hq + 2 * a:i * NH + 4 * hq + 2 * a + 2, :]
                        mm = pe.transpose(half[:, a, i * P:(i + 1) * P], pair.rearrange("p h s -> p (h s)"), identb[:])
                t = done("pe", mm)
                for r, e in enumerate(("act", "dve")):
                    wait(e, t, t_pad, *free)
                    rows = slice(SLOT * r, SLOT * r + SLOT)
                    bank_free[b].append(done(e, act.activation(dst[rows, r], half[rows], ACT.Copy) if e == "act"
                                             else dve.tensor_copy(dst[rows, r], half[rows])))
                t2 = bank_free[b] = bank_free[b][-2:]
                return t, t2

            def max_items(g, hq):
                u = 4 * g + hq
                sq, plain = split_q[g % 2], plain_q[u % 2]

                def first():
                    _, state[("plain", u)] = turn_queries(g, hq, plain, [state[("split", g, i)] for i in range(GT)],
                                                          [state.get(("maxed", u - 2))])

                def one(i, hh, c):
                    n, a, r = GT * g + i, hh // 2, hh % 2
                    w = min(GW, (n + 1) * P - c * GW)
                    diag = c == g
                    b = work_bank()
                    wait("pe", *state[("plain", u)], *k_tok[c], *bank_free[b])
                    mm = pe.matmul(psum[:, b, 0:w], plain[:, r, a, i * P:(i + 1) * P],
                                   keys[:, 2 * hq + a, c * GW:c * GW + w], start=True, stop=not diag)
                    if diag:
                        mm = pe.matmul(psum[:, b, w - P:w], identb[:], mask_q[:], start=False, stop=True)
                    t = done("pe", mm)
                    wait("dve", t, state.get("max_free"))
                    t = done("dve", dve.tensor_reduce(row_max[:, i * 4 + hh, c:c + 1], psum[:, b, 0:w], AX.X, ALU.max))
                    bank_free[b] = [t]
                    state[("maxed", u)] = t

                def finish():
                    wait("dve", state[("maxed", u)])
                    t = done("dve", dve.tensor_reduce(shift, row_max[:, :, 0:g + 1], AX.X, ALU.max, negate=True))
                    state["max_free"] = t
                    heads = sq.rearrange("p (i h) s -> p i h s", i=GT)[:, :, 4 * hq:4 * hq + 4, :]
                    src, rem = (v.rearrange("p (i h) -> p i h", i=GT) for v in (shift, part_))
                    wait("dve", *state[("plain", u)])
                    for k in range(3):
                        wait("dve", t)
                        t = done("dve", dve.tensor_copy(heads[:, :, :, 48 + k], src))
                        if k < 2:
                            wait("dve", t)
                            t = done("dve", dve.tensor_tensor(rem, src, heads[:, :, :, 48 + k], ALU.subtract))
                            src = rem
                    state[("chained", u)] = t

                def turn_shifted():
                    t_pe, state[("shift", u)] = turn_queries(g, hq, shift_q[u % 2], [state[("chained", u)]],
                                                             [state.get(("scored", u - 2))])
                    state.setdefault(("turned", g), []).append(t_pe)

                tiles = [lambda i=i, hh=hh, c=c: one(i, hh, c) for i in range(GT) for hh in range(4) for c in range(g + 1)]
                return first, tiles, finish, turn_shifted

            prob_free = [None] * N_PROB
            prob_turn = [0]
            ot = take(88 * K, GW)
            O_BANK = 4
            wait("dve", *bank_free[O_BANK])
            bank_free[O_BANK] = [done("dve", dve.memset(psum[:, O_BANK, :], 0.0))]
            att_tok = {}

            def score(u, j, a):
                g, hq = u // 4, u % 4
                off = P * max(0, j - GT * g)
                for r in range(2):
                    b = 2 * a + r
                    wait("pe", *state[("shift", u)], k_tok[j // GT][j % GT], *bank_free[b])
                    mm = pe.matmul(psum[:, b, off:GW], keys[:, 2 * hq + a, j * P:(j + 1) * P],
                                   shift_q[u % 2][:, r, a, off:GW], start=True, stop=(j < GT * g))
                if j >= GT * g:
                    for r in range(2):
                        mm = pe.matmul(psum[:, 2 * a + r, off:off + P], identb[:], mask_k[:], start=False, stop=True)
                t = done("pe", mm)
                state[("scored", u)] = t
                pr = prob_turn[0] % N_PROB
                prob_turn[0] += 1
                wait("act", t, prob_free[pr])
                t = done("act", act.activation(prob[pr][:, :, off:GW], psum[:, 2 * a:2 * a + 2, off:GW], ACT.Exp,
                                               scale=INV_SQRT_HD))
                bank_free[2 * a] = [t]
                bank_free[2 * a + 1] = [t]
                return pr, off, t

            def weigh(u, j, a, pr, off, t_exp):
                g, hq = u // 4, u % 4
                wait("pe", t_exp, *v_tok)
                if j == 0:
                    wait("pe", *bank_free[O_BANK])
                for r in range(2):
                    hh = 2 * a + r
                    mm = pe.matmul(psum[32 * hh:32 * hh + 9, O_BANK, off:GW], values[:, j, 4 * hq + hh, :],
                                   prob[pr][:, r, off:GW], start=(j == 0), stop=(j == GT * g + GT - 1),
                                   skip_group_check=True)
                t = done("pe", mm)
                prob_free[pr] = t
                state["weighed"] = t

            def take_out():
                wait("act", state["weighed"], state.get("ot_free"))
                state["ot"] = done("act", act.activation(ot, psum[:, O_BANK, :], ACT.Copy))
                bank_free[O_BANK] = [state["ot"]]

            def turn_out():
                b = state["held"] = work_bank()
                wait("pe", state["ot"], *bank_free[b])
                for i in range(GT):
                    mm = pe.transpose(psum[:, b, i * P:(i + 1) * P], ot[:, i * P:(i + 1) * P], ident[:])
                state["ot_free"] = done("pe", mm)

            def normalise(u):
                g, hq, b, t = u // 4, u % 4, state.pop("held"), state["ot_free"]
                back_ = psum[:, b, :].rearrange("p (i h s) -> p i h s", i=GT, h=4)
                inv_sum = inv_flat.rearrange("p (i h) -> p i h", i=GT)
                wait("dve", t, state.get("inv_free"))
                t = done("dve", dve.reciprocal(inv_sum, back_[:, :, :, 8]))
                wait("dve", t)
                dst = ACC[:, GT * g:GT * g + GT, 4 * hq * HD:(4 * hq + 4) * HD].rearrange("p i (h d) -> p i h d", h=4)
                t = done("dve", dve.tensor_tensor(dst, back_[:, :, :, 0:HD], bcast(inv_sum, HD), ALU.mult))
                state["inv_free"] = t
                bank_free[b] = [t]
                att_tok[g] = t

            n_units = 4 * NG
            others = [] if during_attention is None else during_attention(work_bank)
            side, mark = [], []
            parts = [max_items(u // 4, u % 4) for u in range(n_units)]
            for u in range(n_units):
                first, maxima, finish, turn_shifted = parts[u]
                mine = ([first] if u == 0 else []) + maxima[0 if u == 0 else AHEAD:]
                if u + 1 < n_units:
                    g = (u + 1) // 4
                    mine.insert(len(mine) // 2 if g == u // 4 else len(mine) - 4, parts[u + 1][0])
                if u in (0, 5, 9):
                    for i in range(GT):
                        mine.insert(1 + (i + 1) * len(mine) // 6, lambda g=u // 4 + 1, i=i: prepare_q(g, i, "pool"))
                if u in (8, 9, 10, 11, 12):
                    mine_too = others[(u - 8) * len(others) // 5:(u - 7) * len(others) // 5]
                    for k, piece in enumerate(mine_too):
                        mine.insert(1 + k + (k + 1) * (len(mine) - k - 2) // len(mine_too), piece)
                side += mine + [finish] + (parts[u + 1][1][:AHEAD] if u + 1 < n_units else []) + [turn_shifted]
                mark.append(len(side))
            given = 0

            def give(target):
                nonlocal given
                while given < min(target, len(side)):
                    side[given]()
                    given += 1

            give(mark[0])
            later = []
            out_steps = []

            def catch_up(lag, most):
                while len(later) > lag and most:
                    u, j, *_ = later[0]
                    weigh(*later.pop(0))
                    most -= 1
                    if not later or later[0][0] != u:
                        take_out()
                        out_steps.extend([turn_out, lambda u=u: normalise(u)])
                        return

            def outputs_turned(g):
                b = work_bank()
                wait("pe", att_tok[g], *bank_free[b])
                for i in range(GT):
                    mm = pe.transpose(psum[:, b, i * P:(i + 1) * P], ACC[:, GT * g + i, :], ident[:])
                wait("act", done("pe", mm))
                state[("at", g)] = done("act", act.activation(YT[:, g * GW:(g + 1) * GW], psum[:, b, :], ACT.Copy))
                bank_free[b] = [state[("at", g)]]

            def projected(g):
                b = work_bank()
                wait("pe", state[("at", g)], *bank_free[b])
                for i in range(GT):
                    n = GT * g + i
                    mm = pe.matmul(psum[:, b, i * P:(i + 1) * P], YT[:, n * P:(n + 1) * P], wo1[:], start=True, stop=True)
                wait("dve", done("pe", mm))
                d = Y[:, GT * g:GT * g + GT, :]
                t = done("dve", dve.tensor_tensor(d, psum[:, b, :].rearrange("p (i d) -> p i d", i=GT), d, ALU.add))
                bank_free[b] = [t]
                state[("y2", g)] = t

            def squared(g):
                wait("act", state[("y2", g)])
                for n in tiles(g):
                    state["squares"] = done("act", act.activation(ACC[:, n, :], Y[:, n, :], ACT.Square,
                                                                  accum_out=rstd[:, n:n + 1]))

            piece_of = lambda g: [lambda f=f: f(g) for f in (outputs_turned, projected, squared)]
            after = [f for g in range(NG - 1) for f in piece_of(g)]
            for u in range(n_units):
                steps = [(j, a) for j in range(GT * (u // 4) + GT) for a in range(2)]
                begin = given
                span = 1 - SPARE / len(steps)
                for s, (j, a) in enumerate(steps):
                    got = score(u, j, a)
                    later.append((u, j, a, *got))
                    frac = (s + 1) / len(steps)
                    if out_steps:
                        out_steps.pop(0)()
                    if u + 1 < n_units:
                        give(round(begin + (mark[u + 1] - begin) * min(1, frac / span)))
                        if frac > span and u + 2 < n_units:
                            give(round(mark[u + 1] + (mark[u + 2] - mark[u + 1]) * (frac - span)))
                    if u == n_units - 1 and s % 3 == 2 and after:
                        after.pop(0)()
                    if len(out_steps) != 2 or len(later) >= N_PROB - 1:
                        catch_up(LAG, 2)
            catch_up(0, len(later))
            for f in out_steps:
                f()
            for f in after + piece_of(NG - 1):
                f()
            barrier()
            t_r = rsqrt(rstd[:, :], rstd[:, :], 1.0 / D, EPS_RMS, state["squares"])
            wait("dve", t_r)
            h_ready = [done("dve", dve.tensor_scalar(ACC[:, i, :], Y[:, i, :], rstd[:, i:i + 1], None, ALU.mult))
                       for i in range(NT)]
            feature_major(ACC, h_ready, norm_w[:, 1:2], then=gate_logits(NE1, gate1))

            def load_bias(gate_done):
                b2_1 = hidden_flat[:, (NE1 - 1) * D:(2 * NE1 - 1) * D]
                wait("sp", gate_done)
                dma("sp", "ld_bias1", b2_1, on_all(ins["L1_ffn_b2"], 0, NE1 * D))
                return YT[:], b2_1, dma("sp", "ld_bias1", YT[:], on_all(ins["L1_ffn_b1"], 0, NE1 * HID))

            def add_half_y(g):
                s = slice(GT * g, GT * g + GT)
                done("dve", dve.scalar_tensor_tensor(out=X[:, s, :], in0=Y[:, s, :], scalar=0.5, in1=X[:, s, :],
                                                     op0=ALU.mult, op1=ALU.add))

            beside = [] if during_moe is None else during_moe()
            beside[3:3] = [lambda g=g: add_half_y(g) for g in range(NG)]
            back = moe(NE1, gateb1, order1, w1_1, load_bias, w2_1, const_in, ACC, h_ready,
                       scale_col=norm_w[:, 1:2], beside=beside)
            barrier()
            return add_half(back)

        toep = take(0, D * P).rearrange("p (m x) -> p m x", m=D)
        b_in = take(64 * 256, D * NS).rearrange("p (m n) -> p m n", m=D)
        decay = sb("decay", [P, 64])
        taps = nc.dram_tensor("taps", (D, 2 * P), F32).ap()

        def ssm_far_table(work_bank):
            back = take(111 * 256 + 112, P + 1)
            zero = take(90 * 256, P)
            k_rev = take(92 * 256, T).rearrange("p (b x) -> p b x", b=4)
            tok = {}

            def rates():
                wait("sp", *core.last.values())
                t_back = dma("sp", "ld_back", back, ins["back"])
                dma("sp", "ld_dt", logdt_all, on_all(ins["L1_attn_log_dt"], 0, D))
                t_dt[0] = dma("sp", "ld_dt", alog_all, on_all(ins["L1_attn_A_log"], 0, NS))
                wait("act", const_in)
                t1 = done("act", act.activation(logdt_pair[:], logdt_pair[:], ACT.Exp))
                t2 = done("act", act.activation(alog_col[:], alog_col[:], ACT.Exp))
                wait("pool", t1, t2, const_in, *core.last.values())
                t = done("pool", pool.tensor_scalar(logdt_pair[:], logdt_pair[:], alog_col[:, 0:1], -1.0, ALU.mult, ALU.mult))
                done("pool", pool.memset(zero, 0.0))
                wait("act", t, t_back)

            def powers(a):
                for k in range(a, a + 4):
                    tok["exp"] = done("act", act.activation(E_far[:, k, :], back, ACT.Exp, scale=logdt_pair[:, k:k + 1]))

            def times_c(q):
                s = slice(16 * q, 16 * q + 16)
                wait("pool", tok["exp"])
                t = done("pool", pool.tensor_copy(decay[:, s], E_far[:, s, 0]))
                wait("pool", t)
                tok["mul", q] = done("pool", pool.tensor_tensor(E_far[:, s, :], E_far[:, s, :], bcast(c_pair[:, s], P + 1), ALU.mult))

            def sum_states(bank):
                b = work_bank()
                wait("pe", tok["mul", bank], *bank_free[b])
                for a in range(16 * bank, 16 * bank + 16):
                    q, k = a % 4, a // 4 % 4
                    mm = pe.matmul(psum[32 * q:32 * q + 32, b, k * P:(k + 1) * P], pairs2[:], E_far[:, a, 1:P + 1],
                                   start=True, stop=True)
                t = done("pe", mm)
                wait("act", t)
                tok["k"] = done("act", act.activation(k_rev[:, bank, :], psum[:, b, :], ACT.Copy))
                bank_free[b] = [tok["k"]]

            def store():
                wait("sp", tok["k"], tok["mul", 3])
                for q in range(4):
                    dma("sp", "st_taps", bass.AP(tensor=taps.tensor, offset=2 * q * 2 * P, ap=[[2 * P, 2], [8 * 2 * P, 16], [1, P]]),
                        take(92 * 256, T)[32 * q:32 * q + 2, :].rearrange("p (s x) -> p s x", s=16))
                t_taps[0] = dma("sp", "st_taps", taps[:, P:2 * P], zero)

            pieces = [rates]
            for q in range(4):
                pieces += [lambda a=a: powers(a) for a in range(16 * q, 16 * q + 16, 4)] + [lambda q=q: times_c(q)]
            return pieces + [lambda b=b: sum_states(b) for b in range(4)] + [store]

        def ssm_near_tables():
            step = D // 8
            for e in ("act", "dve", "pool", "sp"):
                wait(e, t_taps[0])

            def blocks():
                wait("sp", t_taps[0], *core.last.values())
                wait("act", t_taps[0], *core.last.values())
                for m in range(0, D, step):
                    t_toep[0] = dma("sp" if (m // step) % 2 else "act", "ld_toep", toep[:, m:m + step, :],
                                    bass.AP(tensor=taps.tensor, offset=m * 2 * P, ap=[[1, P], [2 * P, step], [1, P]]))

            def rates():
                wait("act", t_dt[0])
                t1 = done("act", act.activation(logdt_all, logdt_all, ACT.Exp))
                t_dt[0] = done("act", act.activation(alog_all, alog_all, ACT.Exp))
                done("dve", dve.tensor_scalar(neg_back[:], back_col[:], -1.0, None, ALU.mult))
                wait("dve", t1, t_dt[0])

            def powers(m):
                part = b_in[:, m:m + step, :]
                t = done("dve", dve.tensor_tensor(part, bcast(logdt_all[:, m:m + step], NS),
                                                  alog_all.unsqueeze(1).broadcast_to([P, step, NS]), ALU.mult))
                wait("act", t)
                t_bin[0] = done("act", act.activation(part, part, ACT.Exp, scale=neg_back[:, 0:1]))

            idle = lambda: None
            return [blocks, idle, idle, rates, idle] + [lambda m=m: powers(m) for m in range(0, D, step)]

        neg_back = sb("neg_back", [P, 1])
        t_taps, t_toep, t_dt, t_bin = [None], [None], [None], [None]

        def ssm(name, x_ready):
            core.stage(name)
            C17 = NT + 1
            state_in = take(96 * 256, 64 * C17)
            states = take(101 * 256, 64 * C17)
            mult = take(106 * 256, 64 * C17)
            v3 = lambda t: t.rearrange("p (a c) -> p a c", a=64)
            y_ready = layer_norm(x_ready)
            tz = done("pool", pool.memset(v3(state_in)[:, :, 0:1], 0.0))
            done("pool", pool.memset(v3(mult)[:, :, 0:1], 0.0))
            t_mult = done("pool", pool.tensor_copy(v3(mult)[:, :, 1:C17], bcast(decay[:], NT)))
            for n in range(NT):
                wait("pool", y_ready[n])
            t = done("pool", pool.tensor_tensor(ACC[:, :, :], Y[:, :, :], skip_d[:].unsqueeze(1).broadcast_to([P, NT, D]), ALU.mult))
            wait("pool", t)
            t_skip = done("pool", pool.tensor_tensor(X[:, :, :], X[:, :, :], ACC[:, :, :], ALU.add))
            wait("pe", t_bin[0], *y_ready, *bank_free[0], *bank_free[1])
            for a in range(64):
                for r in range(2):
                    mm = pe.matmul(psum[64 * r:64 * r + 64, a // 32, (a % 32) * NT:(a % 32 + 1) * NT],
                                   b_in[:, 2 * a + r, :], Y[:, :, 2 * a + r], start=True, stop=True)
            t = done("pe", mm)
            wait("dve", t, tz)
            t = done("dve", dve.tensor_copy(v3(state_in)[:, :, 1:C17], psum[:, 0:2, :].rearrange("p b (a c) -> p (b a) c", c=NT)))
            bank_free[0] = bank_free[1] = [t]
            wait("dve", t, t_mult)
            t_st = done("dve", dve.tensor_tensor_scan(states, mult, state_in, 0.0, ALU.mult, ALU.add))
            st3 = v3(states)
            rows_free, tok = [], None
            banks = (0, 1, 2, 3)
            for b in banks:
                wait("dve", *bank_free[b])
                t = done("dve", dve.memset(psum[:, b, :], 0.0))
                bank_free[b] = [t]
            ysb = [ACC[:, 4 * i:4 * i + 4, :] for i in range(4)]
            wait("act", t_skip)
            wait("pe", t_toep[0])
            ysb_free = [[], [], [], []]
            for grp in range(8):
                b = grp % 4
                wait("pe", *bank_free[b])
                for qd in range(4):
                    for q in range(4):
                        m = 16 * grp + 4 * qd + q
                        o = psum[32 * q:32 * q + NT, b, qd * P:(qd + 1) * P]
                        pe.matmul(o, Y[:, :, m], toep[:, m, :], start=True, stop=False, skip_group_check=True)
                    if qd == 0 and grp == 0:
                        wait("pe", t_st)
                    for q in range(4):
                        m = 16 * grp + 4 * qd + q
                        r = 64 * (m % 2)
                        o = psum[32 * q:32 * q + NT, b, qd * P:(qd + 1) * P]
                        mm = pe.matmul(o, st3[r:r + 64, m // 2, 0:NT], E_far[r:r + 64, m // 2, 0:P], start=False,
                                       stop=True, skip_group_check=True)
                t = done("pe", mm)
                ys = ysb[grp % 4]
                wait("act", t, *ysb_free[grp % 4])
                t = done("act", act.activation(ys, psum[:, b, :].rearrange("p (k x) -> p k x", k=4)[:, :, ::-1], ACT.Copy))
                bank_free[b] = [t]
                tb = 4 + grp % 2
                wait("pe", t, *bank_free[tb])
                for qd in range(4):
                    mm = pe.transpose(psum[:, tb, qd * P:(qd + 1) * P], ys[:, qd, :], ident[:])
                t = done("pe", mm)
                ysb_free[grp % 4] = [t]
                wait("dve", t, t_skip)
                add = psum[:, tb, :].rearrange("p (m c) -> p c m", c=32)[:, 0:NT, :]
                dst = X[:, :, 16 * grp:16 * grp + 16]
                tok = done("dve", dve.tensor_tensor(dst, add, dst, ALU.add))
                bank_free[tb] = [tok]
            barrier()
            return [tok] * NG

        ready = macaron_ffn("ffa", x_in)
        if upto >= 2:
            ready = windowed_attention("win", ready)
        if upto >= 3:
            ready = macaron_ffn("ffb", ready)
        if upto >= 4:
            ready = latent_block("la", ready, during_attention=ssm_far_table, during_moe=ssm_near_tables)
            wait("sp", t_toep[0])
        if upto >= 5:
            ready = ssm("ssm", ready)
        if upto >= 6:
            ready = latent_block("lb", ready)
        core.stage("end")
        out_view = out[0].rearrange("(i p) f -> p i f", p=P)
        for g in range(NG):
            wait("sp", settle(ready, g))
            t = dma("sp", "st_out", out_view[:, GT * g:GT * g + GT, :], X[:, GT * g:GT * g + GT, :])
        wait("sp", t, const_in)


_RAW = ["L0_attn_x", "L0_attn_bq", "L0_attn_bk", "L0_attn_bv", "L0_attn_wo", "L0_attn_bo", "L0_attn_qn_w",
        "L0_attn_kn_w", "L0_ffn_gate_b", "L0_ffn_b1", "L0_ffn_b2", "L1_attn_A_log", "L1_attn_D", "L1_attn_log_dt",
        "L1_ffn_gate_b", "L1_ffn_b1", "L1_ffn_b2"]


def kernel(**inputs):
    import numpy as np
    import concourse.bacc as _bacc
    from concourse.bass_utils import run_bass_kernel_spmd as _run

    a = {n: np.ascontiguousarray(inputs[n]) for n in _RAW}
    g = {n: np.asarray(v) for n, v in inputs.items()}

    def lay(name, value):
        a[name] = np.ascontiguousarray(value)

    lay("gate0", g["L0_ffn_gate_w"].T)
    lay("gate1", g["L1_ffn_gate_w"].T)
    for k, (w1, b1, w2, ne) in enumerate((("L0_ffn_w1", "L0_ffn_b1", "L0_ffn_w2", NE0), ("L1_ffn_W1", "L1_ffn_b1", "L1_ffn_W2", NE1))):
        lay(f"w1_{k}", g[w1].transpose(2, 0, 1))
        lay(f"w2_{k}", g[w2].reshape(ne, D, HC, P).transpose(3, 0, 2, 1))
    lay("wqkv", np.concatenate([g["L0_attn_wq"], g["L0_attn_wk"], g["L0_attn_wv"]], axis=1))
    lay("wqd", np.concatenate([g["L1_ffn_Wq"].T, g["L1_ffn_Wdkv"].T], axis=1))
    lay("wukv", np.concatenate([g["L1_ffn_Wuk"].T, g["L1_ffn_Wuv"].T], axis=1))
    lay("wo1", g["L1_ffn_Wo"].T)
    lay("norm_w", np.stack([g["L1_ffn_norm1_w"], g["L1_ffn_norm2_w"]], axis=1))
    lay("ln_gb", np.stack([g["L1_ffn_ln_g"], g["L1_ffn_ln_b"]], axis=1))
    lay("c_pair", g["L1_attn_C_re"].reshape(64, 2 * NS).T)

    lay("logdt_pair", g["L1_attn_log_dt"].reshape(64, 2).T)
    lay("alog_col", g["L1_attn_A_log"][:, None])

    f = np.float32
    lay("order0", np.tile(np.arange(NE0, 0, -1, dtype=f), (P, 1)))
    lay("order1", np.tile(np.arange(NE1, 0, -1, dtype=f), (P, 1)))
    row, col = np.arange(P)[:, None] % W, np.arange(2 * W)[None, :]
    ok = (col <= row + W) & (col > row)
    first = ok & ((np.arange(P)[:, None] >= W) | (col >= W))
    lay("window_mask", np.stack([np.where(first, 0, MASKED), np.where(ok, 0, MASKED)], axis=1).astype(f))
    half = HD // 2
    inv_freq = (f(1.0) / f(10000.0) ** (np.arange(half, dtype=f) / f(half))).astype(f)
    ang = np.arange(T, dtype=f)[:, None] * inv_freq[None, :]
    sin, cos = np.sin(ang).astype(f), np.cos(ang).astype(f)
    table = np.stack([np.concatenate([cos, cos], 1), np.concatenate([-sin, sin], 1)])
    lay("rope", table.reshape(2, NT, P, HD).transpose(2, 0, 1, 3))
    lay("tile_start", np.tile(P * np.arange(NT + NE0 - 1, dtype=f), (P, 1)))
    lay("back", np.tile(np.arange(P, -1, -1, dtype=f), (P, 1)))
    lay("back_col", np.arange(P - 1, -1, -1, dtype=f)[:, None])

    nc = _bacc.Bacc("TRN2", target_bir_lowering=False, num_devices=1)
    arrays = {f"in_{n}": v for n, v in a.items()}
    ins = {n: nc.dram_tensor(f"in_{n}", v.shape, mybir.dt.from_np(v.dtype), kind="ExternalInput").ap() for n, v in a.items()}
    out = nc.dram_tensor("out_0", (1, T, D), F32, kind="ExternalOutput").ap()
    build(nc, ins, out, UPTO)
    r = _run(nc, [arrays], core_ids=[0])
    return r.results[0]["out_0"]


UPTO = 6
```
